# Optimizing a Trainium2 kernel written in Bass

```python
import numpy as np
import jax
import jax.numpy as jnp

def _softmax(x, axis=-1):
    return jax.nn.softmax(x, axis=axis)

def _gelu(x):
    return jax.nn.gelu(x, approximate=True)

def _silu(x):
    return jax.nn.silu(x)

def _sigmoid(x):
    return jax.nn.sigmoid(x)

def _layernorm(x, axis=-1, eps=1e-05):
    m = jnp.mean(x, axis=axis, keepdims=True)
    v = jnp.var(x, axis=axis, keepdims=True)
    return (x - m) / jnp.sqrt(v + eps)

def _scatter_add(tgt, idx, src, axis=0):
    return tgt.at[idx].add(src)

def _segment_sum(src, seg, n):
    return jax.ops.segment_sum(src, seg, n)
kernel_name = 'mk_adaln_d1_jaxref_r8_770c5b'

def setup_inputs(seed: int=0):
    np.random.seed(seed)
    _w = jnp.asarray

    def _L0_attn_setup():
        import jax, jax.numpy as jnp
        import numpy as np
        B, T, D, H = (8, 512, 128, 16)
        DK = D // H
        CHUNK = 64
        E, TOPK, MULT, CAPF = (8, 2, 4, 1.25)
        HID = D * MULT
        N = B * T
        CAPACITY = int(CAPF * (N / E))

        def rmsnorm(x, scale):
            return x / jnp.sqrt(jnp.mean(x * x, axis=-1, keepdims=True)) * scale

        def apply_rope(x):
            half = x.shape[-1] // 2
            t = x.shape[2]
            inv = 1.0 / 10000.0 ** (jnp.arange(half, dtype=jnp.float32) / half)
            ang = jnp.arange(t, dtype=jnp.float32)[:, None] * inv[None, :]
            sin, cos = (jnp.sin(ang)[None, None], jnp.cos(ang)[None, None])
            x1, x2 = (x[..., :half], x[..., half:])
            return jnp.concatenate([x1 * cos - x2 * sin, x1 * sin + x2 * cos], axis=-1)

        def phi(x):
            return jax.nn.elu(x) + 1.0

        def attention(x, Wq, bq, Wk, bk, Wv, bv, Wg, bg, Wo, bo):
            b, t, c = x.shape
            heads = lambda y: y.reshape(b, t, H, DK).transpose(0, 2, 1, 3)
            q = phi(apply_rope(heads(x @ Wq + bq)))
            k = phi(apply_rope(heads(x @ Wk + bk)))
            v = heads(x @ Wv + bv)
            g = heads(jax.nn.sigmoid(x @ Wg + bg))
            nc = t // CHUNK
            to_chunks = lambda y: y.reshape(b, H, nc, CHUNK, DK).transpose(2, 0, 1, 3, 4)
            qs, ks_, vs, gs = map(to_chunks, (q, k, v, g))
            S0 = jnp.zeros((b, H, DK, DK), x.dtype)
            Z0 = jnp.zeros((b, H, DK), x.dtype)

            def step(carry, inp):
                S, Z = carry
                qc, kc, vc, gc = inp
                S = S + jnp.einsum('bhtd,bhte->bhde', kc, vc)
                Z = Z + kc.sum(axis=2)
                num = jnp.einsum('bhtd,bhde->bhte', qc, S)
                den = jnp.einsum('bhtd,bhd->bht', qc, Z)[..., None] + 1e-06
                return ((S, Z), gc * (num / den))
            _, outs = jax.lax.scan(step, (S0, Z0), (qs, ks_, vs, gs))
            out = outs.transpose(1, 2, 0, 3, 4).reshape(b, H, t, DK)
            out = out.transpose(0, 2, 1, 3).reshape(b, t, c)
            return out @ Wo + bo

        def moe(x, router_W, router_b, W1, b1, W2, b2):
            b, t, c = x.shape
            n = b * t
            xf = x.reshape(n, c)
            probs = jax.nn.softmax(xf @ router_W + router_b, axis=-1)
            topk_probs, topk_idx = jax.lax.top_k(probs, TOPK)
            topk_probs = topk_probs / topk_probs.sum(axis=-1, keepdims=True)
            out = jnp.zeros_like(xf)
            load = []
            for eid in range(E):
                mask = (topk_idx == eid).reshape(-1)
                idx = jnp.nonzero(mask, size=CAPACITY, fill_value=n * TOPK)[0]
                valid = idx < n * TOPK
                idxc = jnp.minimum(idx, n * TOPK - 1)
                tok, choice = (idxc // TOPK, idxc % TOPK)
                h = jax.nn.gelu(xf[tok] @ W1[eid] + b1[eid], approximate=False) @ W2[eid] + b2[eid]
                gate = jnp.where(valid, topk_probs[tok, choice], 0.0)
                out = out.at[tok].add(gate[:, None] * h)
                load.append(jnp.minimum(mask.sum(), CAPACITY).astype(xf.dtype))
            load = jnp.stack(load)
            importance = probs.sum(axis=0)
            importance = importance / importance.sum()
            load = load / load.sum()
            aux = (importance * load).sum() * E ** 2
            return (out.reshape(b, t, c), aux)

        def _reference_tuple_inner(x, norm1_scale, norm2_scale, Wq, bq, Wk, bk, Wv, bv, Wg, bg, Wo, bo, router_W, router_b, W1, b1, W2, b2):
            x = x + attention(rmsnorm(x, norm1_scale), Wq, bq, Wk, bk, Wv, bv, Wg, bg, Wo, bo)
            moe_out, aux = moe(rmsnorm(x, norm2_scale), router_W, router_b, W1, b1, W2, b2)
            return (x + moe_out, aux)
        key = jax.random.key(seed)
        ks = jax.random.split(key, 16)
        s = 0.02
        r = lambda k, shape: jax.random.normal(k, shape, jnp.float32) * s
        return {'x': jax.random.normal(ks[0], (B, T, D), jnp.float32), 'norm1_scale': jnp.ones((D,), jnp.float32), 'norm2_scale': jnp.ones((D,), jnp.float32), 'Wq': r(ks[1], (D, D)), 'bq': jnp.zeros((D,), jnp.float32), 'Wk': r(ks[2], (D, D)), 'bk': jnp.zeros((D,), jnp.float32), 'Wv': r(ks[3], (D, D)), 'bv': jnp.zeros((D,), jnp.float32), 'Wg': r(ks[4], (D, D)), 'bg': jnp.zeros((D,), jnp.float32), 'Wo': r(ks[5], (D, D)), 'bo': jnp.zeros((D,), jnp.float32), 'router_W': r(ks[6], (D, E)), 'router_b': jnp.zeros((E,), jnp.float32), 'W1': r(ks[7], (E, D, HID)), 'b1': jnp.zeros((E, HID), jnp.float32), 'W2': r(ks[8], (E, HID, D)), 'b2': jnp.zeros((E, D), jnp.float32)}
    _L0_attn_in = _L0_attn_setup()

    def _L0_ffn_setup():
        import jax, jax.numpy as jnp
        import numpy as np
        N_EMBD = 128
        N_STATE = 512
        key = jax.random.key(seed)
        k_x, k_w1, k_b1, k_w2, k_b2 = jax.random.split(key, 5)
        x = jax.random.normal(k_x, (4, 256, N_EMBD), dtype=jnp.float32)
        w1 = jax.random.normal(k_w1, (N_EMBD, N_STATE), dtype=jnp.float32) * (1.0 / np.sqrt(N_EMBD))
        b1 = jax.random.normal(k_b1, (N_STATE,), dtype=jnp.float32) * 0.02
        w2 = jax.random.normal(k_w2, (N_STATE, N_EMBD), dtype=jnp.float32) * (1.0 / np.sqrt(N_STATE))
        b2 = jax.random.normal(k_b2, (N_EMBD,), dtype=jnp.float32) * 0.02
        return {'x': x, 'w1': w1, 'b1': b1, 'w2': w2, 'b2': b2}
    _L0_ffn_in = _L0_ffn_setup()
    _L0_c = _w((lambda *s: np.random.randn(*s).astype(np.float32) * 0.05)(16, 128))
    _L0_wmod = _w((lambda *s: np.random.randn(*s).astype(np.float32) * 0.05)(128, 6 * 128) * 128 ** (-0.5))
    _d = {'L0_attn_x': _L0_attn_in['x'], 'L0_attn_norm1_scale': _L0_attn_in['norm1_scale'], 'L0_attn_norm2_scale': _L0_attn_in['norm2_scale'], 'L0_attn_Wq': _L0_attn_in['Wq'], 'L0_attn_bq': _L0_attn_in['bq'], 'L0_attn_Wk': _L0_attn_in['Wk'], 'L0_attn_bk': _L0_attn_in['bk'], 'L0_attn_Wv': _L0_attn_in['Wv'], 'L0_attn_bv': _L0_attn_in['bv'], 'L0_attn_Wg': _L0_attn_in['Wg'], 'L0_attn_bg': _L0_attn_in['bg'], 'L0_attn_Wo': _L0_attn_in['Wo'], 'L0_attn_bo': _L0_attn_in['bo'], 'L0_attn_router_W': _L0_attn_in['router_W'], 'L0_attn_router_b': _L0_attn_in['router_b'], 'L0_attn_W1': _L0_attn_in['W1'], 'L0_attn_b1': _L0_attn_in['b1'], 'L0_attn_W2': _L0_attn_in['W2'], 'L0_attn_b2': _L0_attn_in['b2'], 'L0_ffn_w1': _L0_ffn_in['w1'], 'L0_ffn_b1': _L0_ffn_in['b1'], 'L0_ffn_w2': _L0_ffn_in['w2'], 'L0_ffn_b2': _L0_ffn_in['b2'], 'L0_c': _L0_c, 'L0_wmod': _L0_wmod}
    _x0 = _d['L0_attn_x']
    _d['L0_attn_x'] = jax.random.normal(jax.random.fold_in(jax.random.key(seed), 1), (16, 256, 128), dtype=_x0.dtype)
    del _x0
    return _d

def reference(L0_attn_x, L0_attn_norm1_scale, L0_attn_norm2_scale, L0_attn_Wq, L0_attn_bq, L0_attn_Wk, L0_attn_bk, L0_attn_Wv, L0_attn_bv, L0_attn_Wg, L0_attn_bg, L0_attn_Wo, L0_attn_bo, L0_attn_router_W, L0_attn_router_b, L0_attn_W1, L0_attn_b1, L0_attn_W2, L0_attn_b2, L0_ffn_w1, L0_ffn_b1, L0_ffn_w2, L0_ffn_b2, L0_c, L0_wmod):

    def _L0_attn_ref(x, norm1_scale, norm2_scale, Wq, bq, Wk, bk, Wv, bv, Wg, bg, Wo, bo, router_W, router_b, W1, b1, W2, b2):
        import jax, jax.numpy as jnp
        import numpy as np
        B, T, D, H = (8, 512, 128, 16)
        DK = D // H
        CHUNK = 64
        E, TOPK, MULT, CAPF = (8, 2, 4, 1.25)
        HID = D * MULT
        N = B * T
        CAPACITY = int(CAPF * (N / E))

        def rmsnorm(x, scale):
            return x / jnp.sqrt(jnp.mean(x * x, axis=-1, keepdims=True)) * scale

        def apply_rope(x):
            half = x.shape[-1] // 2
            t = x.shape[2]
            inv = 1.0 / 10000.0 ** (jnp.arange(half, dtype=jnp.float32) / half)
            ang = jnp.arange(t, dtype=jnp.float32)[:, None] * inv[None, :]
            sin, cos = (jnp.sin(ang)[None, None], jnp.cos(ang)[None, None])
            x1, x2 = (x[..., :half], x[..., half:])
            return jnp.concatenate([x1 * cos - x2 * sin, x1 * sin + x2 * cos], axis=-1)

        def phi(x):
            return jax.nn.elu(x) + 1.0

        def attention(x, Wq, bq, Wk, bk, Wv, bv, Wg, bg, Wo, bo):
            b, t, c = x.shape
            heads = lambda y: y.reshape(b, t, H, DK).transpose(0, 2, 1, 3)
            q = phi(apply_rope(heads(x @ Wq + bq)))
            k = phi(apply_rope(heads(x @ Wk + bk)))
            v = heads(x @ Wv + bv)
            g = heads(jax.nn.sigmoid(x @ Wg + bg))
            nc = t // CHUNK
            to_chunks = lambda y: y.reshape(b, H, nc, CHUNK, DK).transpose(2, 0, 1, 3, 4)
            qs, ks_, vs, gs = map(to_chunks, (q, k, v, g))
            S0 = jnp.zeros((b, H, DK, DK), x.dtype)
            Z0 = jnp.zeros((b, H, DK), x.dtype)

            def step(carry, inp):
                S, Z = carry
                qc, kc, vc, gc = inp
                S = S + jnp.einsum('bhtd,bhte->bhde', kc, vc)
                Z = Z + kc.sum(axis=2)
                num = jnp.einsum('bhtd,bhde->bhte', qc, S)
                den = jnp.einsum('bhtd,bhd->bht', qc, Z)[..., None] + 1e-06
                return ((S, Z), gc * (num / den))
            _, outs = jax.lax.scan(step, (S0, Z0), (qs, ks_, vs, gs))
            out = outs.transpose(1, 2, 0, 3, 4).reshape(b, H, t, DK)
            out = out.transpose(0, 2, 1, 3).reshape(b, t, c)
            return out @ Wo + bo

        def moe(x, router_W, router_b, W1, b1, W2, b2):
            b, t, c = x.shape
            n = b * t
            xf = x.reshape(n, c)
            probs = jax.nn.softmax(xf @ router_W + router_b, axis=-1)
            topk_probs, topk_idx = jax.lax.top_k(probs, TOPK)
            topk_probs = topk_probs / topk_probs.sum(axis=-1, keepdims=True)
            out = jnp.zeros_like(xf)
            load = []
            for eid in range(E):
                mask = (topk_idx == eid).reshape(-1)
                idx = jnp.nonzero(mask, size=CAPACITY, fill_value=n * TOPK)[0]
                valid = idx < n * TOPK
                idxc = jnp.minimum(idx, n * TOPK - 1)
                tok, choice = (idxc // TOPK, idxc % TOPK)
                h = jax.nn.gelu(xf[tok] @ W1[eid] + b1[eid], approximate=False) @ W2[eid] + b2[eid]
                gate = jnp.where(valid, topk_probs[tok, choice], 0.0)
                out = out.at[tok].add(gate[:, None] * h)
                load.append(jnp.minimum(mask.sum(), CAPACITY).astype(xf.dtype))
            load = jnp.stack(load)
            importance = probs.sum(axis=0)
            importance = importance / importance.sum()
            load = load / load.sum()
            aux = (importance * load).sum() * E ** 2
            return (out.reshape(b, t, c), aux)

        def _reference_tuple_inner(x, norm1_scale, norm2_scale, Wq, bq, Wk, bk, Wv, bv, Wg, bg, Wo, bo, router_W, router_b, W1, b1, W2, b2):
            x = x + attention(rmsnorm(x, norm1_scale), Wq, bq, Wk, bk, Wv, bv, Wg, bg, Wo, bo)
            moe_out, aux = moe(rmsnorm(x, norm2_scale), router_W, router_b, W1, b1, W2, b2)
            return (x + moe_out, aux)
        return _reference_tuple_inner(x, norm1_scale, norm2_scale, Wq, bq, Wk, bk, Wv, bv, Wg, bg, Wo, bo, router_W, router_b, W1, b1, W2, b2)[0]

    def _L0_ffn_ref(x, w1, b1, w2, b2):
        import jax, jax.numpy as jnp
        import numpy as np
        N_EMBD = 128
        N_STATE = 512
        h = jax.nn.gelu(jnp.einsum('bse,eh->bsh', x, w1) + b1, approximate=False)
        return jnp.einsum('bsh,he->bse', h, w2) + b2
    x = L0_attn_x
    mod = (_silu(L0_c) @ L0_wmod).reshape(L0_c.shape[0], 6, 1, -1)
    sa, ca, ga, sb, cb, gb = (mod[:, 0], mod[:, 1], mod[:, 2], mod[:, 3], mod[:, 4], mod[:, 5])
    ga = (2 * (ga >= 0) - 1) * jnp.maximum(jnp.abs(ga), 0.25)
    gb = (2 * (gb >= 0) - 1) * jnp.maximum(jnp.abs(gb), 0.25)
    h = _layernorm(x, axis=-1) * (1 + ca) + sa
    x = x + ga * _L0_attn_ref(h, L0_attn_norm1_scale, L0_attn_norm2_scale, L0_attn_Wq, L0_attn_bq, L0_attn_Wk, L0_attn_bk, L0_attn_Wv, L0_attn_bv, L0_attn_Wg, L0_attn_bg, L0_attn_Wo, L0_attn_bo, L0_attn_router_W, L0_attn_router_b, L0_attn_W1, L0_attn_b1, L0_attn_W2, L0_attn_b2)
    h = _layernorm(x, axis=-1) * (1 + cb) + sb
    x = x + gb * _L0_ffn_ref(h, L0_ffn_w1, L0_ffn_b1, L0_ffn_w2, L0_ffn_b2)
    return x

_drawn_inputs = setup_inputs


def setup_inputs(seed=0):
    import zlib

    import numpy as np

    out = dict(_drawn_inputs(seed))
    spreads = {'L0_attn_norm1_scale': (1.0, 0.6),
     'L0_attn_norm2_scale': (1.0, 0.6),
     'L0_attn_bq': (0.0, 0.8),
     'L0_attn_bk': (0.0, 0.8),
     'L0_attn_bv': (0.0, 0.8),
     'L0_attn_bg': (0.0, 0.8),
     'L0_attn_bo': (0.0, 0.317),
     'L0_attn_router_b': (0.0, 0.652),
     'L0_attn_b1': (0.0, 0.8),
     'L0_attn_b2': (0.0, 0.568)}
    factors = {'L0_attn_Wq': 8.0,
     'L0_attn_Wk': 8.0,
     'L0_attn_Wv': 8.0,
     'L0_attn_Wg': 8.0,
     'L0_attn_Wo': 8.0,
     'L0_attn_router_W': 4.035,
     'L0_attn_W1': 7.69,
     'L0_attn_W2': 6.991,
     'L0_ffn_b1': 22.108,
     'L0_ffn_b2': 8.0}
    for name, (base, spread) in spreads.items():
        noise = np.random.default_rng([zlib.crc32(name.encode()), seed]).standard_normal(out[name].shape)
        drawn = base * np.exp(spread * noise) if base else spread * noise
        out[name] = jnp.asarray(drawn.astype(out[name].dtype))
    for name, factor in factors.items():
        out[name] = (out[name] * factor).astype(out[name].dtype)
    return out
```

```python
from contextlib import ExitStack

import numpy as np

import concourse.bass as bass
from concourse import mybir

F32 = mybir.dt.float32
BF16 = mybir.dt.bfloat16
U32 = mybir.dt.uint32
ALU = mybir.AluOpType
ACT = mybir.ActivationFunctionType
AX = mybir.AxisListType

P = 128
BATCH, SEQ, C = 16, 256, 128
TOKENS = BATCH * SEQ
TILES = TOKENS // P
TPB = SEQ // P
HEADS = 16
DK = C // HEADS
CHUNK = 64
CHUNKS = SEQ // CHUNK
SW = C + HEADS
EXPERTS, TOPK = 8, 2
CAPACITY = int(1.25 * TOKENS / EXPERTS)
HID = 512
HB = HID // P
ST = CAPACITY // P
SLOTS = EXPERTS * CAPACITY
ID, G1, G2, E1, E2, PAY = C, C + 1, C + 2, C + 3, C + 4, C + 5
PAIR = 2 * TPB
IN_LOOP = -1
ROUTE = 17
FAR = 1.0e5
NSUP = BATCH // 2
SUPT = 2 * TPB
SPLIT = 384
PARTS = ((0, SPLIT), (SPLIT, CAPACITY))

K_IDENT, K_TRI, K_KTAB, K_QTAB = 0, 128, 256, 768
K_MASK = 1280
K_IOTA = K_MASK + SW
K_BASE = K_IOTA + EXPERTS
K_TOK = K_BASE + EXPERTS
K_SEL = K_TOK + PAIR
K_ALL = K_SEL + 3
V_S1, V_S2, V_FB1, V_FB2, V_B1 = 0, 1, 2, 6, 7
EV = HB + 1
V_ALL = V_B1 + EXPERTS * EV
B_KVG, B_Q, B_O, B_R = 0, 512, 768, 896
B_ALL = B_R + EXPERTS
SA, CA, GA, SB, CB, GB = (slice(C * i, C * i + C) for i in range(6))


def constants():
    k = np.zeros((P, K_ALL), np.float32)
    k[:, K_IDENT:K_IDENT + P] = np.eye(P)
    k[:, K_TRI:K_TRI + P] = np.triu(np.ones((P, P)), 1)
    half = DK // 2
    inv = np.float32(1.0) / np.float32(10000.0) ** (np.arange(half, dtype=np.float32) / np.float32(half))
    ang = np.arange(SEQ, dtype=np.float32)[:, None] * inv[None, :]
    cos = np.tile(np.concatenate([np.cos(ang), np.cos(ang)], 1), (1, HEADS))
    sin = np.tile(np.concatenate([-np.sin(ang), np.sin(ang)], 1), (1, HEADS))
    k[:, K_KTAB:K_KTAB + 512] = np.stack([cos, sin], 1).reshape(TPB, P, 2 * C).transpose(1, 0, 2).reshape(P, -1)
    k[:, K_QTAB:K_QTAB + 512] = np.concatenate([cos.T, sin.T], 1)
    head = np.arange(C) // DK
    k[:, K_MASK:K_MASK + C] = head[:, None] == head[None, :]
    k[:, K_MASK + C:K_MASK + SW] = head[:, None] == np.arange(HEADS)[None, :]
    k[:, K_IOTA:K_IOTA + EXPERTS] = np.arange(EXPERTS)
    k[:, K_BASE:K_BASE + EXPERTS] = np.arange(EXPERTS) * CAPACITY
    k[:, K_TOK:K_TOK + PAIR] = np.arange(P)[:, None] + P * np.arange(PAIR)[None, :]
    k[:3, K_SEL:K_SEL + 3] = np.eye(3)
    empty = np.zeros((P, ST, PAY), np.float32)
    empty[:, :, ID] = TOKENS + np.arange(P)[:, None] + P * np.arange(ST)[None, :]
    return k, empty


def adaln_moe(nc, x_d, c_d, wmod_d, wkvg_d, wq_d, wo_d, wr_d, w1_d, w2_d, f1_d, f2_d,
              vec_d, bias_d, const_d, empty_d, out_d):
    mod_d = nc.dram_tensor("mod_rows", [BATCH, 6 * C], F32).ap()
    slot_d = nc.dram_tensor("slots", [SLOTS, PAY], F32).ap()
    acc_d = nc.dram_tensor("acc", [TOKENS + CAPACITY, C], F32).ap()

    with ExitStack() as ctx:
        def sb(name, shape, dt=F32):
            return ctx.enter_context(nc.sbuf_tensor(name, shape, dt))

        def sem(name):
            return ctx.enter_context(nc.semaphore(name))

        def sems(name, n=2):
            return [sem(f"{name}{i}") for i in range(n)]

        ps = ctx.enter_context(nc.psum_tensor("ps", [P, 8, 512], F32))
        konst = sb("konst", [P, K_ALL])
        empty = sb("empty", [P, ST, PAY])
        vec = sb("vec", [P, V_ALL])
        x = sb("x", [P, TILES, C])
        wkvg = sb("wkvg", [P, 4 * C])
        wq = sb("wq", [P, 2 * C])
        wo = sb("wo", [P, C])
        wr = sb("wr", [P, EXPERTS])
        f1 = sb("f1", [P, HID])
        f2 = sb("f2", [P, HB, C])
        w1 = sb("w1", [P, 2, HID])
        w2 = sb("w2", [P, 2, HB, C])
        ident = konst[:, K_IDENT:K_IDENT + P]

        cond = sb("cond", [BATCH, C])
        cond_t = sb("cond_t", [BATCH, C])
        silu = sb("silu", [BATCH, C])
        siluT = sb("siluT", [P, BATCH])
        wmod = sb("wmod", [P, 6 * C])
        mod = sb("mod", [BATCH, 6 * C])
        mod_s = sb("mod_s", [BATCH, 2, C])
        mod_m = sb("mod_m", [BATCH, 2, C])
        modT = sb("modT", [P, BATCH, 4])
        bias = sb("bias", [3, B_ALL])
        bpart = sb("bpart", [3, B_ALL], BF16)
        bsum = sb("bsum", [3, B_ALL])
        bias3 = sb("bias3", [3, B_ALL], BF16)
        ones3 = sb("ones3", [3, SEQ], BF16)
        ones = sb("ones", [P, P], BF16)
        tri = sb("tri", [P, P], BF16)
        power = sb("power", [P, TILES])

        stat = sb("stat", [P, TILES, 6])
        mean = sb("mean", [P, TILES])
        var = sb("var", [P, TILES])
        dmean = sb("dmean", [P, TILES])
        rstd = sb("rstd", [P, TILES])
        nmr = sb("nmr", [P, TILES])

        rows = sb("rows", [P, 2, 2 * C])
        xhat = sb("xhat", [P, 2, TPB, C])
        h = sb("h", [P, 4, TPB, C])
        junk = sb("junk", [P, TPB, C])
        ms1 = sb("ms1", [P, 2, TPB])
        r1 = sb("r1", [P, 2, TPB])
        hn = sb("hn", [P, TPB, C])
        hnT = sb("hnT", [P, 2, SEQ])
        kab = sb("kab", [P, TPB, 2 * C])
        qab = sb("qab", [P, 2 * SEQ])
        ka = sb("ka", [P, TPB, C])
        qa = sb("qa", [P, SEQ])
        kexp = sb("kexp", [P, TPB, C])
        krel = sb("krel", [P, TPB, C])
        qexp = sb("qexp", [P, SEQ])
        qrel = sb("qrel", [P, SEQ])
        kphi = sb("kphi", [P, 2, TPB, C])
        qphi = sb("qphi", [P, 2, SEQ])
        vone = sb("vone", [P, 2, TPB, SW])
        gate = sb("gate", [P, 2, TPB, C])
        state = sb("state", [P, CHUNKS, SW])
        gnum = sb("gnum", [P, TPB, C])
        den = sb("den", [P, TPB, HEADS])
        rden = sb("rden", [P, TPB, HEADS])
        o = sb("o", [P, TPB, C])
        oT = sb("oT", [P, 2, SEQ])
        x1 = sb("x1", [P, 2, TPB, C])
        junk2 = sb("junk2", [P, TPB, C])
        ms2 = sb("ms2", [P, 2, TPB])
        r2 = sb("r2", [P, 2, TPB])
        pay = [sb(f"pay{i}", [P, PAIR, PAY]) for i in range(2)]
        xfT = sb("xfT", [P, SEQ])

        logit = sb("logit", [P, PAIR, EXPERTS])
        top = sb("top", [P, PAIR, EXPERTS])
        topi = sb("topi", [P, PAIR, EXPERTS], U32)
        hot = sb("hot", [P, PAIR, TOPK, EXPERTS])
        chosen = sb("chosen", [P, PAIR, EXPERTS], BF16)
        gain = sb("gain", [P, EXPERTS])
        count = sb("count", [P, EXPERTS])
        before = sb("before", [P, EXPERTS], BF16)
        slot = sb("slot", [P, PAIR, EXPERTS])
        over = sb("over", [P, PAIR, EXPERTS])
        slot_of = sb("slot_of", [P, PAIR, TOPK, EXPERTS])
        row_u = [sb(f"row_u{i}", [P, PAIR, TOPK], U32) for i in range(2)]
        row_f = sb("row_f", [P, PAIR, TOPK])
        ldiff = sb("ldiff", [P, PAIR])
        lexp = sb("lexp", [P, PAIR])
        lsum = sb("lsum", [P, PAIR])
        lrec = sb("lrec", [P, PAIR])
        tok = sb("tok", [P, PAIR])
        pair_tokens = sb("pair_tokens", [P, PAIR])

        xs = [sb(f"xs{i}", [P, ST, PAY]) for i in range(2)]
        xeT = sb("xeT", [P, 2, CAPACITY])
        bcol = sb("bcol", [P, 2, EV])
        hid = sb("hid", [P, 2, CAPACITY])
        yeT = sb("yeT", [P, CAPACITY])
        ys = [sb(f"ys{i}", [P, ST, C]) for i in range(2)]
        expert = sb("expert", [P, 2])
        two = sb("two", [P, 1])
        gate1 = sb("gate1", [P, ST])
        gate2 = sb("gate2", [P, ST])
        slot_gate = sb("slot_gate", [P, 2, ST])
        slot_tok = [sb(f"slot_tok{i}", [P, ST], U32) for i in range(2)]
        ac = sb("ac", [P, 2, SUPT, C])
        ga_rows = sb("ga_rows", [P, 2, 2, C])
        x2 = sb("x2", [P, 2, SUPT, C])
        stat2 = sb("stat2", [P, SUPT, 6])
        mv2 = sb("mv2", [P, SUPT, 2])
        var2 = sb("var2", [P, SUPT])
        rstd2 = sb("rstd2", [P, SUPT])
        spare = sb("spare", [P, 2])
        xh2 = sb("xh2", [P, SUPT, C])
        modc = sb("modc", [P, 2, 2, 4])
        hT = sb("hT", [P, 2, SUPT * P])
        hid2 = sb("hid2", [P, 2, SUPT * P])
        y2T = sb("y2T", [P, SUPT * P])
        res = sb("res", [P, 2, SUPT, C])

        ld_const, ld_c, ld_wmod, ld_bias, ld_vec, ld_empty = (sem(f"ld_{n}") for n in ("const", "c", "wmod", "bias", "vec", "empty"))
        ld_x = sems("ld_x", 4)
        ld_kvg, ld_q, ld_o, ld_r, ld_ffn = (sem(f"ld_{n}") for n in ("kvg", "q", "o", "r", "ffn"))
        st_mod, st_empty, st_dummy = sem("st_mod"), sem("st_empty"), sem("st_dummy")
        setup_pool, tanh_c, silu_ok, siluT_mm, siluT_ok, mod_mm, mod_ok = (
            sem(n) for n in ("setup_pool", "tanh_c", "silu_ok", "siluT_mm", "siluT_ok", "mod_mm", "mod_ok"))
        modT_mm, modT_ok, bias_ok, stat_ok, rstd_ok, nmr_ok, setup_dve = (
            sem(n) for n in ("modT_mm", "modT_ok", "bias_ok", "stat_ok", "rstd_ok", "nmr_ok", "setup_dve"))
        mod_step, ln_step, bias_step, stat_n, tok_ok = (sem(n) for n in ("mod_step", "ln_step", "bias_step", "stat_n", "tok_ok"))
        ld_rows = sems("ld_rows")
        (xhat_ok, h_ok, h_step, ms1_ok, r1_ok, hn_ok, hn_tr, hnT_ok) = (
            sem(n) for n in ("xhat_ok", "h_ok", "h_step", "ms1_ok", "r1_ok", "hn_ok", "hn_tr", "hnT_ok"))
        (kvg_mm, q_mm, kab_ok, qab_ok, ka_ok, qa_ok, kexp_ok, krel_ok, qexp_ok, qrel_ok, kphi_ok, qphi_ok, v_ok, g_ok) = (
            sem(n) for n in ("kvg_mm", "q_mm", "kab_ok", "qab_ok", "ka_ok", "qa_ok", "kexp_ok", "krel_ok", "qexp_ok", "qrel_ok",
                             "kphi_ok", "qphi_ok", "v_ok", "g_ok"))
        (kv_mm, state_ok, num_mm, gnum_ok, den_ok, rden_ok, o_ok, o_tr, oT_ok) = (
            sem(n) for n in ("kv_mm", "state_ok", "num_mm", "gnum_ok", "den_ok", "rden_ok", "o_ok", "o_tr", "oT_ok"))
        (ao_mm, x1_ok, ms2_ok, r2_ok, xf_ok, xf_tr, xfT_ok, logit_mm) = (
            sem(n) for n in ("ao_mm", "x1_ok", "ms2_ok", "r2_ok", "xf_ok", "xf_tr", "xfT_ok", "logit_mm"))
        st_x1 = sems("st_x1")
        (logit_ok, routing, chosen_ok, before_ok, pos_mm, ldiff_ok, lexp_ok, row_ok, gates_ok) = (
            sem(n) for n in ("logit_ok", "routing", "chosen_ok", "before_ok", "pos_mm", "ldiff_ok", "lexp_ok", "row_ok", "gates_ok"))
        ld_w, ld_slots = sems("ld_w"), sems("ld_slots")
        (x_tr, xeT_ok, up_mm, gelu_ok, down_mm, yeT_ok, y_tr, ys_ok, gate_step, slot_gate_ok, slot_tok_ok, expert_ok, added) = (
            sem(n) for n in ("x_tr", "xeT_ok", "up_mm", "gelu_ok", "down_mm", "yeT_ok", "y_tr", "ys_ok", "gate_step",
                             "slot_gate_ok", "slot_tok_ok", "expert_ok", "added"))
        ld_ac, st_out = sems("ld_ac"), sems("st_out")
        (ga_step, x2_ok, stat2_ok, mv2_ok, var2_ok, rstd2_ok, xh2_ok, modc_ok, x2_tr, hT_ok, up2_mm, gelu2_ok, down2_mm,
         y2T_ok, y2_tr, res_ok, spare_ok) = (
            sem(n) for n in ("ga_step", "x2_ok", "stat2_ok", "mv2_ok", "var2_ok", "rstd2_ok", "xh2_ok", "modc_ok", "x2_tr",
                             "hT_ok", "up2_mm", "gelu2_ok", "down2_mm", "y2T_ok", "y2_tr", "res_ok", "spare_ok"))
        bcol_ok = sem("bcol_ok")
        rowf_ok, slot_ok = sem("rowf_ok"), sem("slot_ok")
        scattered = sems("scattered")

        block = ctx.enter_context(nc.Block())

        kk_ps = ps[:, 0, :].rearrange("p (t n) -> p t n", t=TPB)
        vg_ps = ps[:, 1, :].rearrange("p (t n) -> p t n", t=TPB)
        q_ps = ps[:, 2, :]
        hnT_ps = ps[:, 3, 0:SEQ]
        tr_ps = ps[:, 3, SEQ:2 * SEQ]
        kv_ps = ps[:, 4:6, :]
        num_ps = ps[:, 6, 0:TPB * SW].rearrange("p (t n) -> p t n", t=TPB)
        ao_ps = ps[:, 7, 0:TPB * C].rearrange("p (t n) -> p t n", t=TPB)
        logit_ps = ps[:, 7, 256:288].rearrange("p (t e) -> p t e", e=EXPERTS)
        pos_ps = ps[:, 7, 288:320].rearrange("p (t e) -> p t e", e=EXPERTS)

        def wait(eng, s, n):
            if not isinstance(n, int) or n > 0:
                eng.wait_ge(s, n)

        def attention_phase(eng, step):
            for s in range(4):
                step(s, (s - 3) // 2, (s - 3) // 4, s, s)
            with eng.Fori(1, BATCH // 4, 1) as turn:
                for j in range(4):
                    step(turn * 4 + j, turn * 2 + (j - 3) // 2, turn + (j - 3) // 4, j, IN_LOOP)
            for s in range(BATCH, BATCH + 4):
                step(s, (s - 3) // 2, (s - 3) // 4, s % 4, s)

        def by_twos(eng, step):
            for e in range(2):
                step(e, e, e)
            with eng.Fori(1, 3, 1) as turn:
                for q in range(2):
                    step(turn * 2 + q, q, IN_LOOP)
            for e in range(6, 8):
                step(e, e - 6, e)

        def live(key, lag):
            return key == IN_LOOP or 0 <= key - lag < BATCH

        @block.sync
        def _(sp):
            sp.dma_start(konst[:, :], const_d).then_inc(ld_const, 16)
            sp.dma_start(cond[:, :], c_d).then_inc(ld_c, 16)
            sp.dma_start(wmod[:, :], wmod_d).then_inc(ld_wmod, 16)
            for i in range(4):
                n = TILES // 4
                sp.dma_start(x[:, n * i:n * i + n, :],
                             x_d[n * i * P:n * (i + 1) * P, :].rearrange("(t p) c -> p t c", p=P)).then_inc(ld_x[i], 16)
            sp.dma_start(vec[:, :], vec_d).then_inc(ld_vec, 16)
            sp.dma_start(bias[:, :], bias_d[0:1, :].to_broadcast([3, B_ALL])).then_inc(ld_bias, 16)
            sp.dma_start(wkvg[:, :], wkvg_d).then_inc(ld_kvg, 16)
            sp.dma_start(wq[:, :], wq_d).then_inc(ld_q, 16)
            sp.wait_ge(mod_ok, 1)
            sp.dma_start(mod_d, mod[:, :]).then_inc(st_mod, 16)
            sp.dma_start(wo[:, :], wo_d).then_inc(ld_o, 16)
            sp.dma_start(wr[:, :], wr_d).then_inc(ld_r, 16)

            def load_w(e, q):
                wait(sp, down_mm, 4 * (e - 1))
                sp.dma_start(w1[:, q, :], w1_d[bass.ds(e, 1), :, :].rearrange("a k n -> k (a n)")).then_inc(ld_w[q], 16)
                sp.dma_start(w2[:, q, :, :], w2_d[bass.ds(e, 1), :, :].rearrange("a (b p) c -> p (a b) c", p=P)).then_inc(ld_w[q], 16)

            sp.dma_start(empty[:, :, :], empty_d).then_inc(ld_empty, 16)
            sp.wait_ge(st_mod, 16)

            def load_rows(b, j):
                wait(sp, h_ok, b - 1)
                sp.dma_start(rows[:, j % 2, :], mod_d[bass.ds(b, 1), 0:2 * C].to_broadcast([P, 2 * C])).then_inc(ld_rows[j % 2], 16)

            sp.wait_ge(ld_empty, 16)
            for e in range(EXPERTS):
                sp.dma_start(slot_d[e * CAPACITY:(e + 1) * CAPACITY, :].rearrange("(t p) c -> p t c", p=P),
                             empty[:, :, :]).then_inc(st_empty, 16)
            sp.dma_start(acc_d[TOKENS:TOKENS + CAPACITY, :].rearrange("(t p) c -> p t c", p=P),
                         empty[:, :, 0:C]).then_inc(st_dummy, 16)

            def step(s, n, m, j, key):
                if live(key, 0):
                    load_rows(s, j)
                if live(key, 4):
                    sp.wait_ge(x1_ok, s - 3)
                    sp.dma_start(acc_d[bass.ds((s - 4) * SEQ, SEQ), :].rearrange("(t p) c -> p t c", p=P),
                                 x1[:, j % 2, :, :]).then_inc(st_x1[j % 2], 16)

            for e in range(2):
                load_w(e, e)
            sp.dma_start(f1[:, :], f1_d).then_inc(ld_ffn, 16)
            sp.dma_start(f2[:, :, :], f2_d.rearrange("(b p) c -> p b c", p=P)).then_inc(ld_ffn, 16)
            attention_phase(sp, step)
            for i in range(2):
                sp.wait_ge(st_x1[i], 16 * (BATCH // 2))
            sp.wait_ge(scattered[0], 128 * 4)
            sp.wait_ge(scattered[1], 128 * 4 + 64)
            sp.wait_ge(st_dummy, 16)

            def expert_step(e, q, key):
                if key not in (0, 1):
                    load_w(e, q)
                wait(sp, x_tr, 2 * (e - 1))
                wait(sp, slot_tok_ok, e - 1)
                wait(sp, slot_gate_ok, e - 1)
                sp.dma_start(xs[q][:, :, :], slot_d[bass.ds(e * CAPACITY, CAPACITY), :].rearrange("(t p) c -> p t c", p=P))\
                  .then_inc(ld_slots[q], 16)

            by_twos(sp, expert_step)
            sp.wait_ge(added, 16 * ST * EXPERTS)

            def group_step(g, q, key):
                wait(sp, ga_step, g - 1)
                sp.dma_start(ac[:, q, :, :], acc_d[bass.ds(g * (SUPT * P), SUPT * P), :].rearrange("(t p) c -> p t c", p=P))\
                  .then_inc(ld_ac[q], 16)
                sp.dma_start(ga_rows[:, q, :, :], mod_d[bass.ds(2 * g, 2), GA].unsqueeze(0).to_broadcast([P, 2, C]))\
                  .then_inc(ld_ac[q], 16)
                if key not in (0, 1):
                    store(g - 2, q)

            def store(g, q):
                sp.wait_ge(res_ok, g + 1)
                sp.dma_start(out_d[bass.ds(g * (SUPT * P), SUPT * P), :].rearrange("(t p) c -> p t c", p=P),
                             res[:, q, :, :]).then_inc(st_out[q], 16)

            by_twos(sp, group_step)
            store(6, 0)
            store(7, 1)
            for i in range(2):
                sp.wait_ge(st_out[i], 16 * NSUP // 2)

        @block.gpsimd
        def _(pool):
            pool.memset(power[:, :], -0.5).then_inc(setup_pool, 1)
            pool.memset(ones3[:, :], 1.0).then_inc(setup_pool, 1)
            pool.memset(ones[:, :], 1.0).then_inc(setup_pool, 1)
            pool.memset(vone[:, :, :, C:SW], 1.0).then_inc(setup_pool, 1)
            pool.memset(count[:, :], 0.0).then_inc(setup_pool, 1)
            pool.memset(pay[1][:, TPB:PAIR, :], 0.0).then_inc(setup_pool, 1)
            pool.memset(row_u[1][:, TPB:PAIR, :], SLOTS).then_inc(setup_pool, 1)
            pool.memset(pair_tokens[:, :], float(PAIR * P)).then_inc(setup_pool, 1)
            pool.memset(expert[:, 0:1], 0.0).then_inc(setup_pool, 1)
            pool.memset(expert[:, 1:2], 1.0).then_inc(setup_pool, 1)
            pool.memset(two[:, :], 2.0).then_inc(setup_pool, 1)
            pool.wait_ge(setup_pool, 11)
            pool.wait_ge(stat_ok, 1)
            pool.tensor_tensor(rstd[:, :], var[:, :], power[:, :], ALU.pow).then_inc(rstd_ok, 1)

            def scatter(q, tiles):
                for t in tiles:
                    for k in range(TOPK):
                        pool.indirect_dma_start(
                            slot_d[:, :], bass.IndirectOffsetOnAxis(row_u[q][:, t, k:k + 1], 0),
                            pay[q][:, t, :], None,
                            bounds_check=SLOTS - 1, oob_is_err=False).then_inc(scattered[q], 16)

            def step(s, n, m, j, key):
                if key == 3:
                    pool.wait_ge(st_empty, 16 * EXPERTS)
                if live(key, 0):
                    pool.wait_ge(ms1_ok, s + 1)
                    pool.tensor_tensor(r1[:, j % 2, :], ms1[:, j % 2, :], power[:, 0:TPB], ALU.pow).then_inc(r1_ok, 1)
                if live(key, 1):
                    pool.wait_ge(kab_ok, s)
                    wait(pool, krel_ok, s - 1)
                    pool.tensor_tensor(ka[:, :, :], kab[:, :, 0:C], kab[:, :, C:2 * C], ALU.add).then_inc(ka_ok, 1)
                    pool.wait_ge(qab_ok, s)
                    wait(pool, qrel_ok, s - 1)
                    pool.tensor_tensor(qa[:, :], qab[:, 0:SEQ], qab[:, SEQ:2 * SEQ], ALU.add).then_inc(qa_ok, 1)
                if live(key, 3):
                    pool.wait_ge(ms2_ok, s - 2)
                    pool.tensor_tensor(r2[:, (j + 1) % 2, :], ms2[:, (j + 1) % 2, :], power[:, 0:TPB], ALU.pow).then_inc(r2_ok, 1)
                if j % 2 == 1 and live(key, 5):
                    pool.wait_ge(row_ok, n)
                    pool.wait_ge(gates_ok, 3 * n)
                    pool.wait_ge(xf_ok, s - 3)
                    pool.tensor_tensor(tok[:, :], tok[:, :], pair_tokens[:, :], ALU.add).then_inc(tok_ok, 1)
                    scatter((j // 2) % 2, (0, 1))
                if j % 2 == 0 and live(key, 6):
                    scatter(((j + 3) % 4 // 2) % 2, (2, 3))

            attention_phase(pool, step)
            scatter(1, (2, 3))

            def expert_step(e, q, key):
                pool.wait_ge(slot_tok_ok, e + 1)
                pool.wait_ge(slot_gate_ok, e + 1)
                wait(pool, added, 16 * ST * e)
                pool.wait_ge(ys_ok, 2 * e + 2)
                pool.tensor_tensor(expert[:, q:q + 1], expert[:, q:q + 1], two[:, :], ALU.add).then_inc(expert_ok, 1)
                for t in range(ST):
                    pool.indirect_dma_start(acc_d[:, :], bass.IndirectOffsetOnAxis(slot_tok[q][:, t:t + 1], 0),
                                            ys[q][:, t, :], None, compute_op=ALU.add).then_inc(added, 16)

            by_twos(pool, expert_step)

            def group_step(g, q, key):
                pool.wait_ge(var2_ok, g + 1)
                wait(pool, xh2_ok, g)
                pool.tensor_tensor(rstd2[:, :], var2[:, :], power[:, 0:SUPT], ALU.pow).then_inc(rstd2_ok, 1)

            by_twos(pool, group_step)

        @block.scalar
        def _(act):
            act.wait_ge(ld_c, 16)
            act.activation(cond_t[:, :], cond[:, :], ACT.Tanh, scale=0.5).then_inc(tanh_c, 1)
            act.wait_ge(nmr_ok, 1)
            act.wait_ge(ld_vec, 16)

            def step(s, n, m, j, key):
                q = j % 2
                if live(key, 0):
                    for t in range(TPB):
                        tile = bass.ds(s * TPB + t, 1)
                        ins = act.activation(xhat[:, q, t, :], x[:, tile, :].rearrange("p a c -> p (a c)"), ACT.Identity,
                                             bias=nmr[:, tile], scale=rstd[:, tile])
                    ins.then_inc(xhat_ok, 1)
                if live(key, 1):
                    act.wait_ge(kvg_mm, s)
                    wait(act, kv_mm, 2 * (s - 2))
                    act.activation(vone[:, 1 - q, :, 0:C], vg_ps[:, :, 0:C], ACT.Copy).then_inc(v_ok, 1)
                    wait(act, gnum_ok, s - 2)
                    act.activation(gate[:, 1 - q, :, :], vg_ps[:, :, C:2 * C], ACT.Tanh, scale=0.5).then_inc(g_ok, 1)
                if live(key, 0):
                    act.wait_ge(h_ok, s + 1)
                    wait(act, r1_ok, s - 1)
                    wait(act, ms1_ok, s)
                    for t in range(TPB):
                        ins = act.activation(junk[:, t, :], h[:, j, t, :], ACT.Square, scale=float(C) ** -0.5,
                                             accum_out=ms1[:, q, t:t + 1])
                    ins.then_inc(ms1_ok, 1)
                if live(key, 3):
                    act.wait_ge(x1_ok, s - 2)
                    wait(act, r2_ok, s - 4)
                    wait(act, ms2_ok, s - 3)
                    for t in range(TPB):
                        ins = act.activation(junk2[:, t, :], x1[:, 1 - q, t, :], ACT.Square, scale=float(C) ** -0.5,
                                             accum_out=ms2[:, 1 - q, t:t + 1])
                    ins.then_inc(ms2_ok, 1)
                if live(key, 0):
                    act.wait_ge(r1_ok, s + 1)
                    wait(act, hn_tr, s)
                    for t in range(TPB):
                        ins = act.activation(hn[:, t, :], h[:, j, t, :], ACT.Copy, scale=r1[:, q, t:t + 1])
                    ins.then_inc(hn_ok, 1)
                if live(key, 1):
                    act.wait_ge(ka_ok, s)
                    wait(act, kphi_ok, s - 1)
                    act.activation(kexp[:, :, :], ka[:, :, :], ACT.Exp).then_inc(kexp_ok, 1)
                    act.activation(krel[:, :, :], ka[:, :, :], ACT.Relu).then_inc(krel_ok, 1)
                if live(key, 0):
                    act.wait_ge(hn_tr, s + 1)
                    wait(act, q_mm, s - 1)
                    act.activation(hnT[:, q, :], hnT_ps, ACT.Copy, scale=vec[:, V_S1:V_S1 + 1]).then_inc(hnT_ok, 1)
                if j % 2 == 1 and live(key, 5):
                    act.wait_ge(ldiff_ok, n)
                    act.activation(lexp[:, :], ldiff[:, :], ACT.Exp).then_inc(lexp_ok, 1)
                if live(key, 1):
                    act.wait_ge(qa_ok, s)
                    wait(act, qphi_ok, s - 1)
                    act.activation(qexp[:, :], qa[:, :], ACT.Exp).then_inc(qexp_ok, 1)
                    act.activation(qrel[:, :], qa[:, :], ACT.Relu).then_inc(qrel_ok, 1)
                if live(key, 3):
                    pay_q = ((j + 1) % 4) // 2
                    act.wait_ge(r2_ok, s - 2)
                    if (j + 1) % 2 == 0 and key != 3:
                        act.wait_ge(scattered[pay_q], m * 128 + 64 * pay_q)
                    for t in range(TPB):
                        ins = act.activation(pay[pay_q][:, TPB * ((j + 1) % 2) + t, 0:C], x1[:, 1 - q, t, :], ACT.Copy,
                                             scale=r2[:, 1 - q, t:t + 1])
                    ins.then_inc(xf_ok, 1)
                if live(key, 2):
                    act.wait_ge(o_tr, s - 1)
                    wait(act, ao_mm, s - 3)
                    act.activation(oT[:, q, :], tr_ps, ACT.Copy).then_inc(oT_ok, 1)
                if live(key, 3):
                    act.wait_ge(xf_tr, s - 2)
                    wait(act, logit_mm, s - 3)
                    act.activation(xfT[:, :], tr_ps, ACT.Copy, scale=vec[:, V_S2:V_S2 + 1]).then_inc(xfT_ok, 1)

            attention_phase(act, step)

            def expert_step(e, q, key):
                act.wait_ge(bcol_ok, e + 1)
                for k in range(HB):
                    wait(act, down_mm, 4 * e + k - 1)
                    for i, (a, b) in enumerate(PARTS):
                        act.wait_ge(up_mm, 8 * e + 2 * k + i + 1)
                        act.activation(hid[:, k % 2, a:b], ps[:, 2 + 2 * (k % 2) + i, 0:b - a], ACT.Gelu,
                                       bias=bcol[:, q, k:k + 1]).then_inc(gelu_ok, 1)
                act.wait_ge(down_mm, 4 * e + 4)
                wait(act, y_tr, 2 * e)
                for i, (a, b) in enumerate(PARTS):
                    act.activation(yeT[:, a:b], ps[:, 6 + i, 0:b - a], ACT.Identity,
                                   bias=bcol[:, q, HB:EV]).then_inc(yeT_ok, 1)

            by_twos(act, expert_step)

            def modulated(g, q):
                act.wait_ge(x2_tr, g + 1)
                act.wait_ge(modc_ok, g + 1)
                wait(act, up2_mm, 4 * (g - 1))
                for i in range(2):
                    act.activation(hT[:, q, SEQ * i:SEQ * i + SEQ], ps[:, 0, SEQ * i:SEQ * i + SEQ], ACT.Identity,
                                   scale=modc[:, q, i, 1:2], bias=modc[:, q, i, 0:1]).then_inc(hT_ok, 1)

            def group_step(g, q, key):
                for k in range(HB):
                    act.wait_ge(up2_mm, 4 * g + k + 1)
                    wait(act, down2_mm, 4 * g + k - 1)
                    act.activation(hid2[:, k % 2, :], ps[:, 2 + k % 2, :], ACT.Gelu,
                                   bias=vec[:, V_FB1 + k:V_FB1 + k + 1]).then_inc(gelu2_ok, 1)
                    if k == 2 and key != NSUP - 1:
                        modulated(g + 1, 1 - q)
                act.wait_ge(down2_mm, 4 * g + 4)
                wait(act, y2_tr, g)
                for i in range(2):
                    act.activation(y2T[:, SEQ * i:SEQ * i + SEQ], ps[:, 4 + q, SEQ * i:SEQ * i + SEQ], ACT.Identity,
                                   scale=modc[:, q, i, 2:3], bias=modc[:, q, i, 3:4]).then_inc(y2T_ok, 1)

            modulated(0, 0)
            by_twos(act, group_step)

        @block.vector
        def _(dve):
            dve.wait_ge(ld_x[0], 16)
            for i in range(4):
                n = TILES // 4
                if i:
                    dve.wait_ge(ld_x[i], 16)
                if i == 1:
                    dve.wait_ge(tanh_c, 1)
                    dve.scalar_tensor_tensor(out=silu[:, :], in0=cond_t[:, :], scalar=1.0, in1=cond[:, :],
                                             op0=ALU.add, op1=ALU.mult).then_inc(setup_dve, 1)
                    dve.wait_ge(setup_dve, 1)
                    dve.tensor_scalar(silu[:, :], silu[:, :], 0.5, None, ALU.mult).then_inc(silu_ok, 1)
                if i == 2:
                    dve.wait_ge(siluT_mm, 1)
                    dve.tensor_copy(siluT[:, :], ps[:, 7, 0:BATCH]).then_inc(siluT_ok, 1)
                for t in range(n * i, n * (i + 1)):
                    dve.bn_stats(stat[:, t, :], x[:, t, :]).then_inc(stat_n, 1)
            dve.wait_ge(mod_mm, 1)
            dve.tensor_copy(mod[:, 0:512], ps[0:BATCH, 5, 0:512]).then_inc(mod_step, 1)
            dve.tensor_copy(mod[:, 512:768], ps[0:BATCH, 6, 0:256]).then_inc(mod_step, 1)
            dve.wait_ge(mod_step, 2)
            dve.tensor_scalar(mod[:, CA], mod[:, CA], 1.0, None, ALU.add).then_inc(mod_step, 1)
            dve.tensor_scalar(mod[:, CB], mod[:, CB], 1.0, None, ALU.add).then_inc(mod_step, 1)
            g = mod[:, :].rearrange("b (k m c) -> b k m c", k=2, m=3)[:, :, 2, :]
            dve.tensor_scalar(mod_s[:, :, :], g, 0.0, 2.0, ALU.is_ge, ALU.mult).then_inc(mod_step, 1)
            dve.scalar_tensor_tensor(out=mod_m[:, :, :], in0=g, scalar=-1.0, in1=g, op0=ALU.mult, op1=ALU.max).then_inc(mod_step, 1)
            dve.wait_ge(mod_step, 6)
            dve.tensor_scalar(mod_s[:, :, :], mod_s[:, :, :], 1.0, None, ALU.subtract).then_inc(mod_step, 1)
            dve.tensor_scalar(mod_m[:, :, :], mod_m[:, :, :], 0.25, None, ALU.max).then_inc(mod_step, 1)
            dve.wait_ge(mod_step, 8)
            dve.tensor_tensor(g, mod_s[:, :, :], mod_m[:, :, :], ALU.mult).then_inc(mod_ok, 1)

            dve.wait_ge(stat_n, TILES)
            dve.tensor_tensor(mean[:, :], stat[:, :, 1], stat[:, :, 4], ALU.add).then_inc(ln_step, 1)
            dve.tensor_tensor(dmean[:, :], stat[:, :, 1], stat[:, :, 4], ALU.subtract).then_inc(ln_step, 1)
            dve.tensor_tensor(var[:, :], stat[:, :, 2], stat[:, :, 5], ALU.add).then_inc(ln_step, 1)
            dve.wait_ge(ln_step, 3)
            dve.tensor_scalar(mean[:, :], mean[:, :], 0.5, None, ALU.mult).then_inc(ln_step, 1)
            dve.tensor_tensor(dmean[:, :], dmean[:, :], dmean[:, :], ALU.mult).then_inc(ln_step, 1)
            dve.tensor_scalar(var[:, :], var[:, :], 1.0 / C, 1e-5, ALU.mult, ALU.add).then_inc(ln_step, 1)
            dve.wait_ge(ln_step, 6)
            dve.scalar_tensor_tensor(out=var[:, :], in0=dmean[:, :], scalar=0.25, in1=var[:, :], op0=ALU.mult,
                                     op1=ALU.add).then_inc(stat_ok, 1)
            dve.wait_ge(ld_bias, 16)
            dve.wait_ge(ld_const, 16)
            sel = konst[0:3, K_SEL:K_SEL + 3]
            dve.tensor_copy(bpart[:, :], bias[:, :]).then_inc(bias_step, 1)
            dve.wait_ge(bias_step, 1)
            dve.tensor_scalar(bsum[:, :], bpart[:, :], sel[:, 0:1], None, ALU.mult).then_inc(bias_step, 1)
            dve.tensor_tensor(bias[:, :], bias[:, :], bpart[:, :], ALU.subtract).then_inc(bias_step, 1)
            dve.wait_ge(bias_step, 3)
            dve.tensor_copy(bpart[:, :], bias[:, :]).then_inc(bias_step, 1)
            dve.wait_ge(bias_step, 4)
            dve.scalar_tensor_tensor(out=bsum[:, :], in0=bpart[:, :], scalar=sel[:, 1:2], in1=bsum[:, :],
                                     op0=ALU.mult, op1=ALU.add).then_inc(bias_step, 1)
            dve.tensor_tensor(bias[:, :], bias[:, :], bpart[:, :], ALU.subtract).then_inc(bias_step, 1)
            dve.wait_ge(bias_step, 6)
            dve.scalar_tensor_tensor(out=bias3[:, :], in0=bias[:, :], scalar=sel[:, 2:3], in1=bsum[:, :],
                                     op0=ALU.mult, op1=ALU.add).then_inc(bias_ok, 1)
            dve.tensor_copy(tri[:, :], konst[:, K_TRI:K_TRI + P]).then_inc(bias_ok, 1)
            dve.wait_ge(rstd_ok, 1)
            dve.scalar_tensor_tensor(out=nmr[:, :], in0=mean[:, :], scalar=-1.0, in1=rstd[:, :], op0=ALU.mult,
                                     op1=ALU.mult).then_inc(nmr_ok, 1)
            dve.wait_ge(modT_mm, 1)
            dve.wait_ge(ld_vec, 16)
            dve.tensor_copy(modT[:, :, 0:3], ps[:, 7, 32:32 + 3 * BATCH].rearrange("p (k b) -> p b k", k=3)).then_inc(modT_ok, 1)
            dve.wait_ge(modT_ok, 1)
            dve.tensor_scalar(modT[:, :, 3:4], modT[:, :, 2:3], vec[:, V_FB2:V_FB2 + 1], None, ALU.mult).then_inc(modT_ok, 1)
            dve.tensor_scalar(tok[:, :], konst[:, K_TOK:K_TOK + PAIR], 0.0, None, ALU.add).then_inc(tok_ok, 1)

            ktab = konst[:, K_KTAB:K_KTAB + 512].rearrange("p (t n) -> p t n", t=TPB)
            qtab = konst[:, K_QTAB:K_QTAB + 512]
            mask = konst[:, K_MASK:K_MASK + SW].unsqueeze(1).to_broadcast([P, 2, SW])
            iota = konst[:, K_IOTA:K_IOTA + EXPERTS].unsqueeze(1).unsqueeze(1).to_broadcast([P, PAIR, TOPK, EXPERTS])
            base = konst[:, K_BASE:K_BASE + EXPERTS].unsqueeze(1).to_broadcast([P, PAIR, EXPERTS])

            def step(s, n, m, j, key):
                q = j % 2
                odd = j % 2 == 1 and live(key, 5)
                if odd:
                    buf = pay[j // 2]
                    dve.wait_ge(logit_mm, s - 3)
                    dve.tensor_copy(logit[:, :, :], logit_ps).then_inc(logit_ok, 1)
                    dve.wait_ge(logit_ok, n)
                    dve.tensor_copy(before[:, :], count[:, :]).then_inc(before_ok, 1)
                    for t in range(PAIR):
                        dve.max(top[:, t, :], logit[:, t, :]).then_inc(routing, 1)
                    dve.wait_ge(routing, ROUTE * (n - 1) + 4)
                    dve.tensor_tensor(ldiff[:, :], top[:, :, 1], top[:, :, 0], ALU.subtract).then_inc(ldiff_ok, 1)
                    for t in range(PAIR):
                        dve.max_index(topi[:, t, :], top[:, t, :], logit[:, t, :]).then_inc(routing, 1)
                if live(key, 0):
                    dve.wait_ge(ld_rows[q], s * 8 + (16 - 8 * q))
                    dve.wait_ge(xhat_ok, s + 1)
                    wait(dve, hn_ok, s - 3)
                    ca = rows[:, q, C:2 * C].unsqueeze(1).to_broadcast([P, TPB, C])
                    sa = rows[:, q, 0:C].unsqueeze(1).to_broadcast([P, TPB, C])
                    wait(dve, x1_ok, s - 3)
                    dve.tensor_tensor(h[:, j, :, :], xhat[:, q, :, :], ca, ALU.mult).then_inc(h_step, 1)
                    dve.wait_ge(h_step, s + 1)
                    dve.tensor_tensor(h[:, j, :, :], h[:, j, :, :], sa, ALU.add).then_inc(h_ok, 1)
                if live(key, 1):
                    dve.wait_ge(kvg_mm, s)
                    wait(dve, ka_ok, s - 1)
                    dve.tensor_tensor(kab[:, :, :], kk_ps, ktab, ALU.mult).then_inc(kab_ok, 1)
                    dve.wait_ge(q_mm, s)
                    wait(dve, qa_ok, s - 1)
                    dve.tensor_tensor(qab[:, :], q_ps, qtab, ALU.mult).then_inc(qab_ok, 1)
                if odd:
                    dve.wait_ge(xf_ok, s - 3)
                    dve.wait_ge(routing, ROUTE * (n - 1) + 8)
                    dve.tensor_copy(buf[:, :, E1:E2 + 1], topi[:, :, 0:TOPK]).then_inc(routing, 1)
                    dve.wait_ge(routing, ROUTE * (n - 1) + 9)
                    dve.tensor_tensor(hot[:, :, :, :], iota,
                                      buf[:, :, E1:E2 + 1].unsqueeze(3).to_broadcast([P, PAIR, TOPK, EXPERTS]),
                                      ALU.is_equal).then_inc(routing, 1)
                    dve.wait_ge(routing, ROUTE * (n - 1) + 10)
                    dve.tensor_tensor(chosen[:, :, :], hot[:, :, 0, :], hot[:, :, 1, :], ALU.add).then_inc(chosen_ok, 1)
                    dve.wait_ge(chosen_ok, n)
                    dve.tensor_reduce(gain[:, :], chosen[:, :, :].rearrange("p t e -> p e t"), AX.X, ALU.add).then_inc(routing, 1)
                    dve.wait_ge(routing, ROUTE * (n - 1) + 11)
                    dve.tensor_tensor(count[:, :], count[:, :], gain[:, :], ALU.add).then_inc(routing, 1)
                if live(key, 2):
                    for i in range(2):
                        dve.wait_ge(kv_mm, 2 * (s - 2) + i + 1)
                        wait(dve, num_mm, s - 2)
                        dve.tensor_tensor(state[:, 2 * i:2 * i + 2, :],
                                          kv_ps[:, i, 0:2 * SW].rearrange("p (a n) -> p a n", a=2), mask,
                                          ALU.mult).then_inc(state_ok, 1)
                if live(key, 3):
                    dve.wait_ge(ao_mm, s - 2)
                    if not (isinstance(s, int) and s < 5):
                        dve.wait_ge(st_x1[1 - q], 8 * (s - 4 + q))
                        dve.wait_ge(xf_ok, s - 4)
                    dve.tensor_tensor(x1[:, 1 - q, :, :], ao_ps, h[:, (j + 1) % 4, :, :], ALU.add).then_inc(x1_ok, 1)
                if live(key, 1):
                    dve.wait_ge(krel_ok, s)
                    wait(dve, kv_mm, 2 * (s - 2))
                    dve.scalar_tensor_tensor(out=kphi[:, 1 - q, :, :], in0=kexp[:, :, :], scalar=1.0, in1=krel[:, :, :],
                                             op0=ALU.min, op1=ALU.add).then_inc(kphi_ok, 1)
                    dve.wait_ge(qrel_ok, s)
                    wait(dve, num_mm, s - 2)
                    dve.scalar_tensor_tensor(out=qphi[:, 1 - q, :], in0=qexp[:, :], scalar=1.0, in1=qrel[:, :],
                                             op0=ALU.min, op1=ALU.add).then_inc(qphi_ok, 1)
                if odd:
                    dve.wait_ge(pos_mm, n)
                    dve.tensor_tensor(slot[:, :, :], pos_ps, base, ALU.add).then_inc(slot_ok, 1)
                    dve.tensor_scalar(over[:, :, :], pos_ps, float(CAPACITY), FAR, ALU.is_ge, ALU.mult).then_inc(slot_ok, 1)
                    dve.wait_ge(slot_ok, 2 * n)
                    dve.tensor_tensor(slot[:, :, :], slot[:, :, :], over[:, :, :], ALU.add).then_inc(routing, 1)
                    dve.wait_ge(lexp_ok, n)
                    dve.tensor_scalar(lsum[:, :], lexp[:, :], 1.0, None, ALU.add).then_inc(routing, 1)
                    dve.wait_ge(routing, ROUTE * (n - 1) + 13)
                    for k in range(TOPK):
                        dve.tensor_tensor(slot_of[:, :, k, :], hot[:, :, k, :], slot[:, :, :], ALU.mult).then_inc(routing, 1)
                    dve.wait_ge(routing, ROUTE * (n - 1) + 14)
                    dve.reciprocal(lrec[:, :], lsum[:, :]).then_inc(routing, 1)
                    dve.wait_ge(routing, ROUTE * (n - 1) + 16)
                    dve.tensor_reduce(row_f[:, :, :], slot_of[:, :, :, :], AX.X, ALU.add).then_inc(rowf_ok, 1)
                    dve.wait_ge(tok_ok, n)
                    dve.tensor_copy(buf[:, :, ID], tok[:, :]).then_inc(gates_ok, 1)
                    dve.wait_ge(routing, ROUTE * (n - 1) + 17)
                    dve.wait_ge(rowf_ok, n)
                    dve.tensor_copy(row_u[j // 2][:, :, :], row_f[:, :, :]).then_inc(row_ok, 1)
                    dve.tensor_copy(buf[:, :, G1], lrec[:, :]).then_inc(gates_ok, 1)
                    dve.tensor_tensor(buf[:, :, G2], lexp[:, :], lrec[:, :], ALU.mult).then_inc(gates_ok, 1)
                if live(key, 2):
                    dve.wait_ge(num_mm, s - 1)
                    dve.wait_ge(g_ok, s - 1)
                    dve.tensor_scalar(den[:, :, :], num_ps[:, :, C:SW], 2.0, 2e-6, ALU.mult, ALU.add).then_inc(den_ok, 1)
                    dve.scalar_tensor_tensor(out=gnum[:, :, :], in0=gate[:, q, :, :], scalar=1.0, in1=num_ps[:, :, 0:C],
                                             op0=ALU.add, op1=ALU.mult).then_inc(gnum_ok, 1)
                    dve.wait_ge(den_ok, s - 1)
                    dve.reciprocal(rden[:, :, :], den[:, :, :]).then_inc(rden_ok, 1)
                    dve.wait_ge(rden_ok, s - 1)
                    wait(dve, o_tr, s - 2)
                    dve.tensor_tensor(o[:, :, :].rearrange("p t (g d) -> p (t g) d", d=DK),
                                      gnum[:, :, :].rearrange("p t (g d) -> p (t g) d", d=DK),
                                      rden[:, :, :].rearrange("p t g -> p (t g)").unsqueeze(2).to_broadcast([P, TPB * HEADS, DK]),
                                      ALU.mult).then_inc(o_ok, 1)

            attention_phase(dve, step)

            def slots_in(e, q):
                dve.wait_ge(ld_slots[q], 8 * (e - q) + 16)
                wait(dve, expert_ok, e - 1)
                wait(dve, ys_ok, 2 * (e - 1))
                wait(dve, slot_gate_ok, e)
                for k, (gcol, ecol, out) in enumerate(((G1, E1, gate1), (G2, E2, gate2))):
                    dve.scalar_tensor_tensor(out=out[:, :], in0=xs[q][:, :, ecol], scalar=expert[:, q:q + 1], in1=xs[q][:, :, gcol],
                                             op0=ALU.is_equal, op1=ALU.mult).then_inc(gate_step, 1)
                wait(dve, added, 16 * ST * (e - 1))
                dve.tensor_copy(slot_tok[q][:, :], xs[q][:, :, ID]).then_inc(slot_tok_ok, 1)
                dve.wait_ge(gate_step, 2 * e + 2)
                dve.tensor_tensor(slot_gate[:, q, :], gate1[:, :], gate2[:, :], ALU.add).then_inc(slot_gate_ok, 1)
                wait(dve, yeT_ok, 2 * (e - 1))
                dve.tensor_scalar(bcol[:, q, :], vec[:, bass.ds(e * EV + V_B1, EV)], 1.0, None, ALU.mult).then_inc(bcol_ok, 1)
                for i, (a, b) in enumerate(PARTS):
                    dve.wait_ge(x_tr, 2 * e + i + 1)
                    wait(dve, up_mm, 8 * (e - 1))
                    dve.tensor_scalar(xeT[:, q, a:b], ps[:, i, 0:b - a], vec[:, V_S2:V_S2 + 1], None, ALU.mult).then_inc(xeT_ok, 1)

            def gated(e, q):
                wait(dve, added, 16 * ST * (e - 1))
                dve.wait_ge(slot_gate_ok, e + 1)
                for i, (a, b) in enumerate(PARTS):
                    t0, t1 = a // P, b // P
                    dve.wait_ge(y_tr, 2 * e + i + 1)
                    dve.tensor_tensor(ys[q][:, t0:t1, :], ps[:, i, 0:b - a].rearrange("p (t c) -> p t c", c=C),
                                      slot_gate[:, q, t0:t1].unsqueeze(2).to_broadcast([P, t1 - t0, C]),
                                      ALU.mult).then_inc(ys_ok, 1)

            def expert_step(e, q, key):
                if key != 0:
                    gated(e - 1, 1 - q)
                if key != EXPERTS - 1:
                    slots_in(e + 1, 1 - q)

            slots_in(0, 0)
            by_twos(dve, expert_step)
            gated(EXPERTS - 1, 1)

            def group_in(g, q):
                dve.wait_ge(ld_ac[q], 16 * (g - q) + 32)
                wait(dve, res_ok, g - 1)
                dve.tensor_tensor(x2[:, q, :, :].rearrange("p (b t) c -> p b t c", b=2),
                                  ac[:, q, :, :].rearrange("p (b t) c -> p b t c", b=2),
                                  ga_rows[:, q, :, :].unsqueeze(2).to_broadcast([P, 2, TPB, C]), ALU.mult).then_inc(ga_step, 1)
                dve.wait_ge(ga_step, g + 1)
                dve.tensor_tensor(x2[:, q, :, :], x2[:, q, :, :], x[:, bass.ds(g * SUPT, SUPT), :], ALU.add).then_inc(x2_ok, 1)
                dve.wait_ge(x2_ok, g + 1)
                for t in range(SUPT):
                    dve.bn_stats(stat2[:, t, :], x2[:, q, t, :]).then_inc(stat2_ok, 1)
                dve.wait_ge(stat2_ok, SUPT * (g + 1))
                dve.memset(spare[:, 0:1], 0.0).then_inc(spare_ok, 1)
                for t in range(SUPT):
                    dve.bn_aggr(mv2[:, t, :], stat2[:, t, :]).then_inc(mv2_ok, 1)
                dve.wait_ge(mv2_ok, SUPT * (g + 1))
                wait(dve, rstd2_ok, g)
                dve.tensor_scalar(var2[:, :], mv2[:, :, 1], 1e-5, None, ALU.add).then_inc(var2_ok, 1)
                wait(dve, y2T_ok, 2 * (g - 1))
                dve.tensor_scalar(modc[:, q, :, :], modT[:, bass.ds(g * 2, 2), :], 1.0, None, ALU.mult).then_inc(modc_ok, 1)
                dve.wait_ge(rstd2_ok, g + 1)
                wait(dve, x2_tr, g)
                for t in range(SUPT):
                    ins = dve.tensor_scalar(xh2[:, t, :], x2[:, q, t, :], mv2[:, t, 0:1], rstd2[:, t:t + 1],
                                            ALU.subtract, ALU.mult)
                ins.then_inc(xh2_ok, 1)

            def result(g, q):
                dve.wait_ge(y2_tr, g + 1)
                wait(dve, st_out[q], 8 * (g - q))
                dve.tensor_tensor(res[:, q, :, :], ps[:, 1, :].rearrange("p (t c) -> p t c", c=C), x2[:, q, :, :],
                                  ALU.add).then_inc(res_ok, 1)

            def group_step(g, q, key):
                if key != 0:
                    result(g - 1, 1 - q)
                if key != NSUP - 1:
                    group_in(g + 1, 1 - q)

            group_in(0, 0)
            by_twos(dve, group_step)
            result(NSUP - 1, 1)

        @block.tensor
        def _(pe):
            pe.wait_ge(ld_const, 16)
            pe.wait_ge(silu_ok, 1)
            pe.transpose(ps[:, 7, 0:BATCH], silu[:, :], ident[0:BATCH, 0:BATCH]).then_inc(siluT_mm, 1)
            pe.wait_ge(siluT_ok, 1)
            pe.wait_ge(ld_wmod, 16)
            pe.matmul(ps[0:BATCH, 5, 0:512], siluT[:, :], wmod[:, 0:512], start=True, stop=True)
            pe.matmul(ps[0:BATCH, 6, 0:256], siluT[:, :], wmod[:, 512:768], start=True, stop=True).then_inc(mod_mm, 1)
            pe.wait_ge(mod_ok, 1)
            for i, part in enumerate((SB, CB, GB)):
                ins = pe.transpose(ps[:, 7, 32 + BATCH * i:32 + BATCH * (i + 1)], mod[:, part], ident[0:BATCH, 0:BATCH])
            ins.then_inc(modT_mm, 1)
            pe.wait_ge(bias_ok, 2)
            pe.wait_ge(setup_pool, 11)
            pe.wait_ge(modT_ok, 1)
            for s, n in ((ld_kvg, 16), (ld_q, 16), (ld_o, 16), (ld_r, 16)):
                pe.wait_ge(s, n)

            def step(s, n, m, j, key):
                q = j % 2
                if live(key, 1):
                    pe.wait_ge(hnT_ok, s)
                    wait(pe, kab_ok, s - 1)
                    wait(pe, g_ok, s - 1)
                    for t in range(TPB):
                        for i, out in enumerate((kk_ps, vg_ps)):
                            cols = slice(2 * C * i, 2 * C * i + 2 * C)
                            pe.matmul(out[:, t, :], hnT[:, 1 - q, P * t:P * t + P], wkvg[:, cols], start=True, stop=False)
                            ins = pe.matmul(out[:, t, :], ones3[:, 0:P], bias3[:, cols], start=False, stop=True)
                    ins.then_inc(kvg_mm, 1)
                    wait(pe, qab_ok, s - 1)
                    for i in range(2):
                        half = slice(SEQ * i, SEQ * i + SEQ)
                        pe.matmul(q_ps[:, half], wq[:, C * i:C * i + C], hnT[:, 1 - q, :], start=True, stop=False)
                        ins = pe.matmul(q_ps[:, half], bias3[:, B_Q + C * i:B_Q + C * i + C], ones3[:, :], start=False, stop=True)
                    ins.then_inc(q_mm, 1)
                if live(key, 2):
                    pe.wait_ge(kphi_ok, s - 1)
                    pe.wait_ge(v_ok, s - 1)
                    wait(pe, state_ok, 2 * (s - 2))
                    for c in range(CHUNKS):
                        out = kv_ps[:, c // 2, (c % 2) * SW:(c % 2) * SW + SW]
                        ends = [P] * ((c + 1) // 2) + [CHUNK] * ((c + 1) % 2)
                        for t, end in enumerate(ends):
                            ins = pe.matmul(out, kphi[0:end, q, t, :], vone[0:end, q, t, :], start=(t == 0), stop=(t == len(ends) - 1))
                        if c % 2:
                            ins.then_inc(kv_mm, 1)
                if live(key, 3):
                    pe.wait_ge(oT_ok, s - 2)
                    pe.wait_ge(modT_ok, 1)
                    wait(pe, x1_ok, s - 3)
                    if j % 2 == 1 and live(key, 5):
                        pe.wait_ge(logit_ok, n)
                    if live(key, 6):
                        wait(pe, slot_ok, 2 * n if j % 2 == 0 else 2 * (n - 1))
                    for t in range(TPB):
                        pe.matmul(ao_ps[:, t, :], oT[:, 1 - q, P * t:P * t + P], wo[:, :], start=True, stop=False)
                        ins = pe.matmul(ao_ps[:, t, :], ones3[:, 0:P], bias3[:, B_O:B_O + C], start=False, stop=True)
                    ins.then_inc(ao_mm, 1)
                if live(key, 0):
                    pe.wait_ge(hn_ok, s + 1)
                    wait(pe, xfT_ok, s - 3)
                    for t in range(TPB):
                        ins = pe.transpose(hnT_ps[:, P * t:P * t + P], hn[:, t, :], ident)
                    ins.then_inc(hn_tr, 1)
                if live(key, 2):
                    pe.wait_ge(qphi_ok, s - 1)
                    wait(pe, gnum_ok, s - 2)
                    for c in range(CHUNKS):
                        if c % 2 == 0:
                            pe.wait_ge(state_ok, 2 * (s - 2) + c // 2 + 1)
                        at = CHUNK * (c % 2)
                        ins = pe.matmul(num_ps[at:at + CHUNK, c // 2, :], qphi[:, q, CHUNK * c:CHUNK * c + CHUNK],
                                        state[:, c, :], start=True, stop=True)
                    ins.then_inc(num_mm, 1)
                if j % 2 == 1 and live(key, 5):
                    pe.wait_ge(chosen_ok, n)
                    pe.wait_ge(logit_ok, n)
                    if live(key, 3):
                        pe.wait_ge(x1_ok, s - 2)
                    pe.matmul(pos_ps, ones[:, :], before[:, :].unsqueeze(1).to_broadcast([P, PAIR, EXPERTS]), start=True, stop=False)
                    for t in range(PAIR - 1):
                        pe.matmul(pos_ps[:, t + 1:PAIR, :], ones[:, :],
                                  chosen[:, t:t + 1, :].to_broadcast([P, PAIR - 1 - t, EXPERTS]), start=False, stop=False)
                    pe.matmul(pos_ps, tri[:, :], chosen[:, :, :], start=False, stop=True).then_inc(pos_mm, 1)
                if live(key, 2):
                    pe.wait_ge(o_ok, s - 1)
                    if live(key, 0):
                        pe.wait_ge(hnT_ok, s + 1)
                    wait(pe, xfT_ok, s - 3)
                    for t in range(TPB):
                        ins = pe.transpose(tr_ps[:, P * t:P * t + P], o[:, t, :], ident)
                    ins.then_inc(o_tr, 1)
                if live(key, 3):
                    pe.wait_ge(xf_ok, s - 2)
                    if live(key, 2):
                        pe.wait_ge(oT_ok, s - 1)
                    buf, half = pay[((j + 1) % 4) // 2], TPB * ((j + 1) % 2)
                    for t in range(TPB):
                        ins = pe.transpose(tr_ps[:, P * t:P * t + P], buf[:, half + t, 0:C], ident)
                    ins.then_inc(xf_tr, 1)
                    pe.wait_ge(xfT_ok, s - 2)
                    if j % 2 == 1 and live(key, 5):
                        pe.wait_ge(logit_ok, n)
                        pe.wait_ge(slot_ok, 2 * n)
                    for t in range(TPB):
                        pe.matmul(logit_ps[:, half + t, :], xfT[:, P * t:P * t + P], wr[:, :], start=True, stop=False)
                        ins = pe.matmul(logit_ps[:, half + t, :], ones3[:, 0:P], bias3[:, B_R:B_R + EXPERTS], start=False, stop=True)
                    ins.then_inc(logit_mm, 1)

            attention_phase(pe, step)

            def transpose_slots(e, q):
                pe.wait_ge(ld_slots[q], 8 * (e - q) + 16)
                wait(pe, ys_ok, 2 * (e - 1))
                for t in range(ST):
                    i, at = (0, P * t) if P * t < SPLIT else (1, P * t - SPLIT)
                    ins = pe.transpose(ps[:, i, at:at + P], xs[q][:, t, 0:C], ident)
                    if t in (SPLIT // P - 1, ST - 1):
                        ins.then_inc(x_tr, 1)

            def up(e, q, k):
                if k == 0:
                    pe.wait_ge(ld_w[q], 16 * (e - q) + 32)
                wait(pe, gelu_ok, 8 * e + 2 * k - 2)
                for i, (a, b) in enumerate(PARTS):
                    if k == 0:
                        pe.wait_ge(xeT_ok, 2 * e + i + 1)
                    pe.matmul(ps[:, 2 + 2 * (k % 2) + i, 0:b - a], w1[:, q, P * k:P * k + P], xeT[:, q, a:b],
                              start=True, stop=True).then_inc(up_mm, 1)

            def down(e, q, k):
                if k == 0:
                    wait(pe, yeT_ok, 2 * e)
                for i, (a, b) in enumerate(PARTS):
                    pe.wait_ge(gelu_ok, 8 * e + 2 * k + i + 1)
                    ins = pe.matmul(ps[:, 6 + i, 0:b - a], w2[:, q, k, :], hid[:, k % 2, a:b], start=(k == 0), stop=(k == HB - 1))
                ins.then_inc(down_mm, 1)

            def transpose_outputs(e):
                if not (isinstance(e, int) and e == EXPERTS - 1):
                    pe.wait_ge(xeT_ok, 2 * e + 4)
                else:
                    pe.wait_ge(ys_ok, 2 * e)
                for t in range(ST):
                    i, at = (0, P * t) if P * t < SPLIT else (1, P * t - SPLIT)
                    pe.wait_ge(yeT_ok, 2 * e + i + 1)
                    ins = pe.transpose(ps[:, i, at:at + P], yeT[:, P * t:P * t + P], ident)
                    if t in (SPLIT // P - 1, ST - 1):
                        ins.then_inc(y_tr, 1)

            def expert_step(e, q, key):
                up(e, q, 0)
                up(e, q, 1)
                if key != 0:
                    transpose_outputs(e - 1)
                down(e, q, 0)
                up(e, q, 2)
                down(e, q, 1)
                up(e, q, 3)
                if key != EXPERTS - 1:
                    transpose_slots(e + 1, 1 - q)
                down(e, q, 2)
                down(e, q, 3)

            transpose_slots(0, 0)
            by_twos(pe, expert_step)
            transpose_outputs(EXPERTS - 1)

            def transpose_group(g):
                pe.wait_ge(xh2_ok, g + 1)
                wait(pe, hT_ok, 2 * g)
                for t in range(SUPT):
                    ins = pe.transpose(ps[:, 0, P * t:P * t + P], xh2[:, t, :], ident)
                ins.then_inc(x2_tr, 1)

            def up2(g, q, k):
                if k == 0:
                    pe.wait_ge(hT_ok, 2 * g + 2)
                wait(pe, gelu2_ok, 4 * g + k - 1)
                pe.matmul(ps[:, 2 + k % 2, :], f1[:, P * k:P * k + P], hT[:, q, :], start=True, stop=True).then_inc(up2_mm, 1)

            def down2(g, q, k):
                if k == 0:
                    wait(pe, y2T_ok, 2 * (g - 1))
                pe.wait_ge(gelu2_ok, 4 * g + k + 1)
                pe.matmul(ps[:, 4 + q, :], f2[:, k, :], hid2[:, k % 2, :], start=(k == 0), stop=(k == HB - 1)).then_inc(down2_mm, 1)

            def transpose_results(g):
                pe.wait_ge(y2T_ok, 2 * g + 2)
                wait(pe, res_ok, g)
                for t in range(SUPT):
                    ins = pe.transpose(ps[:, 1, P * t:P * t + P], y2T[:, P * t:P * t + P], ident)
                ins.then_inc(y2_tr, 1)

            def group_step(g, q, key):
                up2(g, q, 0)
                up2(g, q, 1)
                if key != 0:
                    transpose_results(g - 1)
                down2(g, q, 0)
                up2(g, q, 2)
                down2(g, q, 1)
                if key != NSUP - 1:
                    transpose_group(g + 1)
                up2(g, q, 3)
                down2(g, q, 2)
                down2(g, q, 3)

            pe.wait_ge(ld_ffn, 32)
            transpose_group(0)
            by_twos(pe, group_step)
            transpose_results(NSUP - 1)


def kernel(L0_attn_x, L0_attn_norm1_scale, L0_attn_norm2_scale, L0_attn_Wq, L0_attn_bq, L0_attn_Wk, L0_attn_bk,
           L0_attn_Wv, L0_attn_bv, L0_attn_Wg, L0_attn_bg, L0_attn_Wo, L0_attn_bo, L0_attn_router_W, L0_attn_router_b,
           L0_attn_W1, L0_attn_b1, L0_attn_W2, L0_attn_b2, L0_ffn_w1, L0_ffn_b1, L0_ffn_w2, L0_ffn_b2, L0_c, L0_wmod):
    import concourse.bacc as _bacc
    from concourse.bass_utils import run_bass_kernel_spmd as _run

    def flat(a):
        return np.ascontiguousarray(np.asarray(a))

    swap = np.arange(C).reshape(HEADS, 2, DK // 2)[:, ::-1].reshape(-1)
    wq_, wk, wv, wg = (flat(w) for w in (L0_attn_Wq, L0_attn_Wk, L0_attn_Wv, L0_attn_Wg))
    bq, bk, bv, bg = (flat(w) for w in (L0_attn_bq, L0_attn_bk, L0_attn_bv, L0_attn_bg))
    columns = [flat(L0_attn_norm1_scale)[:, None], flat(L0_attn_norm2_scale)[:, None], flat(L0_ffn_b1).reshape(HB, P).T,
               flat(L0_ffn_b2)[:, None]]
    b1, b2 = flat(L0_attn_b1), flat(L0_attn_b2)
    for e in range(EXPERTS):
        columns += [b1[e].reshape(HB, P).T, b2[e][:, None]]
    konst, empty = constants()
    arrays = {
        "x": flat(L0_attn_x).reshape(TOKENS, C),
        "c": flat(L0_c),
        "wmod": flat(L0_wmod),
        "wkvg": np.concatenate([wk, wk[:, swap], wv, wg], 1),
        "wq": np.concatenate([wq_, wq_[:, swap]], 1),
        "wo": flat(L0_attn_Wo),
        "wr": flat(L0_attn_router_W),
        "w1": flat(L0_attn_W1),
        "w2": flat(L0_attn_W2),
        "f1": flat(L0_ffn_w1),
        "f2": flat(L0_ffn_w2),
        "vec": np.ascontiguousarray(np.concatenate(columns, 1)),
        "bias": np.concatenate([bk, bk[swap], bv, bg, bq, bq[swap], flat(L0_attn_bo), flat(L0_attn_router_b)])[None, :],
        "konst": konst,
        "empty": empty,
    }
    nc = _bacc.Bacc("TRN2", target_bir_lowering=False, num_devices=1)
    args = [nc.dram_tensor(f"in_{n}", a.shape, F32, kind="ExternalInput").ap() for n, a in arrays.items()]
    out = nc.dram_tensor("out", (TOKENS, C), F32, kind="ExternalOutput").ap()
    adaln_moe(nc, *args, out)
    r = _run(nc, [{f"in_{n}": a for n, a in arrays.items()}], core_ids=[0])
    return r.results[0]["out"].reshape(BATCH, SEQ, C)
```

```python
from contextlib import ExitStack

import numpy as np

import concourse.bass as bass
from concourse import mybir

F32 = mybir.dt.float32
BF16 = mybir.dt.bfloat16
U32 = mybir.dt.uint32
ALU = mybir.AluOpType
ACT = mybir.ActivationFunctionType
AX = mybir.AxisListType

P = 128
BATCH, SEQ, C = 16, 256, 128
TOKENS = BATCH * SEQ
TILES = TOKENS // P
TPB = SEQ // P
HEADS = 16
DK = C // HEADS
CHUNK = 64
CHUNKS = SEQ // CHUNK
SW = C + HEADS
EXPERTS, TOPK = 8, 2
CAPACITY = int(1.25 * TOKENS / EXPERTS)
HID = 512
HB = HID // P
ST = CAPACITY // P
SLOTS = EXPERTS * CAPACITY
ID, G1, G2, E1, E2, PAY = C, C + 1, C + 2, C + 3, C + 4, C + 5
PAIR = 2 * TPB
IN_LOOP = -1
STEPS = BATCH + 5
ROUTE = 17
FAR = 1.0e5
NSUP = BATCH // 2
SUPT = 2 * TPB
SPLIT = 384
PARTS = ((0, SPLIT), (SPLIT, CAPACITY))

K_IDENT, K_TRI, K_KTAB, K_QTAB = 0, 128, 256, 768
K_MASK = 1280
K_IOTA = K_MASK + SW
K_BASE = K_IOTA + EXPERTS
K_TOK = K_BASE + EXPERTS
K_SEL = K_TOK + PAIR
K_ALL = K_SEL + 3
V_S1, V_S2, V_FB1, V_FB2, V_B1 = 0, 1, 2, 6, 7
EV = HB + 1
V_ALL = V_B1 + EXPERTS * EV
B_KVG = 0
B_Q = 3 * C
B_O = B_Q + 2 * C
B_R = B_O + C
B_ALL = B_R + EXPERTS
QUARTER = [slice(TILES // 4 * i, TILES // 4 * (i + 1)) for i in range(4)]
SA, CA, GA, SB, CB, GB = (slice(C * i, C * i + C) for i in range(6))


def constants():
    k = np.zeros((P, K_ALL), np.float32)
    k[:, K_IDENT:K_IDENT + P] = np.eye(P)
    k[:, K_TRI:K_TRI + P] = np.triu(np.ones((P, P)), 1)
    half = DK // 2
    inv = np.float32(1.0) / np.float32(10000.0) ** (np.arange(half, dtype=np.float32) / np.float32(half))
    ang = np.arange(SEQ, dtype=np.float32)[:, None] * inv[None, :]
    cos = np.tile(np.concatenate([np.cos(ang), np.cos(ang)], 1), (1, HEADS))
    sin = np.tile(np.concatenate([-np.sin(ang), np.sin(ang)], 1), (1, HEADS))
    k[:, K_KTAB:K_KTAB + 512] = np.stack([cos, -sin]).reshape(2, TPB, P, C).transpose(2, 0, 1, 3).reshape(P, -1)
    k[:, K_QTAB:K_QTAB + 512] = np.concatenate([cos.T, sin.T], 1)
    head = np.arange(C) // DK
    k[:, K_MASK:K_MASK + C] = head[:, None] == head[None, :]
    k[:, K_MASK + C:K_MASK + SW] = head[:, None] == np.arange(HEADS)[None, :]
    k[:, K_IOTA:K_IOTA + EXPERTS] = np.arange(EXPERTS)
    k[:, K_BASE:K_BASE + EXPERTS] = np.arange(EXPERTS) * CAPACITY
    k[:, K_TOK:K_TOK + PAIR] = np.arange(P)[:, None] + P * np.arange(PAIR)[None, :]
    k[:3, K_SEL:K_SEL + 3] = np.eye(3)
    empty = np.zeros((P, ST, PAY), np.float32)
    empty[:, :, ID] = TOKENS + np.arange(P)[:, None] + P * np.arange(ST)[None, :]
    return k, empty


def adaln_moe(nc, x_d, c_d, wmod_d, wkvg_d, wq_d, wo_d, wr_d, w1_d, w2_d, f1_d, f2_d,
              vec_d, bias_d, const_d, empty_d, out_d):
    mod_d = nc.dram_tensor("mod_rows", [BATCH, 6 * C], F32).ap()
    slot_d = nc.dram_tensor("slots", [SLOTS, PAY], F32).ap()
    acc_d = nc.dram_tensor("acc", [TOKENS + CAPACITY, C], F32).ap()

    with ExitStack() as ctx:
        def sb(name, shape, dt=F32):
            return ctx.enter_context(nc.sbuf_tensor(name, shape, dt))

        def sem(name):
            return ctx.enter_context(nc.semaphore(name))

        def sems(name, n=2):
            return [sem(f"{name}{i}") for i in range(n)]

        ps = ctx.enter_context(nc.psum_tensor("ps", [P, 8, 512], F32))
        konst = sb("konst", [P, K_ALL])
        empty = sb("empty", [P, ST, PAY])
        vec = sb("vec", [P, V_ALL])
        x = sb("x", [P, TILES, C])
        wkvg = sb("wkvg", [P, 3 * C])
        wq = sb("wq", [P, 2 * C])
        wo = sb("wo", [P, C])
        wr = sb("wr", [P, EXPERTS])
        f1 = sb("f1", [P, HID])
        f2 = sb("f2", [P, HB, C])
        w1 = sb("w1", [P, 2, HID])
        w2 = sb("w2", [P, 2, HB, C])
        ident = konst[:, K_IDENT:K_IDENT + P]

        cond = sb("cond", [BATCH, C])
        cond_t = sb("cond_t", [BATCH, C])
        silu = sb("silu", [BATCH, C])
        siluT = sb("siluT", [P, BATCH])
        wmod = sb("wmod", [P, 6 * C])
        mod = sb("mod", [BATCH, 6 * C])
        mod_s = sb("mod_s", [BATCH, 2, C])
        mod_m = sb("mod_m", [BATCH, 2, C])
        modT = sb("modT", [P, BATCH, 4])
        bias = sb("bias", [3, B_ALL])
        bpart = sb("bpart", [3, 2, B_ALL], BF16)
        bsum = sb("bsum", [3, B_ALL])
        bias3 = sb("bias3", [3, B_ALL], BF16)
        ones3 = sb("ones3", [3, SEQ], BF16)
        ones = sb("ones", [P, P], BF16)
        tri = sb("tri", [P, P], BF16)
        power = sb("power", [P, TILES])

        stat = sb("stat", [P, TILES, 6])
        mean = sb("mean", [P, TILES])
        var = sb("var", [P, TILES])
        dmean = sb("dmean", [P, TILES])
        rstd = sb("rstd", [P, TILES])
        nmr = sb("nmr", [P, TILES])

        rows = sb("rows", [P, 2, 2 * C])
        xhat = sb("xhat", [P, 2, TPB, C])
        h = sb("h", [P, 4, TPB, C])
        junk = sb("junk", [P, TPB, C])
        ms1 = sb("ms1", [P, 2, TPB])
        r1 = sb("r1", [P, 2, TPB])
        hn = sb("hn", [P, TPB, C])
        hnT = sb("hnT", [P, 2, SEQ])
        kab = sb("kab", [P, 2, TPB, C])
        qab = sb("qab", [P, 2 * SEQ])
        ka = sb("ka", [P, TPB, C])
        qa = sb("qa", [P, SEQ])
        kexp = sb("kexp", [P, TPB, C])
        krel = sb("krel", [P, TPB, C])
        qexp = sb("qexp", [P, SEQ])
        qrel = sb("qrel", [P, SEQ])
        kphi = sb("kphi", [P, 2, TPB, C])
        qphi = sb("qphi", [P, 2, SEQ])
        vone = sb("vone", [P, 2, TPB, SW])
        gate = sb("gate", [P, 2, TPB, C])
        state = sb("state", [P, CHUNKS, SW])
        gnum = sb("gnum", [P, TPB, C])
        den = sb("den", [P, TPB, HEADS])
        rden = sb("rden", [P, TPB, HEADS])
        o = sb("o", [P, TPB, C])
        oT = sb("oT", [P, 2, SEQ])
        x1 = sb("x1", [P, 2, TPB, C])
        junk2 = sb("junk2", [P, TPB, C])
        ms2 = sb("ms2", [P, 2, TPB])
        r2 = sb("r2", [P, 2, TPB])
        pay = [sb(f"pay{i}", [P, PAIR, PAY]) for i in range(2)]
        xfT = sb("xfT", [P, SEQ])

        logit = sb("logit", [P, PAIR, EXPERTS])
        top = sb("top", [P, PAIR, EXPERTS])
        topi = sb("topi", [P, PAIR, EXPERTS], U32)
        hot = sb("hot", [P, PAIR, TOPK, EXPERTS])
        chosen = sb("chosen", [P, PAIR, EXPERTS], BF16)
        gain = sb("gain", [P, EXPERTS])
        count = sb("count", [P, EXPERTS])
        before = sb("before", [P, EXPERTS], BF16)
        slot = sb("slot", [P, PAIR, EXPERTS])
        over = sb("over", [P, PAIR, EXPERTS])
        slot_of = sb("slot_of", [P, PAIR, TOPK, EXPERTS])
        row_u = [sb(f"row_u{i}", [P, PAIR, TOPK], U32) for i in range(2)]
        row_f = sb("row_f", [P, PAIR, TOPK])
        ldiff = sb("ldiff", [P, PAIR])
        lexp = sb("lexp", [P, PAIR])
        lsum = sb("lsum", [P, PAIR])
        lrec = sb("lrec", [P, PAIR])
        tok = sb("tok", [P, PAIR])
        pair_tokens = sb("pair_tokens", [P, PAIR])

        xs = [sb(f"xs{i}", [P, ST, PAY]) for i in range(2)]
        xeT = sb("xeT", [P, 2, CAPACITY])
        bcol = sb("bcol", [P, 2, EV])
        hid = sb("hid", [P, 2, CAPACITY])
        yeT = sb("yeT", [P, CAPACITY])
        ys = [sb(f"ys{i}", [P, ST, C]) for i in range(2)]
        expert = sb("expert", [P, 2])
        two = sb("two", [P, 1])
        gate1 = sb("gate1", [P, ST])
        gate2 = sb("gate2", [P, ST])
        slot_gate = sb("slot_gate", [P, 2, ST])
        slot_tok = [sb(f"slot_tok{i}", [P, ST], U32) for i in range(2)]
        ac = sb("ac", [P, 2, SUPT, C])
        ga_rows = sb("ga_rows", [P, 2, 2, C])
        x2 = sb("x2", [P, 2, SUPT, C])
        stat2 = sb("stat2", [P, SUPT, 6])
        mv2 = sb("mv2", [P, SUPT, 2])
        var2 = sb("var2", [P, SUPT])
        rstd2 = sb("rstd2", [P, SUPT])
        spare = sb("spare", [P, 2])
        xh2 = sb("xh2", [P, SUPT, C])
        modc = sb("modc", [P, 2, 2, 4])
        hT = sb("hT", [P, 2, SUPT * P])
        hid2 = sb("hid2", [P, 2, SUPT * P])
        y2T = sb("y2T", [P, SUPT * P])
        res = sb("res", [P, 2, SUPT, C])

        ld_const, ld_c, ld_wmod, ld_bias, ld_vec, ld_empty = (sem(f"ld_{n}") for n in ("const", "c", "wmod", "bias", "vec", "empty"))
        ld_ident, ld_sel, bias_first, rows_mm, rows_ok = (sem(n) for n in ("ld_ident", "ld_sel", "bias_first", "rows_mm", "rows_ok"))
        ld_x = sems("ld_x", 4)
        ld_kvg, ld_q, ld_o, ld_r, ld_ffn = (sem(f"ld_{n}") for n in ("kvg", "q", "o", "r", "ffn"))
        st_mod, st_empty, st_dummy = sem("st_mod"), sem("st_empty"), sem("st_dummy")
        setup_pool, tanh_c, silu_ok, siluT_mm, siluT_ok, mod_mm, mod_ok = (
            sem(n) for n in ("setup_pool", "tanh_c", "silu_ok", "siluT_mm", "siluT_ok", "mod_mm", "mod_ok"))
        modT_mm, modT_ok, bias_ok, stat_ok, rstd_ok, nmr_ok, setup_dve = (
            sem(n) for n in ("modT_mm", "modT_ok", "bias_ok", "stat_ok", "rstd_ok", "nmr_ok", "setup_dve"))
        mod_step, ln_step, bias_step, stat_n, tok_ok = (sem(n) for n in ("mod_step", "ln_step", "bias_step", "stat_n", "tok_ok"))
        ld_rows = sems("ld_rows")
        (xhat_ok, h_ok, h_step, ms1_ok, r1_ok, hn_ok, hn_tr, hnT_ok) = (
            sem(n) for n in ("xhat_ok", "h_ok", "h_step", "ms1_ok", "r1_ok", "hn_ok", "hn_tr", "hnT_ok"))
        (kk_mm, vg_mm, q_mm, kab_ok, qab_ok, ka_ok, qa_ok, kexp_ok, krel_ok, qexp_ok, qrel_ok, kphi_ok, qphi_ok, v_ok, g_ok) = (
            sem(n) for n in ("kk_mm", "vg_mm", "q_mm", "kab_ok", "qab_ok", "ka_ok", "qa_ok", "kexp_ok", "krel_ok", "qexp_ok", "qrel_ok",
                             "kphi_ok", "qphi_ok", "v_ok", "g_ok"))
        (kvA_mm, kvB_mm, stateA_ok, stateB_ok, num_mm, gnum_ok, den_ok, rden_ok, o_ok, o_tr, oT_ok) = (
            sem(n) for n in ("kvA_mm", "kvB_mm", "stateA_ok", "stateB_ok", "num_mm", "gnum_ok", "den_ok", "rden_ok", "o_ok", "o_tr", "oT_ok"))
        (ao_mm, x1_ok, ms2_ok, r2_ok, xf_ok, xf_tr, xfT_ok, logit_mm) = (
            sem(n) for n in ("ao_mm", "x1_ok", "ms2_ok", "r2_ok", "xf_ok", "xf_tr", "xfT_ok", "logit_mm"))
        st_x1 = sems("st_x1")
        (logit_ok, routing, chosen_ok, before_ok, pos_mm, ldiff_ok, lexp_ok, row_ok, gates_ok) = (
            sem(n) for n in ("logit_ok", "routing", "chosen_ok", "before_ok", "pos_mm", "ldiff_ok", "lexp_ok", "row_ok", "gates_ok"))
        ld_w, ld_slots = sems("ld_w"), sems("ld_slots")
        (x_tr, xeT_ok, up_mm, gelu_ok, down_mm, yeT_ok, y_tr, ys_ok, gate_step, slot_gate_ok, slot_tok_ok, expert_ok, added) = (
            sem(n) for n in ("x_tr", "xeT_ok", "up_mm", "gelu_ok", "down_mm", "yeT_ok", "y_tr", "ys_ok", "gate_step",
                             "slot_gate_ok", "slot_tok_ok", "expert_ok", "added"))
        ld_ac, st_out = sems("ld_ac"), sems("st_out")
        (ga_step, x2_ok, stat2_ok, mv2_ok, var2_ok, rstd2_ok, xh2_ok, modc_ok, x2_tr, hT_ok, up2_mm, gelu2_ok, down2_mm,
         y2T_ok, y2_tr, res_ok, spare_ok) = (
            sem(n) for n in ("ga_step", "x2_ok", "stat2_ok", "mv2_ok", "var2_ok", "rstd2_ok", "xh2_ok", "modc_ok", "x2_tr",
                             "hT_ok", "up2_mm", "gelu2_ok", "down2_mm", "y2T_ok", "y2_tr", "res_ok", "spare_ok"))
        bcol_ok, x2_kept, tri_ok = sem("bcol_ok"), sem("x2_kept"), sem("tri_ok")
        rowf_ok, slot_ok = sem("rowf_ok"), sem("slot_ok")
        scattered = sems("scattered", 4)

        block = ctx.enter_context(nc.Block())

        kk_ps = ps[:, 0, 0:TPB * C].rearrange("p (t n) -> p t n", t=TPB)
        vg_ps = ps[:, 1, :].rearrange("p (t n) -> p t n", t=TPB)
        q_ps = ps[:, 2, :]
        hnT_ps = ps[:, 3, 0:SEQ]
        tr_ps = ps[:, 3, SEQ:2 * SEQ]
        kv_ps = ps[:, 4:6, :]
        num_ps = ps[:, 6, 0:TPB * SW].rearrange("p (t n) -> p t n", t=TPB)
        ao_ps = ps[:, 7, 0:TPB * C].rearrange("p (t n) -> p t n", t=TPB)
        logit_ps = ps[:, 7, 256:288].rearrange("p (t e) -> p t e", e=EXPERTS)
        pos_ps = ps[:, 7, 288:320].rearrange("p (t e) -> p t e", e=EXPERTS)

        def wait(eng, s, n):
            if not isinstance(n, int) or n > 0:
                eng.wait_ge(s, n)

        def attention_phase(eng, step):
            for s in range(7):
                step(s, s // 2, s % 4, s)
            with eng.Fori(1, 3, 1) as turn:
                for i in range(1, 5):
                    step(turn * 4 + 2 + i, turn * 2 + 1 + i // 2, (i + 2) % 4, IN_LOOP)
            for s in range(BATCH - 1, STEPS):
                step(s, s // 2, s % 4, s)

        def by_twos(eng, step):
            for e in range(2):
                step(e, e, e)
            with eng.Fori(1, 3, 1) as turn:
                for q in range(2):
                    step(turn * 2 + q, q, IN_LOOP)
            for e in range(6, 8):
                step(e, e - 6, e)

        def live(key, lag):
            return key == IN_LOOP or 0 <= key - lag < BATCH

        @block.sync
        def _(sp):
            def load_x(i):
                n = TILES // 4
                sp.dma_start(x[:, n * i:n * i + n, :],
                             x_d[n * i * P:n * (i + 1) * P, :].rearrange("(t p) c -> p t c", p=P)).then_inc(ld_x[i], 16)

            def load_rows(b, j):
                wait(sp, h_ok, b - 1)
                sp.dma_start(rows[:, j % 2, :], mod_d[bass.ds(b, 1), 0:2 * C].to_broadcast([P, 2 * C])).then_inc(ld_rows[j % 2], 16)

            sp.dma_start(cond[:, :], c_d).then_inc(ld_c, 16)
            sp.dma_start(konst[:, 0:K_TRI], const_d[:, 0:K_TRI]).then_inc(ld_ident, 16)
            load_x(0)
            sp.dma_start(wmod[:, :], wmod_d).then_inc(ld_wmod, 16)
            sp.dma_start(konst[0:3, K_SEL:K_ALL], const_d[0:3, K_SEL:K_ALL]).then_inc(ld_sel, 16)
            sp.dma_start(bias[:, :], bias_d[0:1, :].to_broadcast([3, B_ALL])).then_inc(ld_bias, 16)
            sp.dma_start(vec[:, :], vec_d).then_inc(ld_vec, 16)
            sp.dma_start(konst[:, K_TRI:K_SEL], const_d[:, K_TRI:K_SEL]).then_inc(ld_const, 16)
            sp.dma_start(wkvg[:, :], wkvg_d).then_inc(ld_kvg, 16)
            sp.dma_start(wq[:, :], wq_d).then_inc(ld_q, 16)
            load_x(1)
            sp.dma_start(wo[:, :], wo_d).then_inc(ld_o, 16)
            sp.dma_start(wr[:, :], wr_d).then_inc(ld_r, 16)
            load_x(2)
            load_x(3)
            sp.dma_start(empty[:, :, :], empty_d).then_inc(ld_empty, 16)
            sp.wait_ge(mod_ok, 1)
            sp.dma_start(mod_d, mod[:, :]).then_inc(st_mod, 16)
            sp.wait_ge(st_mod, 16)

            def load_w(e, q):
                wait(sp, down_mm, 4 * (e - 1))
                sp.dma_start(w1[:, q, :], w1_d[bass.ds(e, 1), :, :].rearrange("a k n -> k (a n)")).then_inc(ld_w[q], 16)
                sp.dma_start(w2[:, q, :, :], w2_d[bass.ds(e, 1), :, :].rearrange("a (b p) c -> p (a b) c", p=P)).then_inc(ld_w[q], 16)

            def empty_slots():
                sp.wait_ge(ld_empty, 16)
                for e in range(EXPERTS):
                    sp.dma_start(slot_d[e * CAPACITY:(e + 1) * CAPACITY, :].rearrange("(t p) c -> p t c", p=P),
                                 empty[:, :, :]).then_inc(st_empty, 16)
                sp.dma_start(acc_d[TOKENS:TOKENS + CAPACITY, :].rearrange("(t p) c -> p t c", p=P),
                             empty[:, :, 0:C]).then_inc(st_dummy, 16)

            def step(s, half, j, key):
                if live(key, 0) and key not in (0, 1):
                    load_rows(s, j)
                if key == 3:
                    empty_slots()
                    for e in range(2):
                        load_w(e, e)
                    sp.dma_start(f1[:, :], f1_d).then_inc(ld_ffn, 16)
                    sp.dma_start(f2[:, :, :], f2_d.rearrange("(b p) c -> p b c", p=P)).then_inc(ld_ffn, 16)
                if live(key, 3):
                    sp.wait_ge(x1_ok, s - 2)
                    sp.dma_start(acc_d[bass.ds((s - 3) * SEQ, SEQ), :].rearrange("(t p) c -> p t c", p=P),
                                 x1[:, (j + 1) % 2, :, :]).then_inc(st_x1[(j + 1) % 2], 16)

            attention_phase(sp, step)
            for i in range(2):
                sp.wait_ge(st_x1[i], 16 * (BATCH // 2))
            for i in range(4):
                sp.wait_ge(scattered[i], 64 * (BATCH // 4))
            sp.wait_ge(st_dummy, 16)

            def expert_step(e, q, key):
                if key not in (0, 1):
                    load_w(e, q)
                wait(sp, x_tr, 2 * (e - 1))
                wait(sp, slot_tok_ok, e - 1)
                wait(sp, slot_gate_ok, e - 1)
                sp.dma_start(xs[q][:, :, :], slot_d[bass.ds(e * CAPACITY, CAPACITY), :].rearrange("(t p) c -> p t c", p=P))\
                  .then_inc(ld_slots[q], 16)

            by_twos(sp, expert_step)
            sp.wait_ge(added, 16 * ST * EXPERTS)

            def group_step(g, q, key):
                wait(sp, ga_step, g - 1)
                sp.dma_start(ac[:, q, :, :], acc_d[bass.ds(g * (SUPT * P), SUPT * P), :].rearrange("(t p) c -> p t c", p=P))\
                  .then_inc(ld_ac[q], 16)
                sp.dma_start(ga_rows[:, q, :, :], mod_d[bass.ds(2 * g, 2), GA].unsqueeze(0).to_broadcast([P, 2, C]))\
                  .then_inc(ld_ac[q], 16)

            by_twos(sp, group_step)
            for i in range(2):
                sp.wait_ge(st_out[i], 16 * NSUP // 2)

        @block.gpsimd
        def _(pool):
            pool.memset(power[:, :], -0.5).then_inc(setup_pool, 1)
            pool.memset(ones3[:, :], 1.0).then_inc(setup_pool, 1)
            pool.memset(ones[:, :], 1.0).then_inc(setup_pool, 1)
            pool.memset(vone[:, :, :, C:SW], 1.0).then_inc(setup_pool, 1)
            pool.memset(count[:, :], 0.0).then_inc(setup_pool, 1)
            pool.memset(pair_tokens[:, :], float(PAIR * P)).then_inc(setup_pool, 1)
            pool.memset(expert[:, 0:1], 0.0).then_inc(setup_pool, 1)
            pool.memset(expert[:, 1:2], 1.0).then_inc(setup_pool, 1)
            pool.memset(two[:, :], 2.0).then_inc(setup_pool, 1)
            pool.wait_ge(setup_pool, 9)

            def norm_scale(i):
                pool.wait_ge(stat_ok, i + 1)
                pool.tensor_tensor(rstd[:, QUARTER[i]], var[:, QUARTER[i]], power[:, QUARTER[i]], ALU.pow).then_inc(rstd_ok, 1)

            norm_scale(0)

            def scatter(j, i):
                q, t, k = (j + 3) % 4 // 2, TPB * ((j + 3) % 2) + i // 2, i % 2
                pool.indirect_dma_start(
                    slot_d[:, :], bass.IndirectOffsetOnAxis(row_u[q][:, t, k:k + 1], 0),
                    pay[q][:, t, :], None,
                    bounds_check=SLOTS - 1, oob_is_err=False).then_inc(scattered[(j + 3) % 4], 16)

            def by_halves(k):
                return k.rearrange("p t (h u d) -> p (t h) u d", u=2, d=DK // 2)

            def step(s, half, j, key):
                if key == 5:
                    pool.wait_ge(st_empty, 16 * EXPERTS)
                if live(key, 0):
                    pool.wait_ge(ms1_ok, s + 1)
                    pool.tensor_tensor(r1[:, j % 2, :], ms1[:, j % 2, :], power[:, 0:TPB], ALU.pow).then_inc(r1_ok, 1)
                if live(key, 5) and j % 2 == 1:
                    pool.wait_ge(row_ok, half - 1)
                    pool.wait_ge(gates_ok, 3 * (half - 1))
                    pool.wait_ge(xf_ok, s - 3)
                    pool.tensor_tensor(tok[:, :], tok[:, :], pair_tokens[:, :], ALU.add).then_inc(tok_ok, 1)
                if live(key, 5):
                    scatter(j, 0)
                if live(key, 1):
                    pool.wait_ge(qab_ok, s)
                    wait(pool, qrel_ok, s - 1)
                    pool.tensor_tensor(qa[:, :], qab[:, 0:SEQ], qab[:, SEQ:2 * SEQ], ALU.add).then_inc(qa_ok, 1)
                if live(key, 5):
                    scatter(j, 1)
                    scatter(j, 2)
                if live(key, 2):
                    pool.wait_ge(ms2_ok, s - 1)
                    pool.tensor_tensor(r2[:, j % 2, :], ms2[:, j % 2, :], power[:, 0:TPB], ALU.pow).then_inc(r2_ok, 1)
                if live(key, 0):
                    pool.wait_ge(kab_ok, s + 1)
                    wait(pool, krel_ok, s)
                    pool.tensor_tensor(by_halves(ka[:, :, :]), by_halves(kab[:, 0, :, :]),
                                       by_halves(kab[:, 1, :, :])[:, :, ::-1, :], ALU.add).then_inc(ka_ok, 1)
                if key in (0, 1, 2):
                    norm_scale(key + 1)
                if live(key, 5):
                    scatter(j, 3)

            attention_phase(pool, step)

            def expert_step(e, q, key):
                pool.wait_ge(slot_tok_ok, e + 1)
                pool.wait_ge(slot_gate_ok, e + 1)
                wait(pool, added, 16 * ST * e)
                pool.wait_ge(ys_ok, 2 * e + 2)
                pool.tensor_tensor(expert[:, q:q + 1], expert[:, q:q + 1], two[:, :], ALU.add).then_inc(expert_ok, 1)
                for t in range(ST):
                    pool.indirect_dma_start(acc_d[:, :], bass.IndirectOffsetOnAxis(slot_tok[q][:, t:t + 1], 0),
                                            ys[q][:, t, :], None, compute_op=ALU.add).then_inc(added, 16)

            by_twos(pool, expert_step)

            def group_step(g, q, key):
                pool.wait_ge(var2_ok, g + 1)
                wait(pool, xh2_ok, g)
                pool.tensor_tensor(rstd2[:, :], var2[:, :], power[:, 0:SUPT], ALU.pow).then_inc(rstd2_ok, 1)

            by_twos(pool, group_step)

        @block.scalar
        def _(act):
            act.wait_ge(ld_c, 16)
            act.activation(cond_t[:, :], cond[:, :], ACT.Tanh, scale=0.5).then_inc(tanh_c, 1)
            act.wait_ge(ld_bias, 16)
            act.wait_ge(ld_sel, 16)
            act.activation(bpart[:, 0, :], bias[:, :], ACT.Copy).then_inc(bias_first, 1)
            act.wait_ge(bias_first, 1)
            act.activation(bsum[:, :], bpart[:, 0, :], ACT.Copy, scale=konst[0:3, K_SEL:K_SEL + 1]).then_inc(bias_first, 1)
            act.wait_ge(nmr_ok, 1)
            act.wait_ge(ld_vec, 16)

            def step(s, half, j, key):
                q = j % 2
                if live(key, 2):
                    act.wait_ge(qa_ok, s - 1)
                    wait(act, qphi_ok, s - 2)
                    act.activation(qrel[:, :], qa[:, :], ACT.Relu).then_inc(qrel_ok, 1)
                if live(key, 3):
                    act.wait_ge(x1_ok, s - 2)
                    wait(act, r2_ok, s - 4)
                    wait(act, ms2_ok, s - 3)
                    for t in range(TPB):
                        ins = act.activation(junk2[:, t, :], x1[:, 1 - q, t, :], ACT.Square, scale=float(C) ** -0.5,
                                             accum_out=ms2[:, 1 - q, t:t + 1])
                    ins.then_inc(ms2_ok, 1)
                if key in (4, 8, 12):
                    act.wait_ge(nmr_ok, key // 4 + 1)
                if live(key, 0):
                    for t in range(TPB):
                        tile = bass.ds(s * TPB + t, 1)
                        ins = act.activation(xhat[:, q, t, :], x[:, tile, :].rearrange("p a c -> p (a c)"), ACT.Identity,
                                             bias=nmr[:, tile], scale=rstd[:, tile])
                    ins.then_inc(xhat_ok, 1)
                if live(key, 3):
                    pay_q = ((j + 1) % 4) // 2
                    act.wait_ge(r2_ok, s - 2)
                    if key not in (3, 4, 5, 6):
                        act.wait_ge(scattered[(j + 1) % 4], (s - 3 - (j + 1) % 4) * 16)
                    for t in range(TPB):
                        ins = act.activation(pay[pay_q][:, TPB * (1 - q) + t, 0:C], x1[:, 1 - q, t, :], ACT.Copy,
                                             scale=r2[:, 1 - q, t:t + 1])
                    ins.then_inc(xf_ok, 1)
                if live(key, 1):
                    act.wait_ge(ka_ok, s)
                    wait(act, kphi_ok, s - 1)
                    act.activation(kexp[:, :, :], ka[:, :, :], ACT.Exp).then_inc(kexp_ok, 1)
                if live(key, 0):
                    act.wait_ge(h_ok, s + 1)
                    wait(act, r1_ok, s - 1)
                    wait(act, ms1_ok, s)
                    for t in range(TPB):
                        ins = act.activation(junk[:, t, :], h[:, j, t, :], ACT.Square, scale=float(C) ** -0.5,
                                             accum_out=ms1[:, q, t:t + 1])
                    ins.then_inc(ms1_ok, 1)
                if live(key, 1):
                    act.activation(krel[:, :, :], ka[:, :, :], ACT.Relu).then_inc(krel_ok, 1)
                if live(key, 3):
                    act.wait_ge(xf_tr, s - 2)
                    wait(act, logit_mm, s - 3)
                    act.activation(xfT[:, :], tr_ps, ACT.Copy, scale=vec[:, V_S2:V_S2 + 1]).then_inc(xfT_ok, 1)
                if live(key, 1):
                    act.wait_ge(vg_mm, s)
                    wait(act, kvA_mm, s - 2)
                    act.activation(vone[:, 1 - q, :, 0:C], vg_ps[:, :, 0:C], ACT.Copy).then_inc(v_ok, 1)
                if live(key, 0):
                    act.wait_ge(r1_ok, s + 1)
                    wait(act, hn_tr, s)
                    for t in range(TPB):
                        ins = act.activation(hn[:, t, :], h[:, j, t, :], ACT.Copy, scale=r1[:, q, t:t + 1])
                    ins.then_inc(hn_ok, 1)
                if live(key, 2):
                    act.wait_ge(o_tr, s - 1)
                    wait(act, ao_mm, s - 3)
                    act.activation(oT[:, q, :], tr_ps, ACT.Copy).then_inc(oT_ok, 1)
                if live(key, 1):
                    wait(act, gnum_ok, s - 2)
                    act.activation(gate[:, 1 - q, :, :], vg_ps[:, :, C:2 * C], ACT.Tanh, scale=0.5).then_inc(g_ok, 1)
                if live(key, 0):
                    act.wait_ge(hn_tr, s + 1)
                    wait(act, q_mm, s - 1)
                    act.activation(hnT[:, q, :], hnT_ps, ACT.Copy, scale=vec[:, V_S1:V_S1 + 1]).then_inc(hnT_ok, 1)
                if q == 0 and live(key, 4):
                    act.wait_ge(ldiff_ok, half - 1)
                    act.activation(lexp[:, :], ldiff[:, :], ACT.Exp).then_inc(lexp_ok, 1)
                if live(key, 1):
                    act.wait_ge(qa_ok, s)
                    wait(act, qphi_ok, s - 1)
                    act.activation(qexp[:, :], qa[:, :], ACT.Exp).then_inc(qexp_ok, 1)

            attention_phase(act, step)

            def expert_step(e, q, key):
                act.wait_ge(bcol_ok, e + 1)
                for k in range(HB):
                    wait(act, down_mm, 4 * e + k - 1)
                    for i, (a, b) in enumerate(PARTS):
                        act.wait_ge(up_mm, 8 * e + 2 * k + i + 1)
                        act.activation(hid[:, k % 2, a:b], ps[:, 2 + 2 * (k % 2) + i, 0:b - a], ACT.Gelu,
                                       bias=bcol[:, q, k:k + 1]).then_inc(gelu_ok, 1)
                act.wait_ge(down_mm, 4 * e + 4)
                wait(act, y_tr, 2 * e)
                for i, (a, b) in enumerate(PARTS):
                    act.activation(yeT[:, a:b], ps[:, 6 + i, 0:b - a], ACT.Identity,
                                   bias=bcol[:, q, HB:EV]).then_inc(yeT_ok, 1)

            by_twos(act, expert_step)

            def modulated(g, q):
                act.wait_ge(x2_tr, g + 1)
                act.wait_ge(modc_ok, g + 1)
                wait(act, up2_mm, 4 * (g - 1))
                for i in range(2):
                    act.activation(hT[:, q, SEQ * i:SEQ * i + SEQ], ps[:, 0, SEQ * i:SEQ * i + SEQ], ACT.Identity,
                                   scale=modc[:, q, i, 1:2], bias=modc[:, q, i, 0:1]).then_inc(hT_ok, 1)

            def store(g, q):
                act.wait_ge(res_ok, g + 1)
                act.dma_start(out_d[bass.ds(g * (SUPT * P), SUPT * P), :].rearrange("(t p) c -> p t c", p=P),
                              res[:, q, :, :]).then_inc(st_out[q], 16)

            def group_step(g, q, key):
                for k in range(HB):
                    if k == 1 and key not in (0, 1):
                        store(g - 2, q)
                    act.wait_ge(up2_mm, 4 * g + k + 1)
                    wait(act, down2_mm, 4 * g + k - 1)
                    act.activation(hid2[:, k % 2, :], ps[:, 2 + k % 2, :], ACT.Gelu,
                                   bias=vec[:, V_FB1 + k:V_FB1 + k + 1]).then_inc(gelu2_ok, 1)
                    if k == 2 and key != NSUP - 1:
                        modulated(g + 1, 1 - q)
                act.wait_ge(down2_mm, 4 * g + 4)
                wait(act, y2_tr, g)
                for i in range(2):
                    act.activation(y2T[:, SEQ * i:SEQ * i + SEQ], ps[:, 4 + q, SEQ * i:SEQ * i + SEQ], ACT.Identity,
                                   scale=modc[:, q, i, 2:3], bias=modc[:, q, i, 3:4]).then_inc(y2T_ok, 1)

            modulated(0, 0)
            by_twos(act, group_step)
            store(NSUP - 2, 0)
            store(NSUP - 1, 1)

        @block.vector
        def _(dve):
            def norm_stats(i):
                tiles = QUARTER[i]
                dve.wait_ge(ld_x[i], 16)
                for t in range(tiles.start, tiles.stop):
                    dve.bn_stats(stat[:, t, :], x[:, t, :]).then_inc(stat_n, 1)
                dve.wait_ge(stat_n, tiles.stop)
                dve.tensor_tensor(mean[:, tiles], stat[:, tiles, 1], stat[:, tiles, 4], ALU.add).then_inc(ln_step, 1)
                dve.tensor_tensor(dmean[:, tiles], stat[:, tiles, 1], stat[:, tiles, 4], ALU.subtract).then_inc(ln_step, 1)
                dve.tensor_tensor(var[:, tiles], stat[:, tiles, 2], stat[:, tiles, 5], ALU.add).then_inc(ln_step, 1)
                dve.wait_ge(ln_step, 6 * i + 3)
                dve.tensor_scalar(mean[:, tiles], mean[:, tiles], 0.5, None, ALU.mult).then_inc(ln_step, 1)
                dve.tensor_tensor(dmean[:, tiles], dmean[:, tiles], dmean[:, tiles], ALU.mult).then_inc(ln_step, 1)
                dve.tensor_scalar(var[:, tiles], var[:, tiles], 1.0 / C, 1e-5, ALU.mult, ALU.add).then_inc(ln_step, 1)
                dve.wait_ge(ln_step, 6 * i + 6)
                dve.scalar_tensor_tensor(out=var[:, tiles], in0=dmean[:, tiles], scalar=0.25, in1=var[:, tiles], op0=ALU.mult,
                                         op1=ALU.add).then_inc(stat_ok, 1)

            def norm_bias(i):
                dve.wait_ge(rstd_ok, i + 1)
                dve.scalar_tensor_tensor(out=nmr[:, QUARTER[i]], in0=mean[:, QUARTER[i]], scalar=-1.0, in1=rstd[:, QUARTER[i]],
                                         op0=ALU.mult, op1=ALU.mult).then_inc(nmr_ok, 1)

            dve.wait_ge(tanh_c, 1)
            dve.scalar_tensor_tensor(out=silu[:, :], in0=cond_t[:, :], scalar=1.0, in1=cond[:, :],
                                     op0=ALU.add, op1=ALU.mult).then_inc(setup_dve, 1)
            dve.wait_ge(setup_dve, 1)
            dve.tensor_scalar(silu[:, :], silu[:, :], 0.5, None, ALU.mult).then_inc(silu_ok, 1)
            dve.wait_ge(siluT_mm, 1)
            dve.tensor_copy(siluT[:, :], ps[:, 7, 0:BATCH]).then_inc(siluT_ok, 1)
            norm_stats(0)
            dve.wait_ge(rows_mm, 1)
            spread = ps[:, 4, :].rearrange("p (b n) -> p b n", b=2)
            dve.tensor_copy(rows[:, :, 0:C], spread[:, :, 0:C]).then_inc(rows_ok, 1)
            dve.tensor_scalar(rows[:, :, C:2 * C], spread[:, :, C:2 * C], 1.0, None, ALU.add).then_inc(rows_ok, 1)

            sel = konst[0:3, K_SEL:K_SEL + 3]
            dve.wait_ge(bias_first, 2)
            dve.wait_ge(ld_sel, 16)
            dve.tensor_tensor(bias[:, :], bias[:, :], bpart[:, 0, :], ALU.subtract).then_inc(bias_step, 1)
            dve.wait_ge(bias_step, 1)
            dve.tensor_copy(bpart[:, 1, :], bias[:, :]).then_inc(bias_step, 1)
            norm_bias(0)
            dve.wait_ge(bias_step, 2)
            dve.scalar_tensor_tensor(out=bsum[:, :], in0=bpart[:, 1, :], scalar=sel[:, 1:2], in1=bsum[:, :],
                                     op0=ALU.mult, op1=ALU.add).then_inc(bias_step, 1)
            dve.tensor_tensor(bias[:, :], bias[:, :], bpart[:, 1, :], ALU.subtract).then_inc(bias_step, 1)

            def last_bias_part():
                dve.wait_ge(bias_step, 4)
                dve.scalar_tensor_tensor(out=bias3[:, :], in0=bias[:, :], scalar=sel[:, 2:3], in1=bsum[:, :],
                                         op0=ALU.mult, op1=ALU.add).then_inc(bias_ok, 1)

            def modulation():
                dve.wait_ge(mod_mm, 1)
                dve.tensor_copy(mod[:, 0:512], ps[0:BATCH, 5, 0:512]).then_inc(mod_step, 1)
                dve.tensor_copy(mod[:, 512:768], ps[0:BATCH, 6, 0:256]).then_inc(mod_step, 1)
                dve.wait_ge(mod_step, 2)
                dve.tensor_scalar(mod[:, CA], mod[:, CA], 1.0, None, ALU.add).then_inc(mod_step, 1)
                dve.tensor_scalar(mod[:, CB], mod[:, CB], 1.0, None, ALU.add).then_inc(mod_step, 1)
                g = mod[:, :].rearrange("b (k m c) -> b k m c", k=2, m=3)[:, :, 2, :]
                dve.tensor_scalar(mod_s[:, :, :], g, 0.0, 2.0, ALU.is_ge, ALU.mult).then_inc(mod_step, 1)
                dve.scalar_tensor_tensor(out=mod_m[:, :, :], in0=g, scalar=-1.0, in1=g, op0=ALU.mult, op1=ALU.max).then_inc(mod_step, 1)
                dve.wait_ge(mod_step, 6)
                dve.tensor_scalar(mod_s[:, :, :], mod_s[:, :, :], 1.0, None, ALU.subtract).then_inc(mod_step, 1)
                dve.tensor_scalar(mod_m[:, :, :], mod_m[:, :, :], 0.25, None, ALU.max).then_inc(mod_step, 1)
                dve.wait_ge(mod_step, 8)
                dve.tensor_tensor(g, mod_s[:, :, :], mod_m[:, :, :], ALU.mult).then_inc(mod_ok, 1)

            def modulation_columns():
                dve.wait_ge(modT_mm, 1)
                dve.wait_ge(ld_vec, 16)
                dve.tensor_copy(modT[:, :, 0:3], ps[:, 7, 32:32 + 3 * BATCH].rearrange("p (k b) -> p b k", k=3)).then_inc(modT_ok, 1)
                dve.wait_ge(modT_ok, 1)
                dve.tensor_scalar(modT[:, :, 3:4], modT[:, :, 2:3], vec[:, V_FB2:V_FB2 + 1], None, ALU.mult).then_inc(modT_ok, 1)
                dve.tensor_copy(tri[:, :], konst[:, K_TRI:K_TRI + P]).then_inc(tri_ok, 1)
                dve.tensor_scalar(tok[:, :], konst[:, K_TOK:K_TOK + PAIR], 0.0, None, ALU.add).then_inc(tok_ok, 1)

            ktab = konst[:, K_KTAB:K_KTAB + 512].rearrange("p (a t n) -> p a t n", a=2, t=TPB)
            qtab = konst[:, K_QTAB:K_QTAB + 512]
            mask = konst[:, K_MASK:K_MASK + SW].unsqueeze(1).to_broadcast([P, 2, SW])
            iota = konst[:, K_IOTA:K_IOTA + EXPERTS].unsqueeze(1).unsqueeze(1).to_broadcast([P, PAIR, TOPK, EXPERTS])
            base = konst[:, K_BASE:K_BASE + EXPERTS].unsqueeze(1).to_broadcast([P, PAIR, EXPERTS])

            def route_top(p, s):
                dve.wait_ge(logit_mm, s - 2)
                dve.tensor_copy(logit[:, :, :], logit_ps).then_inc(logit_ok, 1)
                dve.wait_ge(logit_ok, p + 1)
                dve.tensor_copy(before[:, :], count[:, :]).then_inc(before_ok, 1)
                for t in range(PAIR):
                    dve.max(top[:, t, :], logit[:, t, :]).then_inc(routing, 1)
                dve.wait_ge(routing, ROUTE * p + 4)
                dve.tensor_tensor(ldiff[:, :], top[:, :, 1], top[:, :, 0], ALU.subtract).then_inc(ldiff_ok, 1)
                for t in range(PAIR):
                    dve.max_index(topi[:, t, :], top[:, t, :], logit[:, t, :]).then_inc(routing, 1)

            def route_chosen(p, s, buf):
                dve.wait_ge(xf_ok, s - 2)
                dve.wait_ge(routing, ROUTE * p + 8)
                dve.tensor_copy(buf[:, :, E1:E2 + 1], topi[:, :, 0:TOPK]).then_inc(routing, 1)
                dve.wait_ge(routing, ROUTE * p + 9)
                dve.tensor_tensor(hot[:, :, :, :], iota,
                                  buf[:, :, E1:E2 + 1].unsqueeze(3).to_broadcast([P, PAIR, TOPK, EXPERTS]),
                                  ALU.is_equal).then_inc(routing, 1)
                dve.wait_ge(routing, ROUTE * p + 10)
                dve.tensor_tensor(chosen[:, :, :], hot[:, :, 0, :], hot[:, :, 1, :], ALU.add).then_inc(chosen_ok, 1)
                dve.wait_ge(chosen_ok, p + 1)
                dve.tensor_reduce(gain[:, :], chosen[:, :, :].rearrange("p t e -> p e t"), AX.X, ALU.add).then_inc(routing, 1)
                dve.wait_ge(routing, ROUTE * p + 11)
                dve.tensor_tensor(count[:, :], count[:, :], gain[:, :], ALU.add).then_inc(routing, 1)

            def route_place(p):
                dve.wait_ge(pos_mm, p + 1)
                dve.tensor_tensor(slot[:, :, :], pos_ps, base, ALU.add).then_inc(slot_ok, 1)
                dve.tensor_scalar(over[:, :, :], pos_ps, float(CAPACITY), FAR, ALU.is_ge, ALU.mult).then_inc(slot_ok, 1)

            def route_slots(p, j, buf):
                dve.wait_ge(slot_ok, 2 * (p + 1))
                dve.tensor_tensor(slot[:, :, :], slot[:, :, :], over[:, :, :], ALU.add).then_inc(routing, 1)
                dve.wait_ge(lexp_ok, p + 1)
                dve.tensor_scalar(lsum[:, :], lexp[:, :], 1.0, None, ALU.add).then_inc(routing, 1)
                dve.wait_ge(routing, ROUTE * p + 13)
                for k in range(TOPK):
                    dve.tensor_tensor(slot_of[:, :, k, :], hot[:, :, k, :], slot[:, :, :], ALU.mult).then_inc(routing, 1)
                dve.wait_ge(routing, ROUTE * p + 14)
                dve.reciprocal(lrec[:, :], lsum[:, :]).then_inc(routing, 1)
                dve.wait_ge(routing, ROUTE * p + 16)
                dve.tensor_reduce(row_f[:, :, :], slot_of[:, :, :, :], AX.X, ALU.add).then_inc(rowf_ok, 1)
                dve.wait_ge(tok_ok, p + 1)
                dve.tensor_copy(buf[:, :, ID], tok[:, :]).then_inc(gates_ok, 1)
                dve.wait_ge(routing, ROUTE * p + 17)
                dve.wait_ge(rowf_ok, p + 1)
                dve.tensor_copy(row_u[j // 2][:, :, :], row_f[:, :, :]).then_inc(row_ok, 1)
                dve.tensor_copy(buf[:, :, G1], lrec[:, :]).then_inc(gates_ok, 1)
                dve.tensor_tensor(buf[:, :, G2], lexp[:, :], lrec[:, :], ALU.mult).then_inc(gates_ok, 1)

            def step(s, half, j, key):
                q = j % 2
                if live(key, 0):
                    if key in (0, 1):
                        dve.wait_ge(rows_ok, 2)
                    else:
                        dve.wait_ge(ld_rows[q], s * 8 - 8 * q)
                    dve.wait_ge(xhat_ok, s + 1)
                    wait(dve, hn_ok, s - 3)
                    wait(dve, x1_ok, s - 3)
                    dve.tensor_tensor(h[:, j, :, :], xhat[:, q, :, :], rows[:, q, C:2 * C].unsqueeze(1).to_broadcast([P, TPB, C]),
                                      ALU.mult).then_inc(h_step, 1)
                if live(key, 2):
                    dve.wait_ge(num_mm, s - 1)
                    wait(dve, rden_ok, s - 2)
                    dve.tensor_scalar(den[:, :, :], num_ps[:, :, C:SW], 2.0, 2e-6, ALU.mult, ALU.add).then_inc(den_ok, 1)
                    dve.wait_ge(g_ok, s - 1)
                    wait(dve, o_ok, s - 2)
                    dve.scalar_tensor_tensor(out=gnum[:, :, :], in0=gate[:, q, :, :], scalar=1.0, in1=num_ps[:, :, 0:C],
                                             op0=ALU.add, op1=ALU.mult).then_inc(gnum_ok, 1)
                if live(key, 0):
                    dve.wait_ge(h_step, s + 1)
                    dve.tensor_tensor(h[:, j, :, :], h[:, j, :, :], rows[:, q, 0:C].unsqueeze(1).to_broadcast([P, TPB, C]),
                                      ALU.add).then_inc(h_ok, 1)
                if key in (1, 2, 3):
                    norm_bias(key)
                if key == 0:
                    last_bias_part()
                    modulation()
                    dve.wait_ge(ld_const, 16)
                if live(key, 2):
                    dve.wait_ge(den_ok, s - 1)
                    dve.reciprocal(rden[:, :, :], den[:, :, :]).then_inc(rden_ok, 1)
                if q == 1 and live(key, 5):
                    route_slots(half - 2, (j + 3) % 4, pay[(j + 3) % 4 // 2])
                if live(key, 2):
                    dve.wait_ge(rden_ok, s - 1)
                    dve.wait_ge(gnum_ok, s - 1)
                    wait(dve, o_tr, s - 2)
                    dve.tensor_tensor(o[:, :, :].rearrange("p t (g d) -> p (t g) d", d=DK),
                                      gnum[:, :, :].rearrange("p t (g d) -> p (t g) d", d=DK),
                                      rden[:, :, :].rearrange("p t g -> p (t g)").unsqueeze(2).to_broadcast([P, TPB * HEADS, DK]),
                                      ALU.mult).then_inc(o_ok, 1)
                if live(key, 1):
                    dve.wait_ge(krel_ok, s)
                    wait(dve, kvA_mm, s - 2)
                    dve.scalar_tensor_tensor(out=kphi[:, 1 - q, :, :], in0=kexp[:, :, :], scalar=1.0, in1=krel[:, :, :],
                                             op0=ALU.min, op1=ALU.add).then_inc(kphi_ok, 1)
                    dve.wait_ge(q_mm, s)
                    wait(dve, qa_ok, s - 1)
                    dve.tensor_tensor(qab[:, :], q_ps, qtab, ALU.mult).then_inc(qab_ok, 1)
                if q == 0 and live(key, 4):
                    route_top(half - 2, s)
                if live(key, 1):
                    dve.wait_ge(kvB_mm, s)
                    wait(dve, num_mm, s - 1)
                    dve.tensor_tensor(state[:, 2:4, :], kv_ps[:, 1, 0:2 * SW].rearrange("p (a n) -> p a n", a=2), mask,
                                      ALU.mult).then_inc(stateB_ok, 1)
                if q == 0 and live(key, 4):
                    route_chosen(half - 2, s, pay[j // 2])
                if live(key, 2):
                    dve.wait_ge(ao_mm, s - 1)
                    if key not in (2, 3):
                        dve.wait_ge(st_x1[q], 8 * (s - 2 - q))
                        dve.wait_ge(xf_ok, s - 3)
                    dve.tensor_tensor(x1[:, q, :, :], ao_ps, h[:, (j + 2) % 4, :, :], ALU.add).then_inc(x1_ok, 1)
                if live(key, 1):
                    dve.wait_ge(kvA_mm, s)
                    dve.tensor_tensor(state[:, 0:2, :], kv_ps[:, 0, 0:2 * SW].rearrange("p (a n) -> p a n", a=2), mask,
                                      ALU.mult).then_inc(stateA_ok, 1)
                    dve.wait_ge(qrel_ok, s)
                    wait(dve, num_mm, s - 2)
                    dve.scalar_tensor_tensor(out=qphi[:, 1 - q, :], in0=qexp[:, :], scalar=1.0, in1=qrel[:, :],
                                             op0=ALU.min, op1=ALU.add).then_inc(qphi_ok, 1)
                if live(key, 0):
                    dve.wait_ge(kk_mm, s + 1)
                    wait(dve, ka_ok, s)
                    dve.tensor_tensor(kab[:, :, :, :], kk_ps.unsqueeze(1).to_broadcast([P, 2, TPB, C]), ktab, ALU.mult).then_inc(kab_ok, 1)
                if q == 0 and live(key, 4):
                    route_place(half - 2)
                if key in (0, 1, 2):
                    norm_stats(key + 1)
                if key == 1:
                    modulation_columns()

            attention_phase(dve, step)

            def slots_in(e, q):
                dve.wait_ge(ld_slots[q], 8 * (e - q) + 16)
                wait(dve, expert_ok, e - 1)
                wait(dve, ys_ok, 2 * (e - 1))
                wait(dve, slot_gate_ok, e)
                for k, (gcol, ecol, out) in enumerate(((G1, E1, gate1), (G2, E2, gate2))):
                    dve.scalar_tensor_tensor(out=out[:, :], in0=xs[q][:, :, ecol], scalar=expert[:, q:q + 1], in1=xs[q][:, :, gcol],
                                             op0=ALU.is_equal, op1=ALU.mult).then_inc(gate_step, 1)
                dve.wait_ge(gate_step, 2 * e + 2)
                dve.tensor_tensor(slot_gate[:, q, :], gate1[:, :], gate2[:, :], ALU.add).then_inc(slot_gate_ok, 1)
                wait(dve, yeT_ok, 2 * (e - 1))
                dve.tensor_scalar(bcol[:, q, :], vec[:, bass.ds(e * EV + V_B1, EV)], 1.0, None, ALU.mult).then_inc(bcol_ok, 1)
                for i, (a, b) in enumerate(PARTS):
                    dve.wait_ge(x_tr, 2 * e + i + 1)
                    wait(dve, up_mm, 8 * (e - 1))
                    dve.tensor_scalar(xeT[:, q, a:b], ps[:, i, 0:b - a], vec[:, V_S2:V_S2 + 1], None, ALU.mult).then_inc(xeT_ok, 1)
                wait(dve, added, 16 * ST * (e - 1))
                dve.tensor_copy(slot_tok[q][:, :], xs[q][:, :, ID]).then_inc(slot_tok_ok, 1)

            def gated(e, q):
                wait(dve, added, 16 * ST * (e - 1))
                dve.wait_ge(slot_gate_ok, e + 1)
                for i, (a, b) in enumerate(PARTS):
                    t0, t1 = a // P, b // P
                    dve.wait_ge(y_tr, 2 * e + i + 1)
                    dve.tensor_tensor(ys[q][:, t0:t1, :], ps[:, i, 0:b - a].rearrange("p (t c) -> p t c", c=C),
                                      slot_gate[:, q, t0:t1].unsqueeze(2).to_broadcast([P, t1 - t0, C]),
                                      ALU.mult).then_inc(ys_ok, 1)

            def expert_step(e, q, key):
                if key != 0:
                    gated(e - 1, 1 - q)
                if key != EXPERTS - 1:
                    slots_in(e + 1, 1 - q)

            slots_in(0, 0)
            by_twos(dve, expert_step)
            gated(EXPERTS - 1, 1)

            def group_in(g, q):
                dve.wait_ge(ld_ac[q], 16 * (g - q) + 32)
                dve.tensor_tensor(x2[:, q, :, :].rearrange("p (b t) c -> p b t c", b=2),
                                  ac[:, q, :, :].rearrange("p (b t) c -> p b t c", b=2),
                                  ga_rows[:, q, :, :].unsqueeze(2).to_broadcast([P, 2, TPB, C]), ALU.mult).then_inc(ga_step, 1)
                dve.wait_ge(ga_step, g + 1)
                dve.tensor_tensor(x2[:, q, :, :], x2[:, q, :, :], x[:, bass.ds(g * SUPT, SUPT), :], ALU.add).then_inc(x2_ok, 1)
                dve.wait_ge(x2_ok, g + 1)
                for t in range(SUPT):
                    dve.bn_stats(stat2[:, t, :], x2[:, q, t, :]).then_inc(stat2_ok, 1)
                dve.wait_ge(stat2_ok, SUPT * (g + 1))
                dve.memset(spare[:, 0:1], 0.0).then_inc(spare_ok, 1)
                for t in range(SUPT):
                    dve.bn_aggr(mv2[:, t, :], stat2[:, t, :]).then_inc(mv2_ok, 1)
                dve.wait_ge(mv2_ok, SUPT * (g + 1))
                wait(dve, rstd2_ok, g)
                dve.tensor_scalar(var2[:, :], mv2[:, :, 1], 1e-5, None, ALU.add).then_inc(var2_ok, 1)
                dve.tensor_scalar(x[:, bass.ds(g * SUPT, SUPT), :], x2[:, q, :, :], 1.0, None, ALU.mult).then_inc(x2_kept, 1)
                wait(dve, y2T_ok, 2 * (g - 1))
                dve.tensor_scalar(modc[:, q, :, :], modT[:, bass.ds(g * 2, 2), :], 1.0, None, ALU.mult).then_inc(modc_ok, 1)
                dve.wait_ge(rstd2_ok, g + 1)
                wait(dve, x2_tr, g)
                for t in range(SUPT):
                    ins = dve.tensor_scalar(xh2[:, t, :], x2[:, q, t, :], mv2[:, t, 0:1], rstd2[:, t:t + 1],
                                            ALU.subtract, ALU.mult)
                ins.then_inc(xh2_ok, 1)

            def result(g, q):
                dve.wait_ge(y2_tr, g + 1)
                wait(dve, st_out[q], 8 * (g - q))
                dve.wait_ge(x2_kept, g + 1)
                dve.tensor_tensor(res[:, q, :, :], ps[:, 1, :].rearrange("p (t c) -> p t c", c=C), x[:, bass.ds(g * SUPT, SUPT), :],
                                  ALU.add).then_inc(res_ok, 1)

            def group_step(g, q, key):
                if key != NSUP - 1:
                    group_in(g + 1, 1 - q)
                if key != 0:
                    result(g - 1, 1 - q)

            group_in(0, 0)
            by_twos(dve, group_step)
            result(NSUP - 1, 1)

        @block.tensor
        def _(pe):
            pe.wait_ge(ld_ident, 16)
            pe.wait_ge(silu_ok, 1)
            pe.transpose(ps[:, 7, 0:BATCH], silu[:, :], ident[0:BATCH, 0:BATCH]).then_inc(siluT_mm, 1)
            pe.wait_ge(siluT_ok, 1)
            pe.wait_ge(ld_wmod, 16)
            for b in range(2):
                ins = pe.matmul(ps[:, 4, 2 * C * b:2 * C * b + 2 * C], siluT[:, b:b + 1].to_broadcast([P, P]), wmod[:, 0:2 * C],
                                start=True, stop=True)
            ins.then_inc(rows_mm, 1)
            pe.matmul(ps[0:BATCH, 5, 0:512], siluT[:, :], wmod[:, 0:512], start=True, stop=True)
            pe.matmul(ps[0:BATCH, 6, 0:256], siluT[:, :], wmod[:, 512:768], start=True, stop=True).then_inc(mod_mm, 1)

            def modulation_columns():
                pe.wait_ge(mod_ok, 1)
                for i, part in enumerate((SB, CB, GB)):
                    ins = pe.transpose(ps[:, 7, 32 + BATCH * i:32 + BATCH * (i + 1)], mod[:, part], ident[0:BATCH, 0:BATCH])
                ins.then_inc(modT_mm, 1)

            def project(out, q, t, cols):
                pe.matmul(out[:, t, :], hnT[:, q, P * t:P * t + P], wkvg[:, cols], start=True, stop=False)
                return pe.matmul(out[:, t, :], ones3[:, 0:P], bias3[:, cols], start=False, stop=True)

            def kv_state(q, c):
                out = kv_ps[:, c // 2, (c % 2) * SW:(c % 2) * SW + SW]
                ends = [P] * ((c + 1) // 2) + [CHUNK] * ((c + 1) % 2)
                for t, end in enumerate(ends):
                    ins = pe.matmul(out, kphi[0:end, q, t, :], vone[0:end, q, t, :], start=(t == 0), stop=(t == len(ends) - 1))
                return ins

            def step(s, half, j, key):
                q = j % 2
                if key == 1:
                    pe.wait_ge(ld_q, 16)
                if key == 2:
                    pe.wait_ge(modT_ok, 1)
                    for s_ in (ld_o, ld_r):
                        pe.wait_ge(s_, 16)
                if key == 4:
                    pe.wait_ge(tri_ok, 1)
                if live(key, 1):
                    wait(pe, qab_ok, s - 1)
                    for i in range(2):
                        cols = slice(SEQ * i, SEQ * i + SEQ)
                        pe.matmul(q_ps[:, cols], wq[:, C * i:C * i + C], hnT[:, 1 - q, :], start=True, stop=False)
                        ins = pe.matmul(q_ps[:, cols], bias3[:, B_Q + C * i:B_Q + C * i + C], ones3[:, :], start=False, stop=True)
                    ins.then_inc(q_mm, 1)
                if live(key, 2):
                    pe.wait_ge(o_ok, s - 1)
                    wait(pe, xfT_ok, s - 2)
                    for t in range(TPB):
                        ins = pe.transpose(tr_ps[:, P * t:P * t + P], o[:, t, :], ident)
                    ins.then_inc(o_tr, 1)
                if live(key, 3):
                    pe.wait_ge(xfT_ok, s - 2)
                    pe.wait_ge(x1_ok, s - 2)
                    if q == 1 and live(key, 5):
                        pe.wait_ge(slot_ok, 2 * (half - 1))
                    first = TPB * (1 - q)
                    for t in range(TPB):
                        pe.matmul(logit_ps[:, first + t, :], xfT[:, P * t:P * t + P], wr[:, :], start=True, stop=False)
                        ins = pe.matmul(logit_ps[:, first + t, :], ones3[:, 0:P], bias3[:, B_R:B_R + EXPERTS], start=False, stop=True)
                    ins.then_inc(logit_mm, 1)
                if live(key, 1):
                    pe.wait_ge(kphi_ok, s)
                    pe.wait_ge(v_ok, s)
                    wait(pe, stateB_ok, s - 1)
                    for c in (2, 3):
                        ins = kv_state(1 - q, c)
                    ins.then_inc(kvB_mm, 1)
                if live(key, 0):
                    pe.wait_ge(hn_ok, s + 1)
                    wait(pe, oT_ok, s - 1)
                    for t in range(TPB):
                        ins = pe.transpose(hnT_ps[:, P * t:P * t + P], hn[:, t, :], ident)
                    ins.then_inc(hn_tr, 1)
                if live(key, 2):
                    pe.wait_ge(oT_ok, s - 1)
                    wait(pe, x1_ok, s - 2)
                    if q == 0 and live(key, 4):
                        pe.wait_ge(logit_ok, half - 1)
                    for t in range(TPB):
                        pe.matmul(ao_ps[:, t, :], oT[:, q, P * t:P * t + P], wo[:, :], start=True, stop=False)
                        ins = pe.matmul(ao_ps[:, t, :], ones3[:, 0:P], bias3[:, B_O:B_O + C], start=False, stop=True)
                    ins.then_inc(ao_mm, 1)
                if live(key, 1):
                    wait(pe, stateA_ok, s - 1)
                    for c in (0, 1):
                        ins = kv_state(1 - q, c)
                    ins.then_inc(kvA_mm, 1)
                if live(key, 0):
                    if key == 0:
                        pe.wait_ge(bias_ok, 1)
                        pe.wait_ge(setup_pool, 9)
                        pe.wait_ge(ld_kvg, 16)
                    pe.wait_ge(hnT_ok, s + 1)
                    wait(pe, kab_ok, s)
                    for t in range(TPB):
                        ins = project(kk_ps, q, t, slice(0, C))
                    ins.then_inc(kk_mm, 1)
                if q == 0 and live(key, 4):
                    pe.wait_ge(chosen_ok, half - 1)
                    pe.wait_ge(logit_ok, half - 1)
                    if live(key, 2):
                        pe.wait_ge(x1_ok, s - 1)
                    pe.matmul(pos_ps, ones[:, :], before[:, :].unsqueeze(1).to_broadcast([P, PAIR, EXPERTS]), start=True, stop=False)
                    for t in range(PAIR - 1):
                        pe.matmul(pos_ps[:, t + 1:PAIR, :], ones[:, :],
                                  chosen[:, t:t + 1, :].to_broadcast([P, PAIR - 1 - t, EXPERTS]), start=False, stop=False)
                    pe.matmul(pos_ps, tri[:, :], chosen[:, :, :], start=False, stop=True).then_inc(pos_mm, 1)
                if live(key, 1):
                    pe.wait_ge(qphi_ok, s)
                    wait(pe, gnum_ok, s - 1)
                    pe.wait_ge(stateB_ok, s)
                    pe.wait_ge(stateA_ok, s)
                    for c in range(CHUNKS):
                        at = CHUNK * (c % 2)
                        ins = pe.matmul(num_ps[at:at + CHUNK, c // 2, :], qphi[:, 1 - q, CHUNK * c:CHUNK * c + CHUNK],
                                        state[:, c, :], start=True, stop=True)
                    ins.then_inc(num_mm, 1)
                if live(key, 0):
                    wait(pe, v_ok, s)
                    wait(pe, g_ok, s)
                    for t in range(TPB):
                        ins = project(vg_ps, q, t, slice(C, 3 * C))
                    ins.then_inc(vg_mm, 1)
                if live(key, 2):
                    pe.wait_ge(xf_ok, s - 1)
                    pe.wait_ge(oT_ok, s - 1)
                    if live(key, 0):
                        pe.wait_ge(hnT_ok, s + 1)
                    buf, first = pay[j // 2 ^ 1], TPB * q
                    for t in range(TPB):
                        ins = pe.transpose(tr_ps[:, P * t:P * t + P], buf[:, first + t, 0:C], ident)
                    ins.then_inc(xf_tr, 1)
                if key == 0:
                    modulation_columns()

            attention_phase(pe, step)

            def transpose_slots(e, q):
                pe.wait_ge(ld_slots[q], 8 * (e - q) + 16)
                wait(pe, ys_ok, 2 * (e - 1))
                for t in range(ST):
                    i, at = (0, P * t) if P * t < SPLIT else (1, P * t - SPLIT)
                    ins = pe.transpose(ps[:, i, at:at + P], xs[q][:, t, 0:C], ident)
                    if t in (SPLIT // P - 1, ST - 1):
                        ins.then_inc(x_tr, 1)

            def up(e, q, k):
                if k == 0:
                    pe.wait_ge(ld_w[q], 16 * (e - q) + 32)
                wait(pe, gelu_ok, 8 * e + 2 * k - 2)
                for i, (a, b) in enumerate(PARTS):
                    if k == 0:
                        pe.wait_ge(xeT_ok, 2 * e + i + 1)
                    pe.matmul(ps[:, 2 + 2 * (k % 2) + i, 0:b - a], w1[:, q, P * k:P * k + P], xeT[:, q, a:b],
                              start=True, stop=True).then_inc(up_mm, 1)

            def down(e, q, k):
                if k == 0:
                    wait(pe, yeT_ok, 2 * e)
                for i, (a, b) in enumerate(PARTS):
                    pe.wait_ge(gelu_ok, 8 * e + 2 * k + i + 1)
                    ins = pe.matmul(ps[:, 6 + i, 0:b - a], w2[:, q, k, :], hid[:, k % 2, a:b], start=(k == 0), stop=(k == HB - 1))
                ins.then_inc(down_mm, 1)

            def transpose_outputs(e):
                if not (isinstance(e, int) and e == EXPERTS - 1):
                    pe.wait_ge(xeT_ok, 2 * e + 4)
                else:
                    pe.wait_ge(ys_ok, 2 * e)
                for t in range(ST):
                    i, at = (0, P * t) if P * t < SPLIT else (1, P * t - SPLIT)
                    pe.wait_ge(yeT_ok, 2 * e + i + 1)
                    ins = pe.transpose(ps[:, i, at:at + P], yeT[:, P * t:P * t + P], ident)
                    if t in (SPLIT // P - 1, ST - 1):
                        ins.then_inc(y_tr, 1)

            def expert_step(e, q, key):
                up(e, q, 0)
                up(e, q, 1)
                if key != 0:
                    transpose_outputs(e - 1)
                down(e, q, 0)
                up(e, q, 2)
                down(e, q, 1)
                up(e, q, 3)
                if key != EXPERTS - 1:
                    transpose_slots(e + 1, 1 - q)
                down(e, q, 2)
                down(e, q, 3)

            transpose_slots(0, 0)
            by_twos(pe, expert_step)
            transpose_outputs(EXPERTS - 1)

            def transpose_group(g):
                pe.wait_ge(xh2_ok, g + 1)
                wait(pe, hT_ok, 2 * g)
                for t in range(SUPT):
                    ins = pe.transpose(ps[:, 0, P * t:P * t + P], xh2[:, t, :], ident)
                ins.then_inc(x2_tr, 1)

            def up2(g, q, k):
                if k == 0:
                    pe.wait_ge(hT_ok, 2 * g + 2)
                wait(pe, gelu2_ok, 4 * g + k - 1)
                pe.matmul(ps[:, 2 + k % 2, :], f1[:, P * k:P * k + P], hT[:, q, :], start=True, stop=True).then_inc(up2_mm, 1)

            def down2(g, q, k):
                if k == 0:
                    wait(pe, y2T_ok, 2 * (g - 1))
                pe.wait_ge(gelu2_ok, 4 * g + k + 1)
                pe.matmul(ps[:, 4 + q, :], f2[:, k, :], hid2[:, k % 2, :], start=(k == 0), stop=(k == HB - 1)).then_inc(down2_mm, 1)

            def transpose_results(g):
                pe.wait_ge(y2T_ok, 2 * g + 2)
                wait(pe, res_ok, g)
                for t in range(SUPT):
                    ins = pe.transpose(ps[:, 1, P * t:P * t + P], y2T[:, P * t:P * t + P], ident)
                ins.then_inc(y2_tr, 1)

            def group_step(g, q, key):
                up2(g, q, 0)
                up2(g, q, 1)
                if key != 0:
                    transpose_results(g - 1)
                down2(g, q, 0)
                up2(g, q, 2)
                down2(g, q, 1)
                if key != NSUP - 1:
                    transpose_group(g + 1)
                up2(g, q, 3)
                down2(g, q, 2)
                down2(g, q, 3)

            pe.wait_ge(ld_ffn, 32)
            transpose_group(0)
            by_twos(pe, group_step)
            transpose_results(NSUP - 1)


def kernel(L0_attn_x, L0_attn_norm1_scale, L0_attn_norm2_scale, L0_attn_Wq, L0_attn_bq, L0_attn_Wk, L0_attn_bk,
           L0_attn_Wv, L0_attn_bv, L0_attn_Wg, L0_attn_bg, L0_attn_Wo, L0_attn_bo, L0_attn_router_W, L0_attn_router_b,
           L0_attn_W1, L0_attn_b1, L0_attn_W2, L0_attn_b2, L0_ffn_w1, L0_ffn_b1, L0_ffn_w2, L0_ffn_b2, L0_c, L0_wmod):
    import concourse.bacc as _bacc
    from concourse.bass_utils import run_bass_kernel_spmd as _run

    def flat(a):
        return np.ascontiguousarray(np.asarray(a))

    swap = np.arange(C).reshape(HEADS, 2, DK // 2)[:, ::-1].reshape(-1)
    wq_, wk, wv, wg = (flat(w) for w in (L0_attn_Wq, L0_attn_Wk, L0_attn_Wv, L0_attn_Wg))
    bq, bk, bv, bg = (flat(w) for w in (L0_attn_bq, L0_attn_bk, L0_attn_bv, L0_attn_bg))
    columns = [flat(L0_attn_norm1_scale)[:, None], flat(L0_attn_norm2_scale)[:, None], flat(L0_ffn_b1).reshape(HB, P).T,
               flat(L0_ffn_b2)[:, None]]
    b1, b2 = flat(L0_attn_b1), flat(L0_attn_b2)
    for e in range(EXPERTS):
        columns += [b1[e].reshape(HB, P).T, b2[e][:, None]]
    konst, empty = constants()
    arrays = {
        "x": flat(L0_attn_x).reshape(TOKENS, C),
        "c": flat(L0_c),
        "wmod": flat(L0_wmod),
        "wkvg": np.concatenate([wk, wv, wg], 1),
        "wq": np.concatenate([wq_, wq_[:, swap]], 1),
        "wo": flat(L0_attn_Wo),
        "wr": flat(L0_attn_router_W),
        "w1": flat(L0_attn_W1),
        "w2": flat(L0_attn_W2),
        "f1": flat(L0_ffn_w1),
        "f2": flat(L0_ffn_w2),
        "vec": np.ascontiguousarray(np.concatenate(columns, 1)),
        "bias": np.concatenate([bk, bv, bg, bq, bq[swap], flat(L0_attn_bo), flat(L0_attn_router_b)])[None, :],
        "konst": konst,
        "empty": empty,
    }
    nc = _bacc.Bacc("TRN2", target_bir_lowering=False, num_devices=1)
    args = [nc.dram_tensor(f"in_{n}", a.shape, F32, kind="ExternalInput").ap() for n, a in arrays.items()]
    out = nc.dram_tensor("out", (TOKENS, C), F32, kind="ExternalOutput").ap()
    adaln_moe(nc, *args, out)
    r = _run(nc, [{f"in_{n}": a for n, a in arrays.items()}], core_ids=[0])
    return r.results[0]["out"].reshape(BATCH, SEQ, C)
```

```python
from contextlib import ExitStack

import numpy as np

import concourse.bass as bass
from concourse import mybir

F32 = mybir.dt.float32
BF16 = mybir.dt.bfloat16
U32 = mybir.dt.uint32
ALU = mybir.AluOpType
ACT = mybir.ActivationFunctionType
AX = mybir.AxisListType

P = 128
BATCH, SEQ, C = 16, 256, 128
TOKENS = BATCH * SEQ
TILES = TOKENS // P
TPB = SEQ // P
HEADS = 16
DK = C // HEADS
CHUNK = 64
CHUNKS = SEQ // CHUNK
SW = C + HEADS
EXPERTS, TOPK = 8, 2
CAPACITY = int(1.25 * TOKENS / EXPERTS)
HID = 512
HB = HID // P
ST = CAPACITY // P
SLOTS = EXPERTS * CAPACITY
ID, G1, G2, E1, E2, PAY = C, C + 1, C + 2, C + 3, C + 4, C + 5
PAIR = 2 * TPB
IN_LOOP = -1
STEPS = BATCH + 6
ROUTE = 17
FAR = 1.0e5
NSUP = BATCH // 2
SUPT = 2 * TPB
SPLIT = 384
PARTS = ((0, SPLIT), (SPLIT, CAPACITY))

K_IDENT, K_TRI, K_KTAB, K_QTAB = 0, 128, 256, 768
K_MASK = 1280
K_IOTA = K_MASK + SW
K_BASE = K_IOTA + EXPERTS
K_TOK = K_BASE + EXPERTS
K_SEL = K_TOK + PAIR
K_ALL = K_SEL + 3
V_S1, V_S2, V_FB1 = 0, 1, 2
V_B1 = V_FB1 + HB
V_ALL = V_B1 + EXPERTS * HB
B_KVG = 0
B_Q = 3 * C
B_O = B_Q + 2 * C
B_R = B_O + C
B_ALL = B_R + EXPERTS
QUARTER = [slice(TILES // 4 * i, TILES // 4 * (i + 1)) for i in range(4)]
SA, CA, GA, SB, CB, GB = (slice(C * i, C * i + C) for i in range(6))


def constants():
    k = np.zeros((P, K_ALL), np.float32)
    k[:, K_IDENT:K_IDENT + P] = np.eye(P)
    k[:, K_TRI:K_TRI + P] = np.triu(np.ones((P, P)), 1)
    half = DK // 2
    inv = np.float32(1.0) / np.float32(10000.0) ** (np.arange(half, dtype=np.float32) / np.float32(half))
    ang = np.arange(SEQ, dtype=np.float32)[:, None] * inv[None, :]
    cos = np.tile(np.concatenate([np.cos(ang), np.cos(ang)], 1), (1, HEADS))
    sin = np.tile(np.concatenate([-np.sin(ang), np.sin(ang)], 1), (1, HEADS))
    k[:, K_KTAB:K_KTAB + 512] = np.stack([cos, -sin]).reshape(2, TPB, P, C).transpose(2, 0, 1, 3).reshape(P, -1)
    k[:, K_QTAB:K_QTAB + 512] = np.concatenate([cos.T, sin.T], 1)
    head = np.arange(C) // DK
    k[:, K_MASK:K_MASK + C] = head[:, None] == head[None, :]
    k[:, K_MASK + C:K_MASK + SW] = head[:, None] == np.arange(HEADS)[None, :]
    k[:, K_IOTA:K_IOTA + EXPERTS] = np.arange(EXPERTS)
    k[:, K_BASE:K_BASE + EXPERTS] = np.arange(EXPERTS) * CAPACITY
    k[:, K_TOK:K_TOK + PAIR] = np.arange(P)[:, None] + P * np.arange(PAIR)[None, :]
    k[:3, K_SEL:K_SEL + 3] = np.eye(3)
    empty = np.zeros((P, ST, PAY), np.float32)
    empty[:, :, ID] = TOKENS + np.arange(P)[:, None] + P * np.arange(ST)[None, :]
    return k, empty


def adaln_moe(nc, x_d, c_d, wmod_d, wkvg_d, wq_d, wo_d, wr_d, w1_d, w2_d, f1_d, f2_d,
              vec_d, b2_d, bias_d, const_d, empty_d, out_d):
    mod_d = nc.dram_tensor("mod_rows", [BATCH, 6 * C], F32).ap()
    slot_d = nc.dram_tensor("slots", [SLOTS, PAY], F32).ap()
    acc_d = nc.dram_tensor("acc", [TOKENS + CAPACITY, C], F32).ap()

    with ExitStack() as ctx:
        def sb(name, shape, dt=F32):
            return ctx.enter_context(nc.sbuf_tensor(name, shape, dt))

        def sem(name):
            return ctx.enter_context(nc.semaphore(name))

        def sems(name, n=2):
            return [sem(f"{name}{i}") for i in range(n)]

        ps = ctx.enter_context(nc.psum_tensor("ps", [P, 8, 512], F32))
        konst = sb("konst", [P, K_ALL])
        empty = sb("empty", [P, ST, PAY])
        vec = sb("vec", [P, V_ALL])
        x = sb("x", [P, TILES, C])
        wkvg = sb("wkvg", [P, 3 * C])
        wq = sb("wq", [P, 2 * C])
        wo = sb("wo", [P, C])
        wr = sb("wr", [P, EXPERTS])
        f1 = sb("f1", [P, HID])
        f2 = sb("f2", [P, HB, C])
        w1 = sb("w1", [P, 2, HID])
        w2 = sb("w2", [P, 2, HB, C])
        ident = konst[:, K_IDENT:K_IDENT + P]

        cond = sb("cond", [BATCH, C])
        cond_t = sb("cond_t", [BATCH, C])
        silu = sb("silu", [BATCH, C])
        siluT = sb("siluT", [P, BATCH])
        wmod = sb("wmod", [P, 6 * C])
        mod = sb("mod", [BATCH, 6 * C])
        mod_s = sb("mod_s", [BATCH, 2, C])
        mod_m = sb("mod_m", [BATCH, 2, C])
        modT = sb("modT", [P, BATCH, 2])
        bias = sb("bias", [3, B_ALL])
        bpart = sb("bpart", [3, 2, B_ALL], BF16)
        bsum = sb("bsum", [3, B_ALL])
        bias3 = sb("bias3", [3, B_ALL], BF16)
        ones3 = sb("ones3", [3, SEQ], BF16)
        ones = sb("ones", [P, P], BF16)
        tri = sb("tri", [P, P], BF16)
        power = sb("power", [P, TILES])

        stat = sb("stat", [P, TILES, 6])
        mean = sb("mean", [P, TILES])
        var = sb("var", [P, TILES])
        dmean = sb("dmean", [P, TILES])
        rstd = sb("rstd", [P, TILES])
        nmr = sb("nmr", [P, TILES])

        rows = sb("rows", [P, 2, 2 * C])
        xhat = sb("xhat", [P, 2, TPB, C])
        h = sb("h", [P, 4, TPB, C])
        junk = sb("junk", [P, TPB, C])
        ms1 = sb("ms1", [P, 2, TPB])
        r1 = sb("r1", [P, 2, TPB])
        hn = sb("hn", [P, TPB, C])
        hnT = sb("hnT", [P, 2, SEQ])
        kab = sb("kab", [P, 2, TPB, C])
        qab = sb("qab", [P, 2 * SEQ])
        ka = sb("ka", [P, TPB, C])
        qa = sb("qa", [P, SEQ])
        kexp = sb("kexp", [P, TPB, C])
        krel = sb("krel", [P, TPB, C])
        qexp = sb("qexp", [P, SEQ])
        qrel = sb("qrel", [P, SEQ])
        kphi = sb("kphi", [P, 2, TPB, C])
        qphi = sb("qphi", [P, 2, SEQ])
        vone = sb("vone", [P, 2, TPB, SW])
        gate = sb("gate", [P, 2, TPB, C])
        state = sb("state", [P, CHUNKS, SW])
        gnum = sb("gnum", [P, TPB, C])
        den = sb("den", [P, TPB, HEADS])
        rden = sb("rden", [P, TPB, HEADS])
        o = sb("o", [P, TPB, C])
        oT = sb("oT", [P, 2, SEQ])
        x1 = sb("x1", [P, 2, TPB, C])
        junk2 = sb("junk2", [P, TPB, C])
        ms2 = sb("ms2", [P, 2, TPB])
        r2 = sb("r2", [P, 2, TPB])
        pay = [sb(f"pay{i}", [P, PAIR, PAY]) for i in range(2)]
        xfT = sb("xfT", [P, SEQ])

        logit = sb("logit", [P, PAIR, EXPERTS])
        top = sb("top", [P, PAIR, EXPERTS])
        topi = sb("topi", [P, PAIR, EXPERTS], U32)
        hot = sb("hot", [P, PAIR, TOPK, EXPERTS])
        chosen = sb("chosen", [P, PAIR, EXPERTS], BF16)
        gain = sb("gain", [P, EXPERTS])
        count = sb("count", [P, EXPERTS])
        before = sb("before", [P, EXPERTS], BF16)
        slot = sb("slot", [P, PAIR, EXPERTS])
        over = sb("over", [P, PAIR, EXPERTS])
        slot_of = sb("slot_of", [P, PAIR, TOPK, EXPERTS])
        row_u = [sb(f"row_u{i}", [P, PAIR, TOPK], U32) for i in range(2)]
        row_f = sb("row_f", [P, PAIR, TOPK])
        ldiff = sb("ldiff", [P, PAIR])
        lexp = sb("lexp", [P, PAIR])
        lsum = sb("lsum", [P, PAIR])
        lrec = sb("lrec", [P, PAIR])
        tok = sb("tok", [P, PAIR])
        pair_tokens = sb("pair_tokens", [P, PAIR])

        xs = [sb(f"xs{i}", [P, ST, PAY]) for i in range(2)]
        xeT = sb("xeT", [P, 2, CAPACITY])
        bcol = sb("bcol", [P, 2, HB])
        hid = sb("hid", [P, 2, HB, CAPACITY])
        b2_rows = sb("b2_rows", [P, EXPERTS + 1, C])
        yb = sb("yb", [P, ST, C])
        ys = [sb(f"ys{i}", [P, ST, C]) for i in range(2)]
        expert = sb("expert", [P, 2])
        choice_gate = sb("choice_gate", [P, 2, TOPK, ST])
        slot_gate = sb("slot_gate", [P, ST])
        slot_id = sb("slot_id", [P, 2, ST])
        slot_tok = [sb(f"slot_tok{i}", [P, ST], U32) for i in range(2)]
        ac = sb("ac", [P, 2, SUPT, C])
        ga_rows = sb("ga_rows", [P, BATCH, C])
        gb_rows = sb("gb_rows", [P, BATCH, C])
        x2 = sb("x2", [P, 2, SUPT, C])
        stat2 = sb("stat2", [P, SUPT, 6])
        mv2 = sb("mv2", [P, SUPT, 2])
        var2 = sb("var2", [P, SUPT])
        rstd2 = sb("rstd2", [P, 2, SUPT])
        nmr2 = sb("nmr2", [P, 2, SUPT])
        early = sb("early", [P, 1])
        spare = sb("spare", [P, 2])
        xh2 = sb("xh2", [P, SUPT, C])
        modc = sb("modc", [P, 2, 2, 2])
        hT = sb("hT", [P, 2, SUPT * P])
        hid2 = sb("hid2", [P, 2, HB, SUPT * P])
        y2 = sb("y2", [P, SUPT, C])
        res = sb("res", [P, 2, SUPT, C])

        ld_const, ld_c, ld_wmod, ld_bias, ld_vec, ld_empty = (sem(f"ld_{n}") for n in ("const", "c", "wmod", "bias", "vec", "empty"))
        ld_ident, ld_sel, bias_first, rows_mm, rows_ok = (sem(n) for n in ("ld_ident", "ld_sel", "bias_first", "rows_mm", "rows_ok"))
        ld_x = sems("ld_x", 4)
        ld_kvg, ld_q, ld_o, ld_r, ld_ffn = (sem(f"ld_{n}") for n in ("kvg", "q", "o", "r", "ffn"))
        st_mod, st_empty, st_dummy = sem("st_mod"), sem("st_empty"), sem("st_dummy")
        setup_pool, tanh_c, silu_ok, siluT_mm, siluT_ok, mod_mm, mod_ok = (
            sem(n) for n in ("setup_pool", "tanh_c", "silu_ok", "siluT_mm", "siluT_ok", "mod_mm", "mod_ok"))
        modT_mm, modT_ok, bias_ok, stat_ok, rstd_ok, nmr_ok, setup_dve = (
            sem(n) for n in ("modT_mm", "modT_ok", "bias_ok", "stat_ok", "rstd_ok", "nmr_ok", "setup_dve"))
        mod_step, ln_step, bias_step, stat_n, tok_ok = (sem(n) for n in ("mod_step", "ln_step", "bias_step", "stat_n", "tok_ok"))
        ld_rows = sems("ld_rows")
        (xhat_ok, h_ok, h_step, ms1_ok, r1_ok, hn_ok, hn_tr, hnT_ok) = (
            sem(n) for n in ("xhat_ok", "h_ok", "h_step", "ms1_ok", "r1_ok", "hn_ok", "hn_tr", "hnT_ok"))
        (kk_mm, vg_mm, q_mm, kab_ok, qab_ok, ka_ok, qa_ok, krel_ok, qexp_ok, qrel_ok, kphi_ok, qphi_ok, v_ok, g_ok) = (
            sem(n) for n in ("kk_mm", "vg_mm", "q_mm", "kab_ok", "qab_ok", "ka_ok", "qa_ok", "krel_ok", "qexp_ok", "qrel_ok",
                             "kphi_ok", "qphi_ok", "v_ok", "g_ok"))
        (kvA_mm, kvB_mm, stateA_ok, stateB_ok, num_mm, gnum_ok, den_ok, rden_ok, o_ok, o_tr, oT_ok) = (
            sem(n) for n in ("kvA_mm", "kvB_mm", "stateA_ok", "stateB_ok", "num_mm", "gnum_ok", "den_ok", "rden_ok", "o_ok", "o_tr", "oT_ok"))
        (ao_mm, x1_ok, ms2_ok, r2_ok, xf_ok, xf_tr, xfT_ok, logit_mm) = (
            sem(n) for n in ("ao_mm", "x1_ok", "ms2_ok", "r2_ok", "xf_ok", "xf_tr", "xfT_ok", "logit_mm"))
        st_x1 = sems("st_x1")
        (logit_ok, routing, chosen_ok, pos_mm, ldiff_ok, lexp_ok, row_ok, gates_ok) = (
            sem(n) for n in ("logit_ok", "routing", "chosen_ok", "pos_mm", "ldiff_ok", "lexp_ok", "row_ok", "gates_ok"))
        ld_w1, ld_w2, ld_slots = sems("ld_w1"), sems("ld_w2"), sems("ld_slots")
        (x_tr, xeT_ok, up_mm, gelu_ok, down_mm, yb_ok, ys_ok, gate_step, slot_gate_ok, slot_id_ok, slot_tok_ok, expert_ok, added) = (
            sem(n) for n in ("x_tr", "xeT_ok", "up_mm", "gelu_ok", "down_mm", "yb_ok", "ys_ok", "gate_step",
                             "slot_gate_ok", "slot_id_ok", "slot_tok_ok", "expert_ok", "added"))
        early_ok = sem("early_ok")
        ld_b2, ld_gains, scatter_go = sem("ld_b2"), sem("ld_gains"), sem("scatter_go")
        ld_ac, st_out = sems("ld_ac"), sem("st_out")
        (ga_step, x2_ok, stat2_ok, mv2_ok, var2_ok, rstd2_ok, xh2_ok, modc_ok, x2_tr, hT_ok, up2_mm, gelu2_ok, down2_mm,
         y2_ok, y2_gated, res_ok) = (
            sem(n) for n in ("ga_step", "x2_ok", "stat2_ok", "mv2_ok", "var2_ok", "rstd2_ok", "xh2_ok", "modc_ok", "x2_tr",
                             "hT_ok", "up2_mm", "gelu2_ok", "down2_mm", "y2_ok", "y2_gated", "res_ok"))
        bcol_ok, x2_kept, tri_ok, nmr2_ok = sem("bcol_ok"), sem("x2_kept"), sem("tri_ok"), sem("nmr2_ok")
        rowf_ok, slot_ok = sem("rowf_ok"), sem("slot_ok")
        scattered = sems("scattered", 4)

        block = ctx.enter_context(nc.Block())

        kk_ps = ps[:, 0, 0:TPB * C].rearrange("p (t n) -> p t n", t=TPB)
        vg_ps = ps[:, 1, :].rearrange("p (t n) -> p t n", t=TPB)
        q_ps = ps[:, 2, :]
        hnT_ps = ps[:, 3, 0:SEQ]
        tr_ps = ps[:, 3, SEQ:2 * SEQ]
        kv_ps = ps[:, 4:6, :]
        num_ps = ps[:, 6, 0:TPB * SW].rearrange("p (t n) -> p t n", t=TPB)
        ao_ps = ps[:, 7, 0:TPB * C].rearrange("p (t n) -> p t n", t=TPB)
        logit_ps = ps[:, 7, 256:288].rearrange("p (t e) -> p t e", e=EXPERTS)
        pos_ps = ps[:, 7, 288:320].rearrange("p (t e) -> p t e", e=EXPERTS)

        def wait(eng, s, n):
            if not isinstance(n, int) or n > 0:
                eng.wait_ge(s, n)

        def attention_phase(eng, step):
            for s in range(7):
                step(s, s // 2, s % 4, s)
            with eng.Fori(1, 3, 1) as turn:
                for i in range(1, 5):
                    step(turn * 4 + 2 + i, turn * 2 + 1 + i // 2, (i + 2) % 4, IN_LOOP)
            for s in range(BATCH - 1, STEPS):
                step(s, s // 2, s % 4, s)

        def by_twos(eng, step, peeled):
            for e in range(peeled):
                step(e, e % 2, e)
            with eng.Fori(1, 3, 1) as turn:
                for i in range(2):
                    step(turn * 2 + (peeled - 2 + i), (peeled + i) % 2, IN_LOOP)
            for e in range(peeled + 4, 8):
                step(e, e % 2, e)

        def live(key, lag):
            return key == IN_LOOP or 0 <= key - lag < BATCH

        @block.sync
        def _(sp):
            def load_x(i):
                n = TILES // 4
                sp.dma_start(x[:, n * i:n * i + n, :],
                             x_d[n * i * P:n * (i + 1) * P, :].rearrange("(t p) c -> p t c", p=P)).then_inc(ld_x[i], 16)

            def load_rows(b, j):
                wait(sp, h_ok, b - 1)
                sp.dma_start(rows[:, j % 2, :], mod_d[bass.ds(b, 1), 0:2 * C].to_broadcast([P, 2 * C])).then_inc(ld_rows[j % 2], 16)

            sp.dma_start(cond[:, :], c_d).then_inc(ld_c, 16)
            sp.dma_start(konst[:, 0:K_TRI], const_d[:, 0:K_TRI]).then_inc(ld_ident, 16)
            load_x(0)
            sp.dma_start(wmod[:, :], wmod_d).then_inc(ld_wmod, 16)
            sp.dma_start(konst[0:3, K_SEL:K_ALL], const_d[0:3, K_SEL:K_ALL]).then_inc(ld_sel, 16)
            sp.dma_start(bias[:, :], bias_d[0:1, :].to_broadcast([3, B_ALL])).then_inc(ld_bias, 16)
            sp.dma_start(vec[:, :], vec_d).then_inc(ld_vec, 16)
            sp.dma_start(konst[:, K_TRI:K_SEL], const_d[:, K_TRI:K_SEL]).then_inc(ld_const, 16)
            sp.dma_start(wkvg[:, :], wkvg_d).then_inc(ld_kvg, 16)
            sp.dma_start(wq[:, :], wq_d).then_inc(ld_q, 16)
            load_x(1)
            sp.dma_start(wo[:, :], wo_d).then_inc(ld_o, 16)
            sp.dma_start(wr[:, :], wr_d).then_inc(ld_r, 16)
            load_x(2)
            load_x(3)
            sp.dma_start(empty[:, :, :], empty_d).then_inc(ld_empty, 16)
            sp.wait_ge(mod_ok, 1)
            sp.dma_start(mod_d, mod[:, :]).then_inc(st_mod, 16)
            sp.wait_ge(st_mod, 16)

            def load_w1(e, q):
                wait(sp, up_mm, 8 * (e - 1))
                sp.dma_start(w1[:, q, :], w1_d[bass.ds(e, 1), :, :].rearrange("a k n -> k (a n)")).then_inc(ld_w1[q], 16)

            def load_w2(e, q):
                wait(sp, down_mm, 2 * (e - 1))
                sp.dma_start(w2[:, q, :, :], w2_d[bass.ds(e, 1), :, :].rearrange("a (b p) c -> p (a b) c", p=P)).then_inc(ld_w2[q], 16)

            def empty_slots():
                sp.wait_ge(ld_empty, 16)
                for e in range(EXPERTS):
                    sp.dma_start(slot_d[e * CAPACITY:(e + 1) * CAPACITY, :].rearrange("(t p) c -> p t c", p=P),
                                 empty[:, :, :]).then_inc(st_empty, 16)
                sp.dma_start(acc_d[TOKENS:TOKENS + CAPACITY, :].rearrange("(t p) c -> p t c", p=P),
                             empty[:, :, 0:C]).then_inc(st_dummy, 16)

            def step(s, half, j, key):
                if live(key, 0) and key not in (0, 1):
                    load_rows(s, j)
                if key == 3:
                    empty_slots()
                    for e in range(2):
                        load_w1(e, e)
                        load_w2(e, e)
                    sp.dma_start(b2_rows[:, :, :], b2_d.unsqueeze(0).to_broadcast([P, EXPERTS + 1, C])).then_inc(ld_b2, 16)
                    sp.dma_start(ga_rows[:, :, :], mod_d[:, GA].unsqueeze(0).to_broadcast([P, BATCH, C])).then_inc(ld_gains, 16)
                    sp.dma_start(gb_rows[:, :, :], mod_d[:, GB].unsqueeze(0).to_broadcast([P, BATCH, C])).then_inc(ld_gains, 16)
                    sp.dma_start(f1[:, :], f1_d).then_inc(ld_ffn, 16)
                    sp.dma_start(f2[:, :, :], f2_d.rearrange("(b p) c -> p b c", p=P)).then_inc(ld_ffn, 16)
                if live(key, 3):
                    sp.wait_ge(x1_ok, s - 2)
                    sp.dma_start(acc_d[bass.ds((s - 3) * SEQ, SEQ), :].rearrange("(t p) c -> p t c", p=P),
                                 x1[:, (j + 1) % 2, :, :]).then_inc(st_x1[(j + 1) % 2], 16)

            attention_phase(sp, step)
            for i in range(2):
                sp.wait_ge(st_x1[i], 16 * (BATCH // 2))
            for i in range(4):
                sp.wait_ge(scattered[i], 64 * (BATCH // 4))
            sp.wait_ge(st_dummy, 16)

            def expert_step(e, q, key):
                wait(sp, x_tr, 2 * (e - 1))
                wait(sp, slot_id_ok, e - 1)
                wait(sp, gate_step, 2 * (e - 1))
                sp.dma_start(xs[q][:, :, :], slot_d[bass.ds(e * CAPACITY, CAPACITY), :].rearrange("(t p) c -> p t c", p=P))\
                  .then_inc(ld_slots[q], 16)
                if key not in (0, 1):
                    load_w1(e, q)
                    load_w2(e, q)

            by_twos(sp, expert_step, 3)
            sp.wait_ge(added, 16 * ST * EXPERTS)

            def group_step(g, q, key):
                wait(sp, ga_step, g - 1)
                sp.dma_start(ac[:, q, :, :], acc_d[bass.ds(g * (SUPT * P), SUPT * P), :].rearrange("(t p) c -> p t c", p=P))\
                  .then_inc(ld_ac[q], 16)

            by_twos(sp, group_step, 2)
            sp.wait_ge(st_out, 16 * NSUP)

        @block.gpsimd
        def _(pool):
            pool.memset(power[:, :], -0.5).then_inc(setup_pool, 1)
            pool.memset(ones3[:, :], 1.0).then_inc(setup_pool, 1)
            pool.memset(ones[:, :], 1.0).then_inc(setup_pool, 1)
            pool.memset(vone[:, :, :, C:SW], 1.0).then_inc(setup_pool, 1)
            pool.memset(count[:, :], 0.0).then_inc(setup_pool, 1)
            pool.memset(pair_tokens[:, :], float(PAIR * P)).then_inc(setup_pool, 1)
            pool.memset(expert[:, 0:1], 0.0).then_inc(setup_pool, 1)
            pool.memset(expert[:, 1:2], 1.0).then_inc(setup_pool, 1)
            pool.wait_ge(setup_pool, 8)

            def norm_scale(i):
                pool.wait_ge(stat_ok, i + 1)
                pool.tensor_tensor(rstd[:, QUARTER[i]], var[:, QUARTER[i]], power[:, QUARTER[i]], ALU.pow).then_inc(rstd_ok, 1)

            norm_scale(0)

            def scatter(row, i):
                q, t, k = row // 2, TPB * (row % 2) + i // 2, i % 2
                pool.indirect_dma_start(
                    slot_d[:, :], bass.IndirectOffsetOnAxis(row_u[q][:, t, k:k + 1], 0),
                    pay[q][:, t, :], None,
                    bounds_check=SLOTS - 1, oob_is_err=False).then_inc(scattered[row], 16)

            def by_halves(k):
                return k.rearrange("p t (h u d) -> p (t h) u d", u=2, d=DK // 2)

            def step(s, half, j, key):
                if live(key, 1):
                    pool.wait_ge(kab_ok, s)
                    wait(pool, krel_ok, s - 1)
                    pool.tensor_tensor(by_halves(ka[:, :, :]), by_halves(kab[:, 0, :, :]),
                                       by_halves(kab[:, 1, :, :])[:, :, ::-1, :], ALU.add).then_inc(ka_ok, 1)
                if live(key, 6):
                    scatter((j + 2) % 4, 1)
                if live(key, 0):
                    pool.wait_ge(ms1_ok, s + 1)
                    pool.tensor_tensor(r1[:, j % 2, :], ms1[:, j % 2, :], power[:, 0:TPB], ALU.pow).then_inc(r1_ok, 1)
                if live(key, 6):
                    scatter((j + 2) % 4, 2)
                if live(key, 1):
                    pool.wait_ge(qab_ok, s)
                    wait(pool, qrel_ok, s - 1)
                    pool.tensor_tensor(qa[:, :], qab[:, 0:SEQ], qab[:, SEQ:2 * SEQ], ALU.add).then_inc(qa_ok, 1)
                if live(key, 6):
                    scatter((j + 2) % 4, 3)
                if key == 5:
                    pool.wait_ge(st_empty, 16 * EXPERTS)
                if live(key, 5) and j % 2 == 1:
                    pool.wait_ge(row_ok, half - 1)
                    pool.wait_ge(gates_ok, 3 * (half - 1))
                    pool.wait_ge(xf_ok, s - 3)
                    pool.tensor_tensor(tok[:, :], tok[:, :], pair_tokens[:, :], ALU.add).then_inc(tok_ok, 1)
                if live(key, 5):
                    scatter((j + 3) % 4, 0)
                if live(key, 2):
                    pool.wait_ge(ms2_ok, s - 1)
                    pool.tensor_tensor(r2[:, j % 2, :], ms2[:, j % 2, :], power[:, 0:TPB], ALU.pow).then_inc(r2_ok, 1)
                if key in (1, 2, 3):
                    norm_scale(key)

            attention_phase(pool, step)

            def expert_step(e, q, key):
                pool.wait_ge(slot_tok_ok, e + 1)
                wait(pool, added, 16 * ST * e)
                for i, (a, b) in enumerate(PARTS):
                    pool.wait_ge(ys_ok, 2 * e + i + 1)
                    wait(pool, scatter_go, 2 * e + i)
                    pool.tensor_tensor(spare[:, 1:2], power[:, 0:1], power[:, 0:1], ALU.mult).then_inc(scatter_go, 1)
                    for t in range(a // P, b // P):
                        pool.indirect_dma_start(acc_d[:, :], bass.IndirectOffsetOnAxis(slot_tok[q][:, t:t + 1], 0),
                                                ys[q][:, t, :], None, compute_op=ALU.add).then_inc(added, 16)

            by_twos(pool, expert_step, 3)

            def group_step(g, q, key):
                pool.wait_ge(var2_ok, g + 1)
                wait(pool, xh2_ok, g - 1)
                pool.tensor_tensor(rstd2[:, q, :], var2[:, :], power[:, 0:SUPT], ALU.pow).then_inc(rstd2_ok, 1)

            by_twos(pool, group_step, 2)

        @block.scalar
        def _(act):
            act.wait_ge(ld_c, 16)
            act.activation(cond_t[:, :], cond[:, :], ACT.Tanh, scale=0.5).then_inc(tanh_c, 1)
            act.wait_ge(ld_bias, 16)
            act.wait_ge(ld_sel, 16)
            act.activation(bpart[:, 0, :], bias[:, :], ACT.Copy).then_inc(bias_first, 1)
            act.wait_ge(bias_first, 1)
            act.activation(bsum[:, :], bpart[:, 0, :], ACT.Copy, scale=konst[0:3, K_SEL:K_SEL + 1]).then_inc(bias_first, 1)
            act.wait_ge(nmr_ok, 1)
            act.wait_ge(ld_vec, 16)

            def step(s, half, j, key):
                q = j % 2
                if key in (4, 8, 12):
                    act.wait_ge(nmr_ok, key // 4 + 1)
                if live(key, 0):
                    for t in range(TPB):
                        tile = bass.ds(s * TPB + t, 1)
                        ins = act.activation(xhat[:, q, t, :], x[:, tile, :].rearrange("p a c -> p (a c)"), ACT.Identity,
                                             bias=nmr[:, tile], scale=rstd[:, tile])
                    ins.then_inc(xhat_ok, 1)
                if live(key, 1):
                    act.wait_ge(hn_tr, s)
                    wait(act, q_mm, s - 2)
                    act.activation(hnT[:, 1 - q, :], hnT_ps, ACT.Copy, scale=vec[:, V_S1:V_S1 + 1]).then_inc(hnT_ok, 1)
                if live(key, 2):
                    act.wait_ge(qa_ok, s - 1)
                    wait(act, qphi_ok, s - 2)
                    act.activation(qrel[:, :], qa[:, :], ACT.Relu).then_inc(qrel_ok, 1)
                if q == 1 and live(key, 5):
                    act.wait_ge(ldiff_ok, half - 1)
                    act.activation(lexp[:, :], ldiff[:, :], ACT.Exp).then_inc(lexp_ok, 1)
                if live(key, 2):
                    act.activation(qexp[:, :], qa[:, :], ACT.Exp).then_inc(qexp_ok, 1)
                if live(key, 3):
                    act.wait_ge(x1_ok, s - 2)
                    wait(act, r2_ok, s - 4)
                    wait(act, ms2_ok, s - 3)
                    for t in range(TPB):
                        ins = act.activation(junk2[:, t, :], x1[:, 1 - q, t, :], ACT.Square, scale=float(C) ** -0.5,
                                             accum_out=ms2[:, 1 - q, t:t + 1])
                    ins.then_inc(ms2_ok, 1)
                if live(key, 0):
                    act.wait_ge(h_ok, s + 1)
                    wait(act, r1_ok, s - 1)
                    wait(act, ms1_ok, s)
                    for t in range(TPB):
                        ins = act.activation(junk[:, t, :], h[:, j, t, :], ACT.Square, scale=float(C) ** -0.5,
                                             accum_out=ms1[:, q, t:t + 1])
                    ins.then_inc(ms1_ok, 1)
                if live(key, 3):
                    pay_q = ((j + 1) % 4) // 2
                    act.wait_ge(r2_ok, s - 2)
                    if key not in (3, 4, 5, 6):
                        act.wait_ge(scattered[(j + 1) % 4], (s - 3 - (j + 1) % 4) * 16)
                    for t in range(TPB):
                        ins = act.activation(pay[pay_q][:, TPB * (1 - q) + t, 0:C], x1[:, 1 - q, t, :], ACT.Copy,
                                             scale=r2[:, 1 - q, t:t + 1])
                    ins.then_inc(xf_ok, 1)
                if live(key, 1):
                    act.wait_ge(vg_mm, s)
                    wait(act, kvB_mm, s - 2)
                    act.activation(vone[:, 1 - q, :, 0:C], vg_ps[:, :, 0:C], ACT.Copy).then_inc(v_ok, 1)
                    act.wait_ge(ka_ok, s)
                    wait(act, kphi_ok, s - 1)
                    act.activation(kexp[:, :, :], ka[:, :, :], ACT.Exp)
                    act.activation(krel[:, :, :], ka[:, :, :], ACT.Relu).then_inc(krel_ok, 1)
                if live(key, 3):
                    act.wait_ge(xf_tr, s - 2)
                    wait(act, logit_mm, s - 3)
                    act.activation(xfT[:, :], tr_ps, ACT.Copy, scale=vec[:, V_S2:V_S2 + 1]).then_inc(xfT_ok, 1)
                if live(key, 1):
                    wait(act, gnum_ok, s - 2)
                    act.activation(gate[:, 1 - q, :, :], vg_ps[:, :, C:2 * C], ACT.Tanh, scale=0.5).then_inc(g_ok, 1)
                if live(key, 2):
                    act.wait_ge(o_tr, s - 1)
                    wait(act, ao_mm, s - 3)
                    act.activation(oT[:, q, :], tr_ps, ACT.Copy).then_inc(oT_ok, 1)
                if live(key, 0):
                    act.wait_ge(r1_ok, s + 1)
                    wait(act, hn_tr, s)
                    for t in range(TPB):
                        ins = act.activation(hn[:, t, :], h[:, j, t, :], ACT.Copy, scale=r1[:, q, t:t + 1])
                    ins.then_inc(hn_ok, 1)

            attention_phase(act, step)
            act.activation(early[:, :], nmr[:, 0:1], ACT.Gelu).then_inc(early_ok, 1)

            def expert_step(e, q, key):
                act.wait_ge(bcol_ok, e + 1)
                wait(act, down_mm, 2 * (e - 1))
                for k in range(HB):
                    for i, (a, b) in enumerate(PARTS):
                        act.wait_ge(up_mm, 8 * e + 2 * k + i + 1)
                        act.activation(hid[:, q, k, a:b], ps[:, 2 + 2 * (k % 2) + i, 0:b - a], ACT.Gelu,
                                       bias=bcol[:, q, k:k + 1]).then_inc(gelu_ok, 1)

            by_twos(act, expert_step, 3)

            def normalised(g, q):
                act.wait_ge(nmr2_ok, g + 1)
                wait(act, x2_tr, g)
                for t in range(SUPT):
                    ins = act.activation(xh2[:, t, :], x2[:, q, t, :], ACT.Identity,
                                         bias=nmr2[:, q, t:t + 1], scale=rstd2[:, q, t:t + 1])
                ins.then_inc(xh2_ok, 1)

            def modulated(g, q):
                act.wait_ge(x2_tr, g + 1)
                act.wait_ge(modc_ok, g + 1)
                wait(act, up2_mm, 4 * (g - 1))
                for i in range(2):
                    act.activation(hT[:, q, SEQ * i:SEQ * i + SEQ], ps[:, 0, SEQ * i:SEQ * i + SEQ], ACT.Identity,
                                   scale=modc[:, q, i, 1:2], bias=modc[:, q, i, 0:1]).then_inc(hT_ok, 1)

            def store(g, q):
                act.wait_ge(res_ok, g + 1)
                act.dma_start(out_d[bass.ds(g * (SUPT * P), SUPT * P), :].rearrange("(t p) c -> p t c", p=P),
                              res[:, q, :, :]).then_inc(st_out, 16)

            def group_step(g, q, key):
                wait(act, down2_mm, g - 1)
                for k in range(HB):
                    act.wait_ge(up2_mm, 4 * g + k + 1)
                    act.activation(hid2[:, q, k, :], ps[:, 2 + k % 2, :], ACT.Gelu,
                                   bias=vec[:, V_FB1 + k:V_FB1 + k + 1]).then_inc(gelu2_ok, 1)
                    if k == 0 and key != NSUP - 1:
                        normalised(g + 1, 1 - q)
                    if k == 0 and key not in (0, 1):
                        store(g - 2, q)
                    if k == 2 and key != NSUP - 1:
                        modulated(g + 1, 1 - q)

            normalised(0, 0)
            modulated(0, 0)
            by_twos(act, group_step, 2)
            store(NSUP - 2, 0)
            store(NSUP - 1, 1)

        @block.vector
        def _(dve):
            def norm_stats(i):
                tiles = QUARTER[i]
                dve.wait_ge(ld_x[i], 16)
                for t in range(tiles.start, tiles.stop):
                    dve.bn_stats(stat[:, t, :], x[:, t, :]).then_inc(stat_n, 1)
                dve.wait_ge(stat_n, tiles.stop)
                dve.tensor_tensor(mean[:, tiles], stat[:, tiles, 1], stat[:, tiles, 4], ALU.add).then_inc(ln_step, 1)
                dve.tensor_tensor(dmean[:, tiles], stat[:, tiles, 1], stat[:, tiles, 4], ALU.subtract).then_inc(ln_step, 1)
                dve.tensor_tensor(var[:, tiles], stat[:, tiles, 2], stat[:, tiles, 5], ALU.add).then_inc(ln_step, 1)
                dve.wait_ge(ln_step, 6 * i + 3)
                dve.tensor_scalar(mean[:, tiles], mean[:, tiles], 0.5, None, ALU.mult).then_inc(ln_step, 1)
                dve.tensor_tensor(dmean[:, tiles], dmean[:, tiles], dmean[:, tiles], ALU.mult).then_inc(ln_step, 1)
                dve.tensor_scalar(var[:, tiles], var[:, tiles], 1.0 / C, 1e-5, ALU.mult, ALU.add).then_inc(ln_step, 1)
                dve.wait_ge(ln_step, 6 * i + 6)
                dve.scalar_tensor_tensor(out=var[:, tiles], in0=dmean[:, tiles], scalar=0.25, in1=var[:, tiles], op0=ALU.mult,
                                         op1=ALU.add).then_inc(stat_ok, 1)

            def norm_bias(i):
                dve.wait_ge(rstd_ok, i + 1)
                dve.scalar_tensor_tensor(out=nmr[:, QUARTER[i]], in0=mean[:, QUARTER[i]], scalar=-1.0, in1=rstd[:, QUARTER[i]],
                                         op0=ALU.mult, op1=ALU.mult).then_inc(nmr_ok, 1)

            dve.wait_ge(tanh_c, 1)
            dve.scalar_tensor_tensor(out=silu[:, :], in0=cond_t[:, :], scalar=1.0, in1=cond[:, :],
                                     op0=ALU.add, op1=ALU.mult).then_inc(setup_dve, 1)
            dve.wait_ge(setup_dve, 1)
            dve.tensor_scalar(silu[:, :], silu[:, :], 0.5, None, ALU.mult).then_inc(silu_ok, 1)
            dve.wait_ge(siluT_mm, 1)
            dve.tensor_copy(siluT[:, :], ps[:, 7, 0:BATCH]).then_inc(siluT_ok, 1)
            norm_stats(0)
            dve.wait_ge(rows_mm, 1)
            spread = ps[:, 4, :].rearrange("p (b n) -> p b n", b=2)
            dve.tensor_copy(rows[:, :, 0:C], spread[:, :, 0:C]).then_inc(rows_ok, 1)
            dve.tensor_scalar(rows[:, :, C:2 * C], spread[:, :, C:2 * C], 1.0, None, ALU.add).then_inc(rows_ok, 1)

            sel = konst[0:3, K_SEL:K_SEL + 3]
            dve.wait_ge(bias_first, 2)
            dve.wait_ge(ld_sel, 16)
            dve.tensor_tensor(bias[:, :], bias[:, :], bpart[:, 0, :], ALU.subtract).then_inc(bias_step, 1)
            dve.wait_ge(bias_step, 1)
            dve.tensor_copy(bpart[:, 1, :], bias[:, :]).then_inc(bias_step, 1)
            norm_bias(0)
            dve.wait_ge(bias_step, 2)
            dve.scalar_tensor_tensor(out=bsum[:, :], in0=bpart[:, 1, :], scalar=sel[:, 1:2], in1=bsum[:, :],
                                     op0=ALU.mult, op1=ALU.add).then_inc(bias_step, 1)
            dve.tensor_tensor(bias[:, :], bias[:, :], bpart[:, 1, :], ALU.subtract).then_inc(bias_step, 1)

            def last_bias_part():
                dve.wait_ge(bias_step, 4)
                dve.scalar_tensor_tensor(out=bias3[:, :], in0=bias[:, :], scalar=sel[:, 2:3], in1=bsum[:, :],
                                         op0=ALU.mult, op1=ALU.add).then_inc(bias_ok, 1)

            def modulation():
                dve.wait_ge(mod_mm, 1)
                dve.tensor_copy(mod[:, 0:512], ps[0:BATCH, 5, 0:512]).then_inc(mod_step, 1)
                dve.tensor_copy(mod[:, 512:768], ps[0:BATCH, 6, 0:256]).then_inc(mod_step, 1)
                dve.wait_ge(mod_step, 2)
                dve.tensor_scalar(mod[:, CA], mod[:, CA], 1.0, None, ALU.add).then_inc(mod_step, 1)
                dve.tensor_scalar(mod[:, CB], mod[:, CB], 1.0, None, ALU.add).then_inc(mod_step, 1)
                g = mod[:, :].rearrange("b (k m c) -> b k m c", k=2, m=3)[:, :, 2, :]
                dve.tensor_scalar(mod_s[:, :, :], g, 0.0, 2.0, ALU.is_ge, ALU.mult).then_inc(mod_step, 1)
                dve.scalar_tensor_tensor(out=mod_m[:, :, :], in0=g, scalar=-1.0, in1=g, op0=ALU.mult, op1=ALU.max).then_inc(mod_step, 1)
                dve.wait_ge(mod_step, 6)
                dve.tensor_scalar(mod_s[:, :, :], mod_s[:, :, :], 1.0, None, ALU.subtract).then_inc(mod_step, 1)
                dve.tensor_scalar(mod_m[:, :, :], mod_m[:, :, :], 0.25, None, ALU.max).then_inc(mod_step, 1)
                dve.wait_ge(mod_step, 8)
                dve.tensor_tensor(g, mod_s[:, :, :], mod_m[:, :, :], ALU.mult).then_inc(mod_ok, 1)

            def modulation_columns():
                dve.wait_ge(modT_mm, 1)
                dve.wait_ge(ld_vec, 16)
                dve.tensor_copy(modT[:, :, :], ps[:, 7, 32:32 + 2 * BATCH].rearrange("p (k b) -> p b k", k=2)).then_inc(modT_ok, 1)
                dve.tensor_copy(tri[:, :], konst[:, K_TRI:K_TRI + P]).then_inc(tri_ok, 1)
                dve.tensor_scalar(tok[:, :], konst[:, K_TOK:K_TOK + PAIR], 0.0, None, ALU.add).then_inc(tok_ok, 1)

            ktab = konst[:, K_KTAB:K_KTAB + 512].rearrange("p (a t n) -> p a t n", a=2, t=TPB)
            qtab = konst[:, K_QTAB:K_QTAB + 512]
            mask = konst[:, K_MASK:K_MASK + SW].unsqueeze(1).to_broadcast([P, 2, SW])
            iota = konst[:, K_IOTA:K_IOTA + EXPERTS].unsqueeze(1).unsqueeze(1).to_broadcast([P, PAIR, TOPK, EXPERTS])
            base = konst[:, K_BASE:K_BASE + EXPERTS].unsqueeze(1).to_broadcast([P, PAIR, EXPERTS])

            def route_top(p, s):
                dve.wait_ge(logit_mm, s - 2)
                dve.tensor_copy(logit[:, :, :], logit_ps).then_inc(logit_ok, 1)
                dve.wait_ge(logit_ok, p + 1)
                dve.tensor_copy(before[:, :], count[:, :])
                for t in range(PAIR):
                    dve.max(top[:, t, :], logit[:, t, :]).then_inc(routing, 1)
                dve.wait_ge(routing, ROUTE * p + 4)
                dve.tensor_tensor(ldiff[:, :], top[:, :, 1], top[:, :, 0], ALU.subtract).then_inc(ldiff_ok, 1)
                for t in range(PAIR):
                    dve.max_index(topi[:, t, :], top[:, t, :], logit[:, t, :]).then_inc(routing, 1)

            def route_chosen(p, s, buf):
                dve.wait_ge(xf_ok, s - 3)
                dve.wait_ge(routing, ROUTE * p + 8)
                dve.tensor_copy(buf[:, :, E1:E2 + 1], topi[:, :, 0:TOPK]).then_inc(routing, 1)
                dve.wait_ge(routing, ROUTE * p + 9)
                dve.tensor_tensor(hot[:, :, :, :], iota,
                                  buf[:, :, E1:E2 + 1].unsqueeze(3).to_broadcast([P, PAIR, TOPK, EXPERTS]),
                                  ALU.is_equal).then_inc(routing, 1)
                dve.wait_ge(routing, ROUTE * p + 10)
                dve.tensor_tensor(chosen[:, :, :], hot[:, :, 0, :], hot[:, :, 1, :], ALU.add).then_inc(chosen_ok, 1)
                dve.wait_ge(chosen_ok, p + 1)
                dve.tensor_reduce(gain[:, :], chosen[:, :, :].rearrange("p t e -> p e t"), AX.X, ALU.add).then_inc(routing, 1)
                dve.wait_ge(routing, ROUTE * p + 11)
                dve.tensor_tensor(count[:, :], count[:, :], gain[:, :], ALU.add).then_inc(routing, 1)

            def route_place(p):
                dve.wait_ge(pos_mm, p + 1)
                dve.tensor_tensor(slot[:, :, :], pos_ps, base, ALU.add).then_inc(slot_ok, 1)
                dve.tensor_scalar(over[:, :, :], pos_ps, float(CAPACITY), FAR, ALU.is_ge, ALU.mult).then_inc(slot_ok, 1)

            def route_slots(p, j, buf):
                dve.wait_ge(slot_ok, 2 * (p + 1))
                dve.tensor_tensor(slot[:, :, :], slot[:, :, :], over[:, :, :], ALU.add).then_inc(routing, 1)
                dve.wait_ge(lexp_ok, p + 1)
                dve.tensor_scalar(lsum[:, :], lexp[:, :], 1.0, None, ALU.add).then_inc(routing, 1)
                dve.wait_ge(routing, ROUTE * p + 13)
                for k in range(TOPK):
                    dve.tensor_tensor(slot_of[:, :, k, :], hot[:, :, k, :], slot[:, :, :], ALU.mult).then_inc(routing, 1)
                dve.wait_ge(routing, ROUTE * p + 14)
                dve.reciprocal(lrec[:, :], lsum[:, :]).then_inc(routing, 1)
                dve.wait_ge(routing, ROUTE * p + 16)
                dve.tensor_reduce(row_f[:, :, :], slot_of[:, :, :, :], AX.X, ALU.add).then_inc(rowf_ok, 1)
                dve.wait_ge(tok_ok, p + 1)
                dve.tensor_copy(buf[:, :, ID], tok[:, :]).then_inc(gates_ok, 1)
                dve.wait_ge(routing, ROUTE * p + 17)
                dve.wait_ge(rowf_ok, p + 1)
                dve.tensor_copy(row_u[j // 2][:, :, :], row_f[:, :, :]).then_inc(row_ok, 1)
                dve.tensor_copy(buf[:, :, G1], lrec[:, :]).then_inc(gates_ok, 1)
                dve.tensor_tensor(buf[:, :, G2], lexp[:, :], lrec[:, :], ALU.mult).then_inc(gates_ok, 1)

            def step(s, half, j, key):
                q = j % 2
                if live(key, 0):
                    if key in (0, 1):
                        dve.wait_ge(rows_ok, 2)
                    else:
                        dve.wait_ge(ld_rows[q], s * 8 - 8 * q)
                    dve.wait_ge(xhat_ok, s + 1)
                    wait(dve, hn_ok, s - 3)
                    wait(dve, x1_ok, s - 3)
                    dve.tensor_tensor(h[:, j, :, :], xhat[:, q, :, :], rows[:, q, C:2 * C].unsqueeze(1).to_broadcast([P, TPB, C]),
                                      ALU.mult).then_inc(h_step, 1)
                if live(key, 2):
                    dve.wait_ge(kvB_mm, s - 1)
                    wait(dve, num_mm, s - 2)
                    dve.tensor_tensor(state[:, 2:4, :], kv_ps[:, 1, 0:2 * SW].rearrange("p (a n) -> p a n", a=2), mask,
                                      ALU.mult).then_inc(stateB_ok, 1)
                if live(key, 0):
                    dve.wait_ge(h_step, s + 1)
                    dve.tensor_tensor(h[:, j, :, :], h[:, j, :, :], rows[:, q, 0:C].unsqueeze(1).to_broadcast([P, TPB, C]),
                                      ALU.add).then_inc(h_ok, 1)
                if key in (2, 3, 4):
                    norm_bias(key - 1)
                if key == 0:
                    last_bias_part()
                    modulation()
                    dve.wait_ge(ld_const, 16)
                if live(key, 2):
                    dve.wait_ge(qexp_ok, s - 1)
                    wait(dve, num_mm, s - 3)
                    dve.scalar_tensor_tensor(out=qphi[:, q, :], in0=qexp[:, :], scalar=1.0, in1=qrel[:, :],
                                             op0=ALU.min, op1=ALU.add).then_inc(qphi_ok, 1)
                if live(key, 1):
                    dve.wait_ge(kk_mm, s)
                    wait(dve, ka_ok, s - 1)
                    dve.tensor_tensor(kab[:, :, :, :], kk_ps.unsqueeze(1).to_broadcast([P, 2, TPB, C]), ktab, ALU.mult).then_inc(kab_ok, 1)
                if q == 1 and live(key, 5):
                    route_chosen(half - 2, s, pay[(j + 3) % 4 // 2])
                if live(key, 2):
                    dve.wait_ge(num_mm, s - 1)
                    wait(dve, rden_ok, s - 2)
                    dve.tensor_scalar(den[:, :, :], num_ps[:, :, C:SW], 2.0, 2e-6, ALU.mult, ALU.add).then_inc(den_ok, 1)
                    dve.wait_ge(g_ok, s - 1)
                    wait(dve, o_ok, s - 2)
                    dve.scalar_tensor_tensor(out=gnum[:, :, :], in0=gate[:, q, :, :], scalar=1.0, in1=num_ps[:, :, 0:C],
                                             op0=ALU.add, op1=ALU.mult).then_inc(gnum_ok, 1)
                    dve.wait_ge(den_ok, s - 1)
                    dve.reciprocal(rden[:, :, :], den[:, :, :]).then_inc(rden_ok, 1)
                if q == 1 and live(key, 5):
                    route_place(half - 2)
                if live(key, 2):
                    dve.wait_ge(rden_ok, s - 1)
                    dve.wait_ge(gnum_ok, s - 1)
                    wait(dve, o_tr, s - 2)
                    dve.tensor_tensor(o[:, :, :].rearrange("p t (g d) -> p (t g) d", d=DK),
                                      gnum[:, :, :].rearrange("p t (g d) -> p (t g) d", d=DK),
                                      rden[:, :, :].rearrange("p t g -> p (t g)").unsqueeze(2).to_broadcast([P, TPB * HEADS, DK]),
                                      ALU.mult).then_inc(o_ok, 1)
                if live(key, 1):
                    dve.wait_ge(krel_ok, s)
                    wait(dve, kvB_mm, s - 2)
                    dve.scalar_tensor_tensor(out=kphi[:, 1 - q, :, :], in0=kexp[:, :, :], scalar=1.0, in1=krel[:, :, :],
                                             op0=ALU.min, op1=ALU.add).then_inc(kphi_ok, 1)
                    dve.wait_ge(q_mm, s)
                    wait(dve, qa_ok, s - 1)
                    dve.tensor_tensor(qab[:, :], q_ps, qtab, ALU.mult).then_inc(qab_ok, 1)
                if q == 1 and live(key, 5):
                    route_slots(half - 2, (j + 3) % 4, pay[(j + 3) % 4 // 2])
                if q == 0 and live(key, 4):
                    route_top(half - 2, s)
                if live(key, 1):
                    dve.wait_ge(kvA_mm, s)
                    wait(dve, num_mm, s - 1)
                    dve.tensor_tensor(state[:, 0:2, :], kv_ps[:, 0, 0:2 * SW].rearrange("p (a n) -> p a n", a=2), mask,
                                      ALU.mult).then_inc(stateA_ok, 1)
                if live(key, 2):
                    dve.wait_ge(ao_mm, s - 1)
                    if key not in (2, 3):
                        dve.wait_ge(st_x1[q], 8 * (s - 2 - q))
                        dve.wait_ge(xf_ok, s - 3)
                    dve.tensor_tensor(x1[:, q, :, :], ao_ps, h[:, (j + 2) % 4, :, :], ALU.add).then_inc(x1_ok, 1)
                if key in (0, 1, 2):
                    norm_stats(key + 1)
                if key == 1:
                    modulation_columns()

            attention_phase(dve, step)

            def slots_in(e, q):
                dve.wait_ge(ld_slots[q], 8 * (e - q) + 16)
                wait(dve, expert_ok, e - 1)
                wait(dve, slot_gate_ok, e - 1)
                for k, (gcol, ecol) in enumerate(((G1, E1), (G2, E2))):
                    dve.scalar_tensor_tensor(out=choice_gate[:, q, k, :], in0=xs[q][:, :, ecol], scalar=expert[:, q:q + 1], in1=xs[q][:, :, gcol],
                                             op0=ALU.is_equal, op1=ALU.mult).then_inc(gate_step, 1)
                wait(dve, slot_tok_ok, e - 1)
                dve.tensor_scalar(slot_id[:, q, :], xs[q][:, :, ID], 1.0, None, ALU.mult).then_inc(slot_id_ok, 1)
                dve.wait_ge(gate_step, 2 * e + 2)
                dve.tensor_scalar(expert[:, q:q + 1], expert[:, q:q + 1], 2.0, None, ALU.add).then_inc(expert_ok, 1)
                wait(dve, gelu_ok, 8 * (e - 1))
                dve.tensor_scalar(bcol[:, q, :], vec[:, bass.ds(e * HB + V_B1, HB)], 1.0, None, ALU.mult).then_inc(bcol_ok, 1)
                for i, (a, b) in enumerate(PARTS):
                    dve.wait_ge(x_tr, 2 * e + i + 1)
                    wait(dve, up_mm, 8 * (e - 1))
                    dve.tensor_scalar(xeT[:, q, a:b], ps[:, i, 0:b - a], vec[:, V_S2:V_S2 + 1], None, ALU.mult).then_inc(xeT_ok, 1)

            def gated(e, q, i):
                a, b = PARTS[i]
                t0, t1 = a // P, b // P
                if i == 0:
                    wait(dve, added, 16 * ST * (e - 1))
                    dve.wait_ge(slot_id_ok, e + 1)
                    dve.tensor_copy(slot_tok[q][:, :], slot_id[:, q, :]).then_inc(slot_tok_ok, 1)
                    wait(dve, ys_ok, 2 * e)
                    dve.tensor_tensor(slot_gate[:, :], choice_gate[:, q, 0, :], choice_gate[:, q, 1, :], ALU.add).then_inc(slot_gate_ok, 1)
                dve.wait_ge(down_mm, 2 * e + i + 1)
                wait(dve, ys_ok, 2 * (e - 1) + i + 1)
                dve.tensor_tensor(yb[:, t0:t1, :], ps[:, 6 + i, 0:b - a].rearrange("p (t c) -> p t c", c=C),
                                  b2_rows[:, bass.ds(e, 1), :].to_broadcast([P, t1 - t0, C]), ALU.add).then_inc(yb_ok, 1)
                dve.wait_ge(yb_ok, 2 * e + i + 1)
                dve.wait_ge(slot_gate_ok, e + 1)
                dve.tensor_tensor(ys[q][:, t0:t1, :], yb[:, t0:t1, :],
                                  slot_gate[:, t0:t1].unsqueeze(2).to_broadcast([P, t1 - t0, C]),
                                  ALU.mult).then_inc(ys_ok, 1)

            def expert_step(e, q, key):
                if key != 0:
                    gated(e - 1, 1 - q, 0)
                if key != EXPERTS - 1:
                    slots_in(e + 1, 1 - q)
                if key != 0:
                    gated(e - 1, 1 - q, 1)

            slots_in(0, 0)
            dve.wait_ge(ld_b2, 16)
            by_twos(dve, expert_step, 3)
            for i in range(2):
                gated(EXPERTS - 1, 1, i)
            dve.wait_ge(ld_gains, 32)

            def group_in(g, q):
                dve.wait_ge(ld_ac[q], 8 * (g - q) + 16)
                wait(dve, xh2_ok, g - 1)
                dve.tensor_tensor(x2[:, q, :, :].rearrange("p (b t) c -> p b t c", b=2),
                                  ac[:, q, :, :].rearrange("p (b t) c -> p b t c", b=2),
                                  ga_rows[:, bass.ds(g * 2, 2), :].unsqueeze(2).to_broadcast([P, 2, TPB, C]), ALU.mult).then_inc(ga_step, 1)
                dve.wait_ge(ga_step, g + 1)
                dve.tensor_tensor(x2[:, q, :, :], x2[:, q, :, :], x[:, bass.ds(g * SUPT, SUPT), :], ALU.add).then_inc(x2_ok, 1)
                dve.wait_ge(x2_ok, g + 1)
                for t in range(SUPT):
                    dve.bn_stats(stat2[:, t, :], x2[:, q, t, :]).then_inc(stat2_ok, 1)
                dve.wait_ge(stat2_ok, SUPT * (g + 1))
                dve.memset(spare[:, 0:1], 0.0)
                for t in range(SUPT):
                    dve.bn_aggr(mv2[:, t, :], stat2[:, t, :]).then_inc(mv2_ok, 1)
                dve.wait_ge(mv2_ok, SUPT * (g + 1))
                wait(dve, rstd2_ok, g)
                dve.tensor_scalar(var2[:, :], mv2[:, :, 1], 1e-5, None, ALU.add).then_inc(var2_ok, 1)
                dve.tensor_scalar(x[:, bass.ds(g * SUPT, SUPT), :], x2[:, q, :, :], 1.0, None, ALU.mult).then_inc(x2_kept, 1)
                wait(dve, hT_ok, 2 * (g - 1))
                dve.tensor_scalar(modc[:, q, :, :], modT[:, bass.ds(g * 2, 2), :], 1.0, None, ALU.mult).then_inc(modc_ok, 1)
                dve.wait_ge(rstd2_ok, g + 1)
                dve.scalar_tensor_tensor(out=nmr2[:, q, :], in0=mv2[:, :, 0], scalar=-1.0, in1=rstd2[:, q, :],
                                         op0=ALU.mult, op1=ALU.mult).then_inc(nmr2_ok, 1)

            def result(g, q):
                dve.wait_ge(down2_mm, g + 1)
                wait(dve, res_ok, g)
                dve.tensor_tensor(y2[:, :, :], ps[:, 4 + q, :].rearrange("p (t c) -> p t c", c=C),
                                  b2_rows[:, EXPERTS:EXPERTS + 1, :].to_broadcast([P, SUPT, C]), ALU.add).then_inc(y2_ok, 1)
                dve.wait_ge(y2_ok, g + 1)
                rows_of = y2[:, :, :].rearrange("p (b t) c -> p b t c", b=2)
                dve.tensor_tensor(rows_of, rows_of, gb_rows[:, bass.ds(g * 2, 2), :].unsqueeze(2).to_broadcast([P, 2, TPB, C]),
                                  ALU.mult).then_inc(y2_gated, 1)
                dve.wait_ge(y2_gated, g + 1)
                wait(dve, st_out, 16 * g)
                dve.wait_ge(x2_kept, g + 1)
                dve.tensor_tensor(res[:, q, :, :], y2[:, :, :], x[:, bass.ds(g * SUPT, SUPT), :], ALU.add).then_inc(res_ok, 1)

            def group_step(g, q, key):
                if key not in (NSUP - 2, NSUP - 1):
                    group_in(g + 2, q)
                if key != 0:
                    result(g - 1, 1 - q)

            group_in(0, 0)
            group_in(1, 1)
            by_twos(dve, group_step, 2)
            result(NSUP - 1, 1)

        @block.tensor
        def _(pe):
            pe.wait_ge(ld_ident, 16)
            pe.wait_ge(silu_ok, 1)
            pe.transpose(ps[:, 7, 0:BATCH], silu[:, :], ident[0:BATCH, 0:BATCH]).then_inc(siluT_mm, 1)
            pe.wait_ge(siluT_ok, 1)
            pe.wait_ge(ld_wmod, 16)
            for b in range(2):
                ins = pe.matmul(ps[:, 4, 2 * C * b:2 * C * b + 2 * C], siluT[:, b:b + 1].to_broadcast([P, P]), wmod[:, 0:2 * C],
                                start=True, stop=True)
            ins.then_inc(rows_mm, 1)
            pe.matmul(ps[0:BATCH, 5, 0:512], siluT[:, :], wmod[:, 0:512], start=True, stop=True)
            pe.matmul(ps[0:BATCH, 6, 0:256], siluT[:, :], wmod[:, 512:768], start=True, stop=True).then_inc(mod_mm, 1)

            def modulation_columns():
                pe.wait_ge(mod_ok, 1)
                for i, part in enumerate((SB, CB)):
                    ins = pe.transpose(ps[:, 7, 32 + BATCH * i:32 + BATCH * (i + 1)], mod[:, part], ident[0:BATCH, 0:BATCH])
                ins.then_inc(modT_mm, 1)

            def project(out, q, t, cols):
                pe.matmul(out[:, t, :], hnT[:, q, P * t:P * t + P], wkvg[:, cols], start=True, stop=False)
                return pe.matmul(out[:, t, :], ones3[:, 0:P], bias3[:, cols], start=False, stop=True)

            def kv_state(q, c):
                out = kv_ps[:, c // 2, (c % 2) * SW:(c % 2) * SW + SW]
                ends = [P] * ((c + 1) // 2) + [CHUNK] * ((c + 1) % 2)
                for t, end in enumerate(ends):
                    ins = pe.matmul(out, kphi[0:end, q, t, :], vone[0:end, q, t, :], start=(t == 0), stop=(t == len(ends) - 1))
                return ins

            def step(s, half, j, key):
                q = j % 2
                if live(key, 0):
                    pe.wait_ge(hn_ok, s + 1)
                    wait(pe, oT_ok, s - 1)
                    for t in range(TPB):
                        ins = pe.transpose(hnT_ps[:, P * t:P * t + P], hn[:, t, :], ident)
                    ins.then_inc(hn_tr, 1)
                if live(key, 1):
                    pe.wait_ge(kphi_ok, s)
                    pe.wait_ge(v_ok, s)
                    wait(pe, stateB_ok, s - 1)
                    for c in (2, 3):
                        ins = kv_state(1 - q, c)
                    ins.then_inc(kvB_mm, 1)
                if live(key, 0):
                    if key == 0:
                        pe.wait_ge(bias_ok, 1)
                        pe.wait_ge(setup_pool, 8)
                        pe.wait_ge(ld_kvg, 16)
                        pe.wait_ge(ld_q, 16)
                    pe.wait_ge(hnT_ok, s + 1)
                    wait(pe, kab_ok, s)
                    for t in range(TPB):
                        ins = project(kk_ps, q, t, slice(0, C))
                    ins.then_inc(kk_mm, 1)
                    wait(pe, v_ok, s)
                    wait(pe, g_ok, s)
                    for t in range(TPB):
                        ins = project(vg_ps, q, t, slice(C, 3 * C))
                    ins.then_inc(vg_mm, 1)
                if live(key, 1):
                    pe.wait_ge(qphi_ok, s)
                    wait(pe, gnum_ok, s - 1)
                    pe.wait_ge(stateA_ok, s)
                    pe.wait_ge(stateB_ok, s)
                    for c in range(CHUNKS):
                        at = CHUNK * (c % 2)
                        ins = pe.matmul(num_ps[at:at + CHUNK, c // 2, :], qphi[:, 1 - q, CHUNK * c:CHUNK * c + CHUNK],
                                        state[:, c, :], start=True, stop=True)
                    ins.then_inc(num_mm, 1)
                if q == 0 and live(key, 4):
                    if key == 4:
                        pe.wait_ge(tri_ok, 1)
                    pe.wait_ge(chosen_ok, half - 1)
                    pe.wait_ge(logit_ok, half - 1)
                    if live(key, 2):
                        pe.wait_ge(x1_ok, s - 1)
                    pe.matmul(pos_ps, ones[:, :], before[:, :].unsqueeze(1).to_broadcast([P, PAIR, EXPERTS]), start=True, stop=False)
                    for t in range(PAIR - 1):
                        pe.matmul(pos_ps[:, t + 1:PAIR, :], ones[:, :],
                                  chosen[:, t:t + 1, :].to_broadcast([P, PAIR - 1 - t, EXPERTS]), start=False, stop=False)
                    pe.matmul(pos_ps, tri[:, :], chosen[:, :, :], start=False, stop=True).then_inc(pos_mm, 1)
                if live(key, 2):
                    pe.wait_ge(xf_ok, s - 1)
                    pe.wait_ge(oT_ok, s - 1)
                    if live(key, 0):
                        pe.wait_ge(hnT_ok, s + 1)
                    buf, first = pay[j // 2 ^ 1], TPB * q
                    for t in range(TPB):
                        ins = pe.transpose(tr_ps[:, P * t:P * t + P], buf[:, first + t, 0:C], ident)
                    ins.then_inc(xf_tr, 1)
                if live(key, 0):
                    wait(pe, qab_ok, s)
                    for i in range(2):
                        cols = slice(SEQ * i, SEQ * i + SEQ)
                        pe.matmul(q_ps[:, cols], wq[:, C * i:C * i + C], hnT[:, q, :], start=True, stop=False)
                        ins = pe.matmul(q_ps[:, cols], bias3[:, B_Q + C * i:B_Q + C * i + C], ones3[:, :], start=False, stop=True)
                    ins.then_inc(q_mm, 1)
                if live(key, 1):
                    pe.wait_ge(o_ok, s)
                    if key == 1:
                        pe.wait_ge(hnT_ok, s + 1)
                    else:
                        pe.wait_ge(xfT_ok, s - 1)
                    for t in range(TPB):
                        ins = pe.transpose(tr_ps[:, P * t:P * t + P], o[:, t, :], ident)
                    ins.then_inc(o_tr, 1)
                if live(key, 2):
                    if key == 2:
                        pe.wait_ge(ld_r, 16)
                    pe.wait_ge(xfT_ok, s - 1)
                    pe.wait_ge(x1_ok, s - 1)
                    if q == 0 and live(key, 4):
                        pe.wait_ge(slot_ok, 2 * (half - 1))
                    first = TPB * q
                    for t in range(TPB):
                        pe.matmul(logit_ps[:, first + t, :], xfT[:, P * t:P * t + P], wr[:, :], start=True, stop=False)
                        ins = pe.matmul(logit_ps[:, first + t, :], ones3[:, 0:P], bias3[:, B_R:B_R + EXPERTS], start=False, stop=True)
                    ins.then_inc(logit_mm, 1)
                if live(key, 0):
                    pe.wait_ge(kphi_ok, s + 1)
                    pe.wait_ge(v_ok, s + 1)
                    wait(pe, stateA_ok, s)
                    for c in (0, 1):
                        ins = kv_state(q, c)
                    ins.then_inc(kvA_mm, 1)
                if key == 0:
                    modulation_columns()
                if live(key, 1):
                    if key == 1:
                        pe.wait_ge(modT_ok, 1)
                        pe.wait_ge(ld_o, 16)
                    pe.wait_ge(oT_ok, s)
                    wait(pe, x1_ok, s - 1)
                    if q == 1 and key != 1:
                        pe.wait_ge(logit_ok, half)
                    for t in range(TPB):
                        pe.matmul(ao_ps[:, t, :], oT[:, 1 - q, P * t:P * t + P], wo[:, :], start=True, stop=False)
                        ins = pe.matmul(ao_ps[:, t, :], ones3[:, 0:P], bias3[:, B_O:B_O + C], start=False, stop=True)
                    ins.then_inc(ao_mm, 1)

            attention_phase(pe, step)

            def transpose_slots(e, q):
                pe.wait_ge(ld_slots[q], 8 * (e - q) + 16)
                wait(pe, xeT_ok, 2 * e)
                for t in range(ST):
                    i, at = (0, P * t) if P * t < SPLIT else (1, P * t - SPLIT)
                    ins = pe.transpose(ps[:, i, at:at + P], xs[q][:, t, 0:C], ident)
                    if t in (SPLIT // P - 1, ST - 1):
                        ins.then_inc(x_tr, 1)

            def up(e, q, k):
                if k == 0:
                    pe.wait_ge(ld_w1[q], 8 * (e - q) + 16)
                wait(pe, gelu_ok, 8 * e + 2 * k - 2)
                for i, (a, b) in enumerate(PARTS):
                    if k == 0:
                        pe.wait_ge(xeT_ok, 2 * e + i + 1)
                    pe.matmul(ps[:, 2 + 2 * (k % 2) + i, 0:b - a], w1[:, q, P * k:P * k + P], xeT[:, q, a:b],
                              start=True, stop=True).then_inc(up_mm, 1)

            def down(e, q, t):
                i, at = (0, P * t) if P * t < SPLIT else (1, P * t - SPLIT)
                if t == 0:
                    pe.wait_ge(ld_w2[q], 8 * (e - q) + 16)
                    pe.wait_ge(gelu_ok, 8 * e + 8)
                if at == 0:
                    wait(pe, yb_ok, 2 * (e - 1) + i + 1)
                for k in range(HB):
                    ins = pe.matmul(ps[:, 6 + i, at:at + P], hid[:, q, k, P * t:P * t + P], w2[:, q, k, :],
                                    start=(k == 0), stop=(k == HB - 1))
                if t in (SPLIT // P - 1, ST - 1):
                    ins.then_inc(down_mm, 1)

            def expert_step(e, q, key):
                for k in range(HB):
                    up(e, q, k)
                    if key == EXPERTS - 1 and k == 0:
                        for t in range(ST):
                            down(e - 1, 1 - q, t)
                    if key not in (0, EXPERTS - 1):
                        down(e - 1, 1 - q, k)
                    if k == HB - 2 and key != EXPERTS - 1:
                        transpose_slots(e + 1, 1 - q)
                if key not in (0, EXPERTS - 1):
                    down(e - 1, 1 - q, ST - 1)

            transpose_slots(0, 0)
            by_twos(pe, expert_step, 3)
            for t in range(ST):
                down(EXPERTS - 1, 1, t)

            def transpose_group(g):
                pe.wait_ge(xh2_ok, g + 1)
                wait(pe, hT_ok, 2 * g)
                for t in range(SUPT):
                    ins = pe.transpose(ps[:, 0, P * t:P * t + P], xh2[:, t, :], ident)
                ins.then_inc(x2_tr, 1)

            def up2(g, q, k):
                if k == 0:
                    pe.wait_ge(hT_ok, 2 * g + 2)
                wait(pe, gelu2_ok, 4 * g + k - 1)
                pe.matmul(ps[:, 2 + k % 2, :], f1[:, P * k:P * k + P], hT[:, q, :], start=True, stop=True).then_inc(up2_mm, 1)

            def down2(g, q, t):
                if t == 0:
                    pe.wait_ge(gelu2_ok, 4 * g + 4)
                    wait(pe, y2_ok, g)
                for k in range(HB):
                    ins = pe.matmul(ps[:, 4 + q, P * t:P * t + P], hid2[:, q, k, P * t:P * t + P], f2[:, k, :],
                                    start=(k == 0), stop=(k == HB - 1))
                if t == SUPT - 1:
                    ins.then_inc(down2_mm, 1)

            def group_step(g, q, key):
                for k, tiles in enumerate(((0,), (1, 2), (3,), ())):
                    up2(g, q, k)
                    if k == 2 and key != NSUP - 1:
                        transpose_group(g + 1)
                    if key != 0:
                        for t in tiles:
                            down2(g - 1, 1 - q, t)

            pe.wait_ge(ld_ffn, 32)
            transpose_group(0)
            by_twos(pe, group_step, 2)
            for t in range(SUPT):
                down2(NSUP - 1, 1, t)


def kernel(L0_attn_x, L0_attn_norm1_scale, L0_attn_norm2_scale, L0_attn_Wq, L0_attn_bq, L0_attn_Wk, L0_attn_bk,
           L0_attn_Wv, L0_attn_bv, L0_attn_Wg, L0_attn_bg, L0_attn_Wo, L0_attn_bo, L0_attn_router_W, L0_attn_router_b,
           L0_attn_W1, L0_attn_b1, L0_attn_W2, L0_attn_b2, L0_ffn_w1, L0_ffn_b1, L0_ffn_w2, L0_ffn_b2, L0_c, L0_wmod):
    import concourse.bacc as _bacc
    from concourse.bass_utils import run_bass_kernel_spmd as _run

    def flat(a):
        return np.ascontiguousarray(np.asarray(a))

    swap = np.arange(C).reshape(HEADS, 2, DK // 2)[:, ::-1].reshape(-1)
    wq_, wk, wv, wg = (flat(w) for w in (L0_attn_Wq, L0_attn_Wk, L0_attn_Wv, L0_attn_Wg))
    bq, bk, bv, bg = (flat(w) for w in (L0_attn_bq, L0_attn_bk, L0_attn_bv, L0_attn_bg))
    columns = [flat(L0_attn_norm1_scale)[:, None], flat(L0_attn_norm2_scale)[:, None], flat(L0_ffn_b1).reshape(HB, P).T,
               flat(L0_attn_b1).reshape(EXPERTS * HB, P).T]
    konst, empty = constants()
    arrays = {
        "x": flat(L0_attn_x).reshape(TOKENS, C),
        "c": flat(L0_c),
        "wmod": flat(L0_wmod),
        "wkvg": np.concatenate([wk, wv, wg], 1),
        "wq": np.concatenate([wq_, wq_[:, swap]], 1),
        "wo": flat(L0_attn_Wo),
        "wr": flat(L0_attn_router_W),
        "w1": flat(L0_attn_W1),
        "w2": flat(L0_attn_W2),
        "f1": flat(L0_ffn_w1),
        "f2": flat(L0_ffn_w2),
        "vec": np.ascontiguousarray(np.concatenate(columns, 1)),
        "b2": np.concatenate([flat(L0_attn_b2), flat(L0_ffn_b2)[None, :]]),
        "bias": np.concatenate([bk, bv, bg, bq, bq[swap], flat(L0_attn_bo), flat(L0_attn_router_b)])[None, :],
        "konst": konst,
        "empty": empty,
    }
    nc = _bacc.Bacc("TRN2", target_bir_lowering=False, num_devices=1)
    args = [nc.dram_tensor(f"in_{n}", a.shape, F32, kind="ExternalInput").ap() for n, a in arrays.items()]
    out = nc.dram_tensor("out", (TOKENS, C), F32, kind="ExternalOutput").ap()
    adaln_moe(nc, *args, out)
    r = _run(nc, [{f"in_{n}": a for n, a in arrays.items()}], core_ids=[0])
    return r.results[0]["out"].reshape(BATCH, SEQ, C)
```
